# Optimizing a Trainium2 kernel written in Bass

```python
import numpy as np
import jax
import jax.numpy as jnp

def _softmax(x, axis=-1):
    return jax.nn.softmax(x, axis=axis)

def _gelu(x):
    return jax.nn.gelu(x, approximate=True)

def _silu(x):
    return jax.nn.silu(x)

def _sigmoid(x):
    return jax.nn.sigmoid(x)

def _layernorm(x, axis=-1, eps=1e-05):
    m = jnp.mean(x, axis=axis, keepdims=True)
    v = jnp.var(x, axis=axis, keepdims=True)
    return (x - m) / jnp.sqrt(v + eps)

def _scatter_add(tgt, idx, src, axis=0):
    return tgt.at[idx].add(src)

def _segment_sum(src, seg, n):
    return jax.ops.segment_sum(src, seg, n)
kernel_name = 'mk_decoder_preln_d1_seqx_r8_2d7449'

def setup_inputs(seed: int=0):
    np.random.seed(seed)
    _w = jnp.asarray

    def _rec_inputs():
        import jax
        import jax.numpy as jnp
        _rk = jax.random.key(seed)
        x = -0.000125 + 0.9999 * jax.random.normal(jax.random.fold_in(_rk, 1), (2, 256, 512), jnp.float32)
        _lenS = 256 - jax.random.randint(jax.random.fold_in(_rk, 7), (2,), 0, max(1, 256 // 4) + 1, jnp.int32)
        _lenS2 = 512 - jax.random.randint(jax.random.fold_in(_rk, 8), (2,), 0, max(1, 512 // 4) + 1, jnp.int32)
        _ctx_4096P = jax.random.normal(jax.random.fold_in(_rk, 11), (2, 16, 512), jnp.float32)
        _ctx_4096c = jax.random.dirichlet(jax.random.fold_in(_rk, 511), 0.3 * jnp.ones((16,), jnp.float32), (2, 512))
        _ctx_4096t = jnp.einsum('bsk,bkd->bsd', _ctx_4096c, _ctx_4096P)
        _ctx_4096t = _ctx_4096t * jax.lax.rsqrt(jnp.mean(jnp.square(_ctx_4096t)) + 1e-12) * 0.953939
        ctx_4096 = -5.72187e-05 + 0.999849 * (_ctx_4096t + 0.3 * jax.random.normal(jax.random.fold_in(_rk, 611), (2, 512, 512), jnp.float32))
        return (x, ctx_4096)
    x, ctx_4096 = _rec_inputs()

    def _L0_attn_setup():
        import jax, jax.numpy as jnp
        import numpy as np
        H_M, P_M, G_M, N_M, K_CONV, CHUNK = (128, 64, 8, 128, 4, 128)
        D_MODEL = 512
        D_INNER = H_M * P_M
        CONV_DIM = D_INNER + 2 * G_M * N_M
        PROJ_DIM = D_INNER + CONV_DIM + H_M
        EPS = 1e-05

        def segsum(x):
            l = x.shape[-1]
            xe = jnp.broadcast_to(x[..., None], x.shape + (l,))
            m1 = jnp.tril(jnp.ones((l, l), dtype=bool), -1)
            s = jnp.cumsum(jnp.where(m1, xe, 0.0), axis=-2)
            m2 = jnp.tril(jnp.ones((l, l), dtype=bool), 0)
            return jnp.where(m2, s, -jnp.inf)

        def causal_conv(x, w, bconv):
            k = w.shape[1]
            s = x.shape[1]
            xp = jnp.pad(x, ((0, 0), (k - 1, 0), (0, 0)))
            y = sum((xp[:, i:i + s, :] * w[:, i] for i in range(k)))
            return y + bconv
        key = jax.random.key(seed)
        ks = jax.random.split(key, 8)
        B_, S = (1, 256)
        sc = 0.02
        return {'x': jax.random.normal(ks[0], (B_, S, D_MODEL), dtype=jnp.float32), 'norm_w': jnp.ones((D_MODEL,), dtype=jnp.float32), 'in_proj_w': jax.random.normal(ks[1], (PROJ_DIM, D_MODEL), dtype=jnp.float32) * sc, 'conv_w': jax.random.normal(ks[2], (CONV_DIM, K_CONV), dtype=jnp.float32) * 0.2, 'conv_b': jnp.zeros((CONV_DIM,), dtype=jnp.float32), 'dt_bias': jax.random.uniform(ks[3], (H_M,), dtype=jnp.float32) * 0.1, 'A_log': jnp.log(1.0 + 15.0 * jax.random.uniform(ks[4], (H_M,), dtype=jnp.float32)), 'Dp': jnp.ones((H_M,), dtype=jnp.float32), 'gnorm_w': jnp.ones((D_INNER,), dtype=jnp.float32), 'out_proj_w': jax.random.normal(ks[5], (D_MODEL, D_INNER), dtype=jnp.float32) * sc}
    _L0_attn_all = _L0_attn_setup()
    _L0_attn_in = {k: v for k, v in _L0_attn_all.items() if k in ('norm_w', 'in_proj_w', 'conv_w', 'conv_b', 'dt_bias', 'A_log', 'Dp', 'gnorm_w', 'out_proj_w')}
    del _L0_attn_all

    def _L0_xattn_setup():
        import jax, jax.numpy as jnp
        import numpy as np
        QMIN = 0.0
        QMAX = 255.0

        def fake_quant(x, scale, zp):
            s = scale.reshape(())
            z = zp.reshape(())
            q = jnp.clip(jnp.round(x / s + z), QMIN, QMAX)
            return (q - z) * s
        key = jax.random.key(seed)
        k1, k2 = jax.random.split(key)
        B, M, K, N = (4, 256, 512, 512)
        x1 = jax.random.normal(k1, (B, M, K), dtype=jnp.float32)
        x2 = jax.random.normal(k2, (B, K, N), dtype=jnp.float32)
        x1_scale = jnp.full((1,), 8.0 / 255.0, dtype=jnp.float32)
        x1_zp = jnp.full((1,), 128.0, dtype=jnp.float32)
        x2_scale = jnp.full((1,), 8.0 / 255.0, dtype=jnp.float32)
        x2_zp = jnp.full((1,), 128.0, dtype=jnp.float32)
        return {'x1': x1, 'x2': x2, 'x1_scale': x1_scale, 'x1_zp': x1_zp, 'x2_scale': x2_scale, 'x2_zp': x2_zp}
    _L0_xattn_all = _L0_xattn_setup()
    _L0_xattn_in = {k: v for k, v in _L0_xattn_all.items() if k in ('x1_scale', 'x1_zp', 'x2_scale', 'x2_zp')}
    del _L0_xattn_all

    def _L0_ffn_setup():
        import jax, jax.numpy as jnp
        import numpy as np
        NUM_EXPERTS = 4
        HIDDEN = 512
        RANK = 8
        ALPHA = 8.0
        SCALE = ALPHA / RANK
        key = jax.random.key(seed)
        ks = jax.random.split(key, 6)
        B, T, H, E, R = (4, 512, HIDDEN, NUM_EXPERTS, RANK)
        x = jax.random.normal(ks[0], (B, T, H), dtype=jnp.float32)
        W_up = jax.random.normal(ks[1], (H, H), dtype=jnp.float32) / np.sqrt(H)
        gate_w = jax.random.normal(ks[2], (E, H), dtype=jnp.float32) / np.sqrt(H)
        expert_bias = jnp.zeros((E,), dtype=jnp.float32)
        lora_A = jax.random.normal(ks[3], (E, R, H), dtype=jnp.float32) / np.sqrt(H)
        lora_B = jax.random.normal(ks[4], (E, H, R), dtype=jnp.float32) * 0.01
        return {'x': x, 'W_up': W_up, 'gate_w': gate_w, 'expert_bias': expert_bias, 'lora_A': lora_A, 'lora_B': lora_B}
    _L0_ffn_all = _L0_ffn_setup()
    _L0_ffn_in = {k: v for k, v in _L0_ffn_all.items() if k in ('W_up', 'gate_w', 'expert_bias', 'lora_A', 'lora_B')}
    del _L0_ffn_all
    return {'x': x, 'ctx_4096': ctx_4096, 'L0_attn_norm_w': _L0_attn_in['norm_w'], 'L0_attn_in_proj_w': _L0_attn_in['in_proj_w'], 'L0_attn_conv_w': _L0_attn_in['conv_w'], 'L0_attn_conv_b': _L0_attn_in['conv_b'], 'L0_attn_dt_bias': _L0_attn_in['dt_bias'], 'L0_attn_A_log': _L0_attn_in['A_log'], 'L0_attn_Dp': _L0_attn_in['Dp'], 'L0_attn_gnorm_w': _L0_attn_in['gnorm_w'], 'L0_attn_out_proj_w': _L0_attn_in['out_proj_w'], 'L0_xattn_x1_scale': _L0_xattn_in['x1_scale'], 'L0_xattn_x1_zp': _L0_xattn_in['x1_zp'], 'L0_xattn_x2_scale': _L0_xattn_in['x2_scale'], 'L0_xattn_x2_zp': _L0_xattn_in['x2_zp'], 'L0_ffn_W_up': _L0_ffn_in['W_up'], 'L0_ffn_gate_w': _L0_ffn_in['gate_w'], 'L0_ffn_expert_bias': _L0_ffn_in['expert_bias'], 'L0_ffn_lora_A': _L0_ffn_in['lora_A'], 'L0_ffn_lora_B': _L0_ffn_in['lora_B']}

def reference(x, ctx_4096, L0_attn_norm_w, L0_attn_in_proj_w, L0_attn_conv_w, L0_attn_conv_b, L0_attn_dt_bias, L0_attn_A_log, L0_attn_Dp, L0_attn_gnorm_w, L0_attn_out_proj_w, L0_xattn_x1_scale, L0_xattn_x1_zp, L0_xattn_x2_scale, L0_xattn_x2_zp, L0_ffn_W_up, L0_ffn_gate_w, L0_ffn_expert_bias, L0_ffn_lora_A, L0_ffn_lora_B):
    import jax
    import jax.numpy as jnp

    def _L0_attn_ref(x, norm_w, in_proj_w, conv_w, conv_b, dt_bias, A_log, Dp, gnorm_w, out_proj_w):
        import jax, jax.numpy as jnp
        import numpy as np
        H_M, P_M, G_M, N_M, K_CONV, CHUNK = (128, 64, 8, 128, 4, 128)
        D_MODEL = 512
        D_INNER = H_M * P_M
        CONV_DIM = D_INNER + 2 * G_M * N_M
        PROJ_DIM = D_INNER + CONV_DIM + H_M
        EPS = 1e-05

        def segsum(x):
            l = x.shape[-1]
            xe = jnp.broadcast_to(x[..., None], x.shape + (l,))
            m1 = jnp.tril(jnp.ones((l, l), dtype=bool), -1)
            s = jnp.cumsum(jnp.where(m1, xe, 0.0), axis=-2)
            m2 = jnp.tril(jnp.ones((l, l), dtype=bool), 0)
            return jnp.where(m2, s, -jnp.inf)

        def causal_conv(x, w, bconv):
            k = w.shape[1]
            s = x.shape[1]
            xp = jnp.pad(x, ((0, 0), (k - 1, 0), (0, 0)))
            y = sum((xp[:, i:i + s, :] * w[:, i] for i in range(k)))
            return y + bconv
        b, s, _ = x.shape
        residual = x
        h = x * jax.lax.rsqrt(jnp.mean(x * x, axis=-1, keepdims=True) + EPS) * norm_w
        proj = jnp.einsum('bsd,od->bso', h, in_proj_w)
        gate = proj[..., :D_INNER]
        hBC = proj[..., D_INNER:D_INNER + CONV_DIM]
        dt = proj[..., D_INNER + CONV_DIM:]
        hBC = jax.nn.silu(causal_conv(hBC, conv_w, conv_b))
        hid = hBC[..., :D_INNER].reshape(b, s, H_M, P_M)
        B = hBC[..., D_INNER:D_INNER + G_M * N_M].reshape(b, s, G_M, N_M)
        C = hBC[..., D_INNER + G_M * N_M:].reshape(b, s, G_M, N_M)
        dt = jax.nn.softplus(dt + dt_bias)
        A = -jnp.exp(A_log)
        pad = -s % CHUNK
        D_res = Dp[None, None, :, None] * hid
        hid_dt = hid * dt[..., None]
        A_full = A[None, None, :] * dt

        def padseq(t):
            return jnp.pad(t, [(0, 0), (0, pad)] + [(0, 0)] * (t.ndim - 2))
        hid_dt, A_full, Bp, Cp = (padseq(hid_dt), padseq(A_full), padseq(B), padseq(C))
        S = s + pad
        c, l = (S // CHUNK, CHUNK)
        hc = hid_dt.reshape(b, c, l, H_M, P_M)
        Ac = A_full.reshape(b, c, l, H_M).transpose(0, 3, 1, 2)
        rep = H_M // G_M
        Bh = jnp.repeat(Bp.reshape(b, c, l, G_M, N_M), rep, axis=3)
        Ch = jnp.repeat(Cp.reshape(b, c, l, G_M, N_M), rep, axis=3)
        A_cs = jnp.cumsum(Ac, axis=-1)
        L = jnp.exp(segsum(Ac))
        M = jnp.einsum('bcihn,bcjhn->bcijh', Ch, Bh) * jnp.transpose(L, (0, 2, 3, 4, 1))
        Y_diag = jnp.einsum('bcijh,bcjhp->bcihp', M, hc)
        decay_states = jnp.exp(A_cs[..., -1:] - A_cs)
        states = jnp.einsum('bclhn,bhcl,bclhp->bchpn', Bh, decay_states, hc)
        A_last = jnp.pad(A_cs[..., -1], ((0, 0), (0, 0), (1, 0)))
        decay_chunk = jnp.exp(segsum(A_last))
        states_cat = jnp.concatenate([jnp.zeros_like(states[:, :1]), states], axis=1)
        prev_states = jnp.einsum('bhij,bjhpn->bihpn', decay_chunk, states_cat)[:, :-1]
        Y_off = jnp.einsum('bclhn,bchpn,bhcl->bclhp', Ch, prev_states, jnp.exp(A_cs))
        y = (Y_diag + Y_off).reshape(b, S, H_M, P_M)[:, :s] + D_res
        y = y.reshape(b, s, D_INNER)
        yg = y * jax.nn.silu(gate)
        gsz = D_INNER // G_M
        ygr = yg.reshape(b, s, G_M, gsz)
        ygr = ygr * jax.lax.rsqrt(jnp.mean(ygr * ygr, axis=-1, keepdims=True) + EPS)
        y = ygr.reshape(b, s, D_INNER) * gnorm_w
        out = jnp.einsum('bsd,od->bso', y, out_proj_w)
        return residual + out

    def _L0_xattn_ref(x1, x2, x1_scale, x1_zp, x2_scale, x2_zp):
        import jax, jax.numpy as jnp
        import numpy as np
        QMIN = 0.0
        QMAX = 255.0

        def fake_quant(x, scale, zp):
            s = scale.reshape(())
            z = zp.reshape(())
            q = jnp.clip(jnp.round(x / s + z), QMIN, QMAX)
            return (q - z) * s
        q1 = fake_quant(x1, x1_scale, x1_zp)
        q2 = fake_quant(x2, x2_scale, x2_zp)
        return jnp.matmul(q1, q2)

    def _L0_ffn_ref(x, W_up, gate_w, expert_bias, lora_A, lora_B):
        import jax, jax.numpy as jnp
        import numpy as np
        NUM_EXPERTS = 4
        HIDDEN = 512
        RANK = 8
        ALPHA = 8.0
        SCALE = ALPHA / RANK
        B, T, H = x.shape
        E = gate_w.shape[0]
        x_flat = x.reshape(-1, H)
        logits = x_flat @ gate_w.T + expert_bias
        top1 = jnp.argmax(logits, axis=-1)
        one_hot = jax.nn.one_hot(top1, E, dtype=x_flat.dtype)
        base_out = jnp.einsum('bth,oh->bto', x, W_up)
        z = jnp.einsum('nh,erh->ner', x_flat, lora_A)
        d = jnp.einsum('ner,ehr->neh', z, lora_B) * SCALE
        delta = jnp.einsum('neh,ne->nh', d, one_hot)
        return base_out + delta.reshape(B, T, H)
    x = x + _L0_attn_ref(_layernorm(x, axis=-1), L0_attn_norm_w, L0_attn_in_proj_w, L0_attn_conv_w, L0_attn_conv_b, L0_attn_dt_bias, L0_attn_A_log, L0_attn_Dp, L0_attn_gnorm_w, L0_attn_out_proj_w)
    x = x + _L0_xattn_ref(_layernorm(x, axis=-1), ctx_4096, L0_xattn_x1_scale, L0_xattn_x1_zp, L0_xattn_x2_scale, L0_xattn_x2_zp)
    x = x + _L0_ffn_ref(_layernorm(x, axis=-1), L0_ffn_W_up, L0_ffn_gate_w, L0_ffn_expert_bias, L0_ffn_lora_A, L0_ffn_lora_B)
    return x

_drawn_inputs = setup_inputs


def setup_inputs(seed=0):
    import zlib

    import numpy as np

    out = dict(_drawn_inputs(seed))
    spreads = {'L0_attn_norm_w': (1.0, 0.2),
     'L0_attn_conv_b': (0.0, 0.1),
     'L0_attn_Dp': (1.0, 0.2),
     'L0_attn_gnorm_w': (1.0, 0.2),
     'L0_ffn_expert_bias': (0.0, 0.8)}
    factors = {'L0_attn_dt_bias': 8.0,
     'L0_attn_A_log': 4.63,
     'L0_ffn_gate_w': 8.0,
     'L0_ffn_lora_A': 8.0,
     'L0_ffn_lora_B': 8.0}
    for name, (base, spread) in spreads.items():
        noise = np.random.default_rng([zlib.crc32(name.encode()), seed]).standard_normal(out[name].shape)
        drawn = base * np.exp(spread * noise) if base else spread * noise
        out[name] = jnp.asarray(drawn.astype(out[name].dtype))
    for name, factor in factors.items():
        out[name] = (out[name] * factor).astype(out[name].dtype)
    return out
```

```python
from contextlib import ExitStack

import numpy as np

import concourse.bass as bass
from concourse import mybir

P = 128
D_MODEL = 512
KT = D_MODEL // P
TOK = 512
BLK = TOK // P
SEQS, SEQ = 2, 256
GROUPS = 8
PAIRS = 8
HEADS = 16
HD = 64
TILES = 2 * PAIRS + 2
CONVS = PAIRS + 2
WRING = 3
TAPS = 4
PAD_TILES = 4
EPS = 1e-5
MASKED = -1e30
EXPERTS, RANK = 4, 8
LORA = EXPERTS * RANK
ROUND = float(2 ** 23)
MID = 128.0

F32 = mybir.dt.float32
F32R = mybir.dt.float32r
BF16 = mybir.dt.bfloat16
ACT = mybir.ActivationFunctionType
ALU = mybir.AluOpType
AX_X = mybir.AxisListType.X

CREDIT = 2
O_CREDIT = BLK


def decoder_program(nc, x, w_in, conv_tab, d_tab, gn_tab, nw_tab, dtb_tab, alog_tab, w_out, ctx_in,
                    w_up, w_z, lora_b, consts, acs_rows, out):
    x_blocks = x.rearrange("b (c p) d -> p (b c) d", p=P)
    out_blocks = out.rearrange("b (c p) d -> p (b c) d", p=P)
    ctx_tiles = ctx_in.rearrange("b (k p) n -> p b k n", p=P)

    with ExitStack() as stack:
        def sem(name):
            return stack.enter_context(nc.semaphore(name))

        base = (nc.sbuf_base + 63) // 64 * 64
        top = [base]

        def put(name, shape, dt, at=None):
            size = int(np.prod(shape[1:])) * (2 if dt == BF16 else 4)
            where = top[0] if at is None else at[0]
            t = nc.alloc_sbuf_tensor_at(name, shape, dt, offset=where)
            if at is None:
                top[0] = where + (size + 31) // 32 * 32
            else:
                at[0] = where + (size + 31) // 32 * 32
            return t

        acc = put("acc", [P, BLK, D_MODEL], F32)
        ident = put("ident", [P, P], F32)
        ident_bf = put("ident_bf", [P, P], BF16)
        mask_bf = put("mask_bf", [P, BLK, P], BF16)
        ones_f = put("ones_f", [P, 2], F32)
        half_f = put("half_f", [P, BLK], F32)
        ones_r = put("ones_r", [2, P], F32R)
        conv_all = put("conv_all", [P, GROUPS, CONVS, TAPS + 1], F32)
        d_all = put("d_all", [P, GROUPS, PAIRS], F32)
        gn_all = put("gn_all", [P, GROUPS, PAIRS], F32)
        cst = put("cst", [P, 8], F32)
        nacs_all = put("nacs_all", [P, BLK, P], F32)
        dt_all = put("dt_all", [P, BLK, P], F32)
        dtd_all = put("dtd_all", [P, SEQS, P], F32)
        conv_g = put("conv_g", [P, CONVS, TAPS + 1], F32)
        d_g = put("d_g", [P, PAIRS], F32)
        gn_g = put("gn_g", [P, PAIRS], F32)
        nacs_g = put("nacs_g", [P, BLK, HEADS], F32)
        dt_g = put("dt_g", [P, BLK, HEADS], F32)
        dtd_g = put("dtd_g", [P, SEQS, HEADS], F32)
        ss_g = put("ss_g", [P, BLK], F32)
        rstd_g = put("rstd_g", [P, BLK], F32)
        stats = put("stats", [P, BLK, 6], F32)
        mv = put("mv", [P, BLK, 2], F32)
        var_e = put("var_e", [P, BLK], F32)
        rstd_t = put("rstd_t", [P, BLK], F32)

        hid = put("hid", [P, PAIRS, TOK], F32)
        gate = put("gate", [P, PAIRS, TOK], F32)
        b_t = put("b_t", [P, TOK], F32)
        c_t = put("c_t", [P, TOK], F32)
        b_tok = put("b_tok", [P, SEQS, P], F32)
        cb = put("cb", [P, BLK, P], F32)
        rows = put("rows", [2, 2, TOK], F32R)
        decay = put("decay", [P, 2, 2, TOK], F32)
        eacs = put("eacs", [P, 2, 2, SEQS, P], F32)
        c_dec = put("c_dec", [P, 2, 2, SEQS, P], F32)
        hc = put("hc", [P, 2, BLK, P], F32)
        hcd = put("hcd", [P, 2, SEQS, P], F32)
        prev = put("prev", [P, 2, SEQS, P], F32)
        y1 = put("y1", [P, TOK], F32)
        yg = put("yg", [P, 2, TOK], F32)
        ysq = put("ysq", [P, TOK], F32)
        ysum = put("ysum", [P, TOK], F32)

        cacc = put("cacc", [P, 2, SEQS, SEQ], F32)
        th = put("th", [P, 2, TOK], F32)
        thg = put("thg", [P, TOK], F32)
        wo_raw = put("wo_raw", [P, 2, D_MODEL], F32)
        region_h = [top[0]]
        h_hi = put("h_hi", [P, KT, TOK], F32R)
        h_lo = put("h_lo", [P, KT, TOK], F32R)
        region_w = [top[0]]
        w_raw = put("w_raw", [P, WRING, D_MODEL], F32)
        w_hi = put("w_hi", [P, WRING, D_MODEL], F32R)
        w_lo = put("w_lo", [P, WRING, D_MODEL], F32R)

        region_y = top[0]
        y_hi = put("y_hi", [P, PAIRS, TOK], F32R)
        y_lo = put("y_lo", [P, PAIRS, TOK], F32R)
        wo_hi = put("wo_hi", [P, PAIRS, D_MODEL], F32R)
        wo_lo = put("wo_lo", [P, PAIRS, D_MODEL], F32R)
        assert top[0] <= nc.sbuf_usable_end, (top[0], nc.sbuf_usable_end)

        at = [region_y]
        xt = put("xt", [P, BLK, D_MODEL], F32, at)
        hn = put("hn", [P, BLK, D_MODEL], F32, at)
        hs = put("hs", [P, BLK, D_MODEL], F32, at)
        wdt_raw = put("wdt_raw", [P, D_MODEL], F32, at)
        wdt_hi = put("wdt_hi", [P, D_MODEL], F32R, at)
        wdt_lo = put("wdt_lo", [P, D_MODEL], F32R, at)
        dtx = put("dtx", [P, TOK], F32, at)
        ex = put("ex", [P, TOK], F32, at)
        zz = put("zz", [P, 2, TOK], F32, at)
        poly = put("poly", [P, TOK], F32, at)
        dt_h = put("dt_h", [P, TOK], F32, at)
        ac_h = put("ac_h", [P, TOK], F32, at)
        acs_h = put("acs_h", [P, TOK], F32, at)
        acs_hi = put("acs_hi", [P, TOK], F32R, at)
        acs_lo = put("acs_lo", [P, TOK], F32R, at)
        dtd_h = put("dtd_h", [P, SEQS, P], F32, at)
        one_row = put("one_row", [P, P], F32, at)
        nw = put("nw", [P, KT], F32, at)
        dtb = put("dtb", [P, 1], F32, at)
        alog = put("alog", [P, 1], F32, at)
        neg_a = put("neg_a", [P, 1], F32, at)
        ms = put("ms", [P, BLK], F32, at)
        ms_e = put("ms_e", [P, BLK], F32, at)
        rms = put("rms", [P, BLK], F32, at)
        assert at[0] <= top[0]

        ctx_raw = put("ctx_raw", [P, KT, D_MODEL], F32, region_h)
        ctx_q = put("ctx_q", [P, KT, D_MODEL], F32, region_h)
        lvl2 = put("lvl2", [P, SEQS, KT, D_MODEL], BF16, region_w)
        wup = put("wup", [P, KT, D_MODEL], F32, region_w)
        assert region_h[0] <= region_w[0] and region_w[0] <= region_y
        at = [region_y]
        n_t = put("n_t", [P, BLK, D_MODEL], F32, at)
        q_a = put("q_a", [P, BLK, D_MODEL], F32, at)
        lvl1 = put("lvl1", [P, BLK, D_MODEL], BF16, at)
        lvl1_t = put("lvl1_t", [P, KT, TOK], BF16, at)
        col = put("col", [P, SEQS, D_MODEL], F32, at)
        n_tt = put("n_tt", [P, KT, TOK], F32, at)
        wz = put("wz", [P, KT, LORA + EXPERTS], F32, at)
        lb = put("lb", [LORA, D_MODEL], F32, at)
        ones_bf = put("ones_bf", [P, P], BF16, at)
        inv = put("inv", [P, 2], F32, at)
        shift = put("shift", [P, 2], F32, at)
        s12 = put("s12", [P, 4], F32, at)
        rsum = put("rsum", [P, BLK], F32, at)
        zl = put("zl", [P, BLK, LORA + EXPERTS], F32, at)
        lmax = put("lmax", [P, BLK], F32, at)
        hit = put("hit", [P, BLK, EXPERTS], F32, at)
        free_ = put("free_", [P, BLK, EXPERTS], F32, at)
        zm = put("zm", [P, BLK, LORA], F32, at)
        zm_t = put("zm_t", [LORA, BLK, P], F32, at)
        assert at[0] <= top[0]

        ps_p = [stack.enter_context(nc.psum_tensor(f"ps_p{i}", [P, TOK], F32)) for i in range(2)]
        ps_a = stack.enter_context(nc.psum_tensor("ps_a", [P, 2, TOK], F32))
        ps_t = stack.enter_context(nc.psum_tensor("ps_t", [P, TOK], F32))
        ps_y = stack.enter_context(nc.psum_tensor("ps_y", [P, TOK], F32))
        ps_o = stack.enter_context(nc.psum_tensor("ps_o", [P, TOK], F32))
        ps_x = stack.enter_context(nc.psum_tensor("ps_x", [P, TOK], F32))

        x_in = sem("x_in")
        tabs_in = sem("tabs_in")
        wdt_in = sem("wdt_in")
        w_in_s = [sem(f"w_in{i}") for i in range(WRING)]
        wo_in_s = [sem(f"wo_in{i}") for i in range(2)]
        rows_out = sem("rows_out")
        rows_in = sem("rows_in")
        ctx_in_s = sem("ctx_in_s")
        ffn_in = sem("ffn_in")
        stored = sem("stored")
        pool_pre = sem("pool_pre")
        vec_pre = sem("vec_pre")
        act_pre = sem("act_pre")
        pe_pre = sem("pe_pre")
        vec_tail = sem("vec_tail")
        act_tail = sem("act_tail")
        pool_tail = sem("pool_tail")
        pe_tail = sem("pe_tail")
        w_hi_made = sem("w_hi_made")
        w_lo_made = sem("w_lo_made")
        proj_made = sem("proj_made")
        tapped = sem("tapped")
        conved = sem("conved")
        conv_tanh = sem("conv_tanh")
        silu_made = sem("silu_made")
        gate_tanh = sem("gate_tanh")
        gate_made = sem("gate_made")
        tab_set = sem("tab_set")
        head_tabs = sem("head_tabs")
        hid_turned = sem("hid_turned")
        acs_spread = sem("acs_spread")
        acs_masked = sem("acs_masked")
        e_made = sem("e_made")
        l_made = sem("l_made")
        hc_made = sem("hc_made")
        hcd_made = sem("hcd_made")
        m_made = sem("m_made")
        cdec_made = sem("cdec_made")
        state_made = sem("state_made")
        prev_made = sem("prev_made")
        y_made = sem("y_made")
        y1_made = sem("y1_made")
        yg_made = sem("yg_made")
        ysq_made = sem("ysq_made")
        ysum_made = sem("ysum_made")
        y_hi_made = sem("y_hi_made")
        y_lo_made = sem("y_lo_made")
        b_turned = sem("b_turned")
        btok_made = sem("btok_made")
        cb_made = sem("cb_made")
        cb_kept = sem("cb_kept")
        wo_hi_made = sem("wo_hi_made")
        wo_lo_made = sem("wo_lo_made")
        ss_summed = sem("ss_summed")
        ss_kept = sem("ss_kept")
        rstd_made = sem("rstd_made")
        o_made = sem("o_made")
        o_added = sem("o_added")

        def past(eng, s, count):
            if isinstance(count, int) and count < 1:
                return
            eng.wait_ge(s, count)

        def ps_bf(k):
            return (ps_t if k % 2 == 0 else ps_y)[:, 0:TOK // 2].bitcast(BF16)

        last_group = GROUPS - 1

        block = stack.enter_context(nc.Block())

        @block.sync
        def _(sp):
            def load_w(p, t):
                past(sp, w_lo_made, TILES * p + t - WRING + 1)
                sp.dma_start(w_raw[:, t % WRING, :],
                             w_in[bass.ds(TILES * p + t, 1)].rearrange("o p d -> p (o d)")
                             ).then_inc(w_in_s[t % WRING], 16)

            def load_wo(g, u):
                past(sp, wo_lo_made, CREDIT + PAIRS * g + u - 1)
                sp.dma_start(wo_raw[:, u % 2, :],
                             w_out[bass.ds(PAIRS * g + u, 1)].rearrange("o p d -> p (o d)")
                             ).then_inc(wo_in_s[u % 2], 16)

            def load_rows(g, u):
                past(sp, acs_spread, PAIRS * g + u)
                sp.dma_start(rows[:].bitcast(F32), acs_rows[:, bass.ds(PAIRS * g + u, 1)].rearrange(
                    "s o h t -> s (o h) t")).then_inc(rows_in, 16)

            sp.dma_start(xt[:], x_blocks).then_inc(x_in, 16)
            sp.dma_start(wdt_raw[:], w_in[TILES * GROUPS]).then_inc(wdt_in, 16)
            for dst, src in ((nw, nw_tab), (dtb, dtb_tab), (alog, alog_tab), (d_all, d_tab),
                             (gn_all, gn_tab), (conv_all, conv_tab)):
                sp.dma_start(dst[:], src).then_inc(tabs_in, 16)
            sp.dma_start(cst[:], consts.to_broadcast([P, 8])).then_inc(tabs_in, 16)
            for t in range(5):
                load_w(0, t)
            sp.wait_ge(vec_pre, V_ACS_SPLIT)
            for i, part in enumerate((acs_hi, acs_lo)):
                sp.dma_start(acs_rows[i].rearrange("q h t -> (q h) t"), part[:].bitcast(F32)).then_inc(rows_out, 16)
            for u in range(PAIRS):
                load_w(0, 2 * u + 5)
                load_w(0, 2 * u + 6)
            load_w(0, TILES + 3)
            load_w(0, TILES + 4)
            sp.wait_ge(rows_out, 32)
            load_rows(0, 0)
            load_rows(0, 1)
            load_wo(0, 0)
            load_wo(0, 1)

            def step(g, u, ahead):
                if ahead:
                    load_w(g + 1, 2 * u + 5)
                if ahead or u + 2 < PAIRS:
                    load_rows(g, u + 2)
                    load_wo(g, u + 2)
                if ahead:
                    load_w(g + 1, 2 * u + 6)

            with sp.Fori(0, last_group) as g:
                for u in range(PAIRS):
                    step(g, u, True)
                load_w(g + 1, TILES + 3)
                load_w(g + 1, TILES + 4)
            for u in range(PAIRS):
                step(last_group, u, False)
            sp.wait_ge(proj_made, TILES * GROUPS)
            sp.wait_ge(w_lo_made, TILES * GROUPS + 2)
            for s_w in range(WRING):
                sp.wait_ge(w_in_s[s_w], 16 * ((TILES * GROUPS + 4 - s_w) // WRING + 1))
            sp.dma_start(ctx_raw[:], ctx_tiles[:, 0]).then_inc(ctx_in_s, 16)
            sp.wait_ge(o_made, O_CREDIT + BLK * GROUPS)
            sp.dma_start(wup[:], w_up).then_inc(ffn_in, 16)
            sp.dma_start(wz[:], w_z).then_inc(ffn_in, 16)
            sp.dma_start(lb[:], lora_b).then_inc(ffn_in, 16)
            sp.wait_ge(vec_tail, VT_Q0)
            sp.dma_start(ctx_raw[:], ctx_tiles[:, 1]).then_inc(ctx_in_s, 16)
            for b in range(BLK):
                sp.wait_ge(vec_tail, VT_OUT + b)
                sp.dma_start(out_blocks[:, b], acc[:, b, :]).then_inc(stored, 16)
            sp.wait_ge(stored, 16 * BLK)

        @block.gpsimd
        def _(pool):
            for i, ap in enumerate((ident, ident_bf, mask_bf)):
                nc.gpsimd.memset(ap[:], 0.0).then_inc(pool_pre, 1)
            nc.gpsimd.memset(ones_f[:], 1.0).then_inc(pool_pre, 1)
            nc.gpsimd.memset(half_f[:], -0.5).then_inc(pool_pre, 1)
            nc.gpsimd.memset(one_row[:], 1.0).then_inc(pool_pre, 1)
            pool.wait_ge(pool_pre, 6)
            for ap in (ident, ident_bf):
                nc.gpsimd.affine_select(out=ap[:], in_=ap[:], compare_op=ALU.not_equal, fill=1.0, base=0,
                                        pattern=[[-1, P]], channel_multiplier=1).then_inc(pool_pre, 1)
            nc.gpsimd.affine_select(out=mask_bf[:], in_=mask_bf[:], compare_op=ALU.is_ge, fill=MASKED,
                                    base=0, pattern=[[0, BLK], [1, P]],
                                    channel_multiplier=-1).then_inc(pool_pre, 1)
            pool.sem_inc(cdec_made, CREDIT)
            pool.sem_inc(y_lo_made, CREDIT)
            pool.wait_ge(vec_pre, V_VAR)
            nc.gpsimd.tensor_tensor(rstd_t[:], var_e[:], half_f[:], ALU.pow).then_inc(pool_pre, 1)
            pool.wait_ge(vec_pre, V_MS)
            nc.gpsimd.tensor_tensor(rms[:], ms_e[:], half_f[:], ALU.pow).then_inc(pool_pre, 1)

            def c_decayed(g, u):
                pool.wait_ge(e_made, PAIRS * g + u + 1)
                pool.wait_ge(y_made, CREDIT + PAIRS * g + u - 1)
                for h in range(2):
                    ins = nc.gpsimd.tensor_tensor(
                        c_dec[:, u % 2, h], eacs[:, u % 2, h],
                        c_t[:].rearrange("n (b c i) -> n b c i", b=SEQS, c=2)[:, :, 1, :], ALU.mult)
                ins.then_inc(cdec_made, 1)

            def low_part(g, u):
                pool.wait_ge(y_hi_made, PAIRS * g + u + 1)
                pool.wait_ge(o_made, O_CREDIT + BLK * g)
                nc.gpsimd.tensor_tensor(y_lo[:, u, :], yg[:, u % 2, :], y_hi[:, u, :].bitcast(F32),
                                        ALU.subtract).then_inc(y_lo_made, 1)

            def norm(g):
                pool.wait_ge(ss_kept, g + 1)
                pool.wait_ge(o_added, O_CREDIT + BLK * g)
                nc.gpsimd.tensor_tensor(rstd_g[:], ss_g[:], half_f[:], ALU.pow).then_inc(rstd_made, 1)

            pool.wait_ge(silu_made, CONVS)
            c_decayed(0, 0)

            def step(g, u, ahead):
                if u + 1 < PAIRS:
                    c_decayed(g, u + 1)
                low_part(g, u)

            with pool.Fori(0, last_group) as g:
                for u in range(PAIRS):
                    step(g, u, True)
                norm(g)
                pool.wait_ge(silu_made, CONVS * g + 2 * CONVS)
                c_decayed(g + 1, 0)
            for u in range(PAIRS):
                step(last_group, u, False)
            norm(last_group)
            pool.wait_ge(vec_tail, VT_VAR1)
            nc.gpsimd.tensor_tensor(rstd_t[:], var_e[:], half_f[:], ALU.pow).then_inc(pool_tail, 1)
            pool.wait_ge(vec_tail, VT_VAR2)
            nc.gpsimd.tensor_tensor(rstd_t[:], var_e[:], half_f[:], ALU.pow).then_inc(pool_tail, 1)

        @block.scalar
        def _(act):
            act.sem_inc(ysq_made, CREDIT)
            act.sem_inc(prev_made, CREDIT)
            for b in range(BLK):
                act.wait_ge(vec_pre, V_HN + b)
                nc.scalar.activation(hs[:, b, :], hn[:, b, :], ACT.Square,
                                     accum_out=ms[:, b:b + 1]).then_inc(act_pre, 1)
            act.wait_ge(tabs_in, 16 * 7)
            nc.scalar.activation(neg_a[:], alog[:], ACT.Exp).then_inc(act_pre, 1)
            act.wait_ge(wdt_in, 16)
            nc.scalar.activation(wdt_hi[:], wdt_raw[:], ACT.Copy).then_inc(act_pre, 1)

            def hi_part(p, t):
                act.wait_ge(w_in_s[t % WRING], 96 * p + 16 * (t // WRING + 1))
                past(act, proj_made, TILES * p + t - WRING + 1)
                nc.scalar.activation(w_hi[:, t % WRING, :], w_raw[:, t % WRING, :],
                                     ACT.Copy).then_inc(w_hi_made, 1)

            hi_part(0, 0)
            hi_part(0, 1)
            for k in range(KT):
                act.wait_ge(pe_pre, k + 1)
                nc.scalar.activation(h_hi[:, k, :], (ps_t if k % 2 == 0 else ps_y)[:], ACT.Copy,
                                     scale=nw[:, k:k + 1]).then_inc(act_pre, 1)
            act.wait_ge(vec_pre, V_DTX)
            nc.scalar.activation(ex[:], dtx[:], ACT.Abs).then_inc(act_pre, 1)
            act.wait_ge(act_pre, 11)
            nc.scalar.activation(ex[:], ex[:], ACT.Exp, scale=-1.0).then_inc(act_pre, 1)

            def tap(p, u):
                t = 2 * u if u < PAIRS else PAIRS + u
                act.wait_ge(proj_made, TILES * p + t + 1)
                past(act, silu_made, CONVS * p + u - 1)
                nc.scalar.activation(cacc[:, u % 2].rearrange("c b t -> c (b t)"), ps_p[t % 2][:],
                                     ACT.Identity, bias=conv_g[:, u, TAPS:TAPS + 1],
                                     scale=conv_g[:, u, TAPS - 1:TAPS]).then_inc(tapped, 1)

            def tanh_conv(p, u):
                act.wait_ge(conved, 3 * (CONVS * p + u) + 3)
                nc.scalar.activation(th[:, u % 2, :], cacc[:, u % 2].rearrange("c b t -> c (b t)"),
                                     ACT.Tanh).then_inc(conv_tanh, 1)

            def tanh_gate(p, u):
                act.wait_ge(proj_made, TILES * p + 2 * u + 2)
                past(act, gate_made, PAIRS * p + u)
                nc.scalar.activation(thg[:], ps_p[1][:], ACT.Tanh, scale=0.5).then_inc(gate_tanh, 1)

            def exp_rows(g, u):
                act.wait_ge(acs_spread, PAIRS * g + u + 1)
                act.wait_ge(cdec_made, CREDIT + PAIRS * g + u - 1)
                nc.scalar.activation(
                    eacs[:, u % 2], ps_a[:].rearrange("n h (b c i) -> n h b c i", b=SEQS, c=2)[:, :, :, 1, :],
                    ACT.Exp).then_inc(e_made, 1)

            def exp_decay(g, u):
                act.wait_ge(acs_masked, PAIRS * g + u + 1)
                act.wait_ge(y_made, CREDIT + PAIRS * g + u - 1)
                for h in range(2):
                    for b in range(BLK):
                        ins = nc.scalar.activation(
                            decay[:, u % 2, h, b * P:(b + 1) * P], ps_a[:, h, b * P:(b + 1) * P], ACT.Exp,
                            bias=nacs_g[:, b, 2 * u + h:2 * u + h + 1])
                ins.then_inc(l_made, 1)

            def keep_state(g, u):
                act.wait_ge(state_made, CREDIT + PAIRS * g + u + 1)
                act.wait_ge(y_made, CREDIT + PAIRS * g + u - 1)
                nc.scalar.copy(prev[:, u % 2], ps_x[:, 0:2 * P].rearrange("n (b c) -> n b c", b=SEQS)
                               ).then_inc(prev_made, 1)

            def high_and_square(g, u):
                act.wait_ge(yg_made, PAIRS * g + u + 1)
                act.wait_ge(o_made, O_CREDIT + BLK * g)
                nc.scalar.activation(y_hi[:, u, :], yg[:, u % 2, :], ACT.Copy).then_inc(y_hi_made, 1)
                act.wait_ge(ysum_made, CREDIT + PAIRS * g + u)
                nc.scalar.activation(ysq[:], yg[:, u % 2, :], ACT.Square).then_inc(ysq_made, 1)

            def hi_part_out(g, u):
                act.wait_ge(wo_in_s[u % 2], 64 * g + 16 * (u // 2 + 1))
                act.wait_ge(o_made, O_CREDIT + BLK * g)
                nc.scalar.activation(wo_hi[:, u, :], wo_raw[:, u % 2, :], ACT.Copy,
                                     scale=gn_g[:, u:u + 1]).then_inc(wo_hi_made, 1)

            def turn_b(g):
                act.wait_ge(b_turned, g + 1)
                past(act, state_made, CREDIT + PAIRS * g)
                nc.scalar.copy(b_tok[:], ps_t[:, 0:2 * P].rearrange("n (b c) -> n b c", b=SEQS)
                               ).then_inc(btok_made, 1)

            def project(p):
                for u in range(PAIRS):
                    hi_part(p, 2 * u + 2)
                    tap(p, u)
                    hi_part(p, 2 * u + 3)
                    tanh_conv(p, u)
                    tanh_gate(p, u)

            def last_tiles(p):
                tap(p, PAIRS)
                tap(p, PAIRS + 1)
                tanh_conv(p, PAIRS)
                tanh_conv(p, PAIRS + 1)
                hi_part(p, TILES)
                hi_part(p, TILES + 1)

            act.wait_ge(tab_set, 1)
            hi_part(0, 2)
            tap(0, 0)
            hi_part(0, 3)
            for b in range(SEQS):
                act.wait_ge(vec_pre, V_ACS)
                nc.scalar.activation(dtd_h[:, b, :], acs_h[:, 2 * b * P:(2 * b + 1) * P], ACT.Exp,
                                     scale=-1.0, bias=acs_h[:, (2 * b + 1) * P - 1:(2 * b + 1) * P]
                                     ).then_inc(act_pre, 1)
            tanh_conv(0, 0)
            tanh_gate(0, 0)
            act.wait_ge(pe_pre, PE_ACS_T)
            nc.scalar.activation(nacs_all[:].rearrange("t b h -> t (b h)"), ps_y[:], ACT.Copy,
                                 scale=-1.0).then_inc(act_pre, 1)
            for u in range(1, PAIRS):
                hi_part(0, 2 * u + 2)
                tap(0, u)
                hi_part(0, 2 * u + 3)
                tanh_conv(0, u)
                tanh_gate(0, u)
            last_tiles(0)
            turn_b(0)
            exp_rows(0, 0)
            act.wait_ge(head_tabs, 1)
            exp_decay(0, 0)
            keep_state(0, 0)

            def step(g, u, ahead):
                if u + 1 < PAIRS:
                    exp_rows(g, u + 1)
                    exp_decay(g, u + 1)
                high_and_square(g, u)
                if ahead:
                    hi_part(g + 1, 2 * u + 2)
                    tap(g + 1, u)
                    hi_part(g + 1, 2 * u + 3)
                if u + 1 < PAIRS:
                    keep_state(g, u + 1)
                if ahead:
                    tanh_conv(g + 1, u)
                hi_part_out(g, u)
                if ahead:
                    tanh_gate(g + 1, u)

            with act.Fori(0, last_group) as g:
                act.wait_ge(tab_set, g + 2)
                for u in range(PAIRS):
                    step(g, u, True)
                last_tiles(g + 1)
                turn_b(g + 1)
                exp_rows(g + 1, 0)
                act.wait_ge(head_tabs, g + 2)
                exp_decay(g + 1, 0)
                keep_state(g + 1, 0)
            act.wait_ge(tab_set, GROUPS + 1)
            for u in range(PAIRS):
                step(last_group, u, False)

            for k in range(KT):
                act.wait_ge(pe_tail, k + 1)
                nc.scalar.copy(lvl1_t[:, k, :], ps_bf(k)).then_inc(act_tail, 1)
            for k in range(KT):
                act.wait_ge(pe_tail, PT_N2 + k)
                nc.scalar.copy(n_tt[:, k, :], (ps_t if k % 2 == 0 else ps_y)[:]).then_inc(act_tail, 1)

        @block.tensor
        def _(pe):
            pe.sem_inc(y_made, CREDIT)
            pe.sem_inc(state_made, CREDIT)
            pe.sem_inc(o_made, O_CREDIT)
            pe.sem_inc(ss_summed, 1)

            def three(bank, stat_hi, stat_lo, mov_hi, mov_lo, first, last):
                nc.tensor.matmul(bank, stat_hi, mov_hi, start=first, stop=False)
                nc.tensor.matmul(bank, stat_lo, mov_hi, start=False, stop=False)
                return nc.tensor.matmul(bank, stat_hi, mov_lo, start=False, stop=last)

            pe.wait_ge(pool_pre, G_CONST)
            for k in range(KT):
                bank = ps_t if k % 2 == 0 else ps_y
                if k >= 2:
                    pe.wait_ge(vec_pre, V_HLO + k - 2)
                for b in range(BLK):
                    if k == 0:
                        pe.wait_ge(vec_pre, V_HS + b)
                    ins = nc.tensor.transpose(bank[:, b * P:(b + 1) * P], hs[:, b, k * P:(k + 1) * P],
                                              ident[:])
                ins.then_inc(pe_pre, 1)
            pe.wait_ge(vec_pre, V_WDT)
            for k in range(KT):
                pe.wait_ge(vec_pre, V_HLO + k)
                ins = three(ps_x[:], wdt_hi[:, k * P:(k + 1) * P], wdt_lo[:, k * P:(k + 1) * P],
                            h_hi[:, k, :], h_lo[:, k, :], k == 0, k == KT - 1)
            ins.then_inc(pe_pre, 1)

            def project(p, t):
                pe.wait_ge(w_lo_made, TILES * p + t + 1)
                if t == 0:
                    past(pe, conved, 3 * (CONVS * p - 1))
                elif t == 1:
                    past(pe, conved, 3 * CONVS * p)
                elif t % 2 == 0:
                    pe.wait_ge(conved, 3 * (CONVS * p + t // 2))
                else:
                    pe.wait_ge(gate_made, PAIRS * p + t // 2)
                s = t % WRING
                for k in range(KT):
                    w = slice(k * P, (k + 1) * P)
                    ins = three(ps_p[t % 2][:], w_hi[:, s, w], w_lo[:, s, w], h_hi[:, k, :], h_lo[:, k, :],
                                k == 0, k == KT - 1)
                ins.then_inc(proj_made, 1)

            def turn_hid(g, u):
                past(pe, hcd_made, PAIRS * g + u)
                pe.wait_ge(silu_made, CONVS * g + u + 1)
                for b in range(BLK):
                    ins = nc.tensor.transpose(ps_t[:, b * P:(b + 1) * P], hid[:, u, b * P:(b + 1) * P],
                                              ident[:])
                ins.then_inc(hid_turned, 1)

            def spread(g, u):
                pe.wait_ge(rows_in, 16 * PAIRS * g + 16 * (u + 1))
                past(pe, l_made, PAIRS * g + u)
                for h in range(2):
                    ins = nc.tensor.matmul(ps_a[:, h, :], ones_r[:], rows[:, h, :], start=True, stop=True)
                ins.then_inc(acs_spread, 1)

            def add_mask(g, u):
                pe.wait_ge(e_made, PAIRS * g + u + 1)
                for h in range(2):
                    ins = nc.tensor.matmul(ps_a[:, h, :], ident_bf[:],
                                           mask_bf[:].rearrange("j b i -> j (b i)"),
                                           start=False, stop=True, skip_group_check=True)
                ins.then_inc(acs_masked, 1)

            def states(g, u):
                pe.wait_ge(hcd_made, PAIRS * g + u + 1)
                if u == 0:
                    pe.wait_ge(cb_kept, g + 1)
                    pe.wait_ge(btok_made, g + 1)
                else:
                    pe.wait_ge(prev_made, CREDIT + PAIRS * g + u)
                for b in range(SEQS):
                    ins = nc.tensor.matmul(ps_x[:, b * P:(b + 1) * P], b_tok[:, b, :],
                                           hcd[:, u % 2, b, :], start=True, stop=True)
                ins.then_inc(state_made, 1)

            def scan(g, u):
                pe.wait_ge(m_made, PAIRS * g + u + 1)
                pe.wait_ge(hc_made, PAIRS * g + u + 1)
                pe.wait_ge(prev_made, CREDIT + PAIRS * g + u + 1)
                pe.wait_ge(cdec_made, CREDIT + PAIRS * g + u + 1)
                if u == 0:
                    pe.wait_ge(o_added, O_CREDIT + BLK * g)
                else:
                    pe.wait_ge(y1_made, PAIRS * g + u)
                r = u % 2
                for b in range(BLK):
                    for h in range(2):
                        ch = slice(h * HD, (h + 1) * HD)
                        dst = ps_y[ch, b * P:(b + 1) * P]
                        ins = nc.tensor.matmul(dst, hc[:, r, b, ch], decay[:, r, h, b * P:(b + 1) * P],
                                               start=True, stop=(b % 2 == 0))
                    if b % 2 == 1:
                        for h in range(2):
                            ch = slice(h * HD, (h + 1) * HD)
                            dst = ps_y[ch, b * P:(b + 1) * P]
                            ins = nc.tensor.matmul(dst, prev[:, r, b // 2, ch], c_dec[:, r, h, b // 2, :],
                                                   start=False, stop=True)
                ins.then_inc(y_made, 1)

            def group_products(g):
                pe.wait_ge(silu_made, CONVS * (g + 1))
                past(pe, hcd_made, PAIRS * g)
                for b in range(SEQS):
                    ins = nc.tensor.transpose(ps_t[:, b * P:(b + 1) * P],
                                              b_t[:, 2 * b * P:(2 * b + 1) * P], ident[:])
                ins.then_inc(b_turned, 1)
                if not (isinstance(g, int) and g == 0):
                    pe.wait_ge(ss_kept, g)
                for b in range(BLK):
                    ins = nc.tensor.matmul(ps_x[:, b * P:(b + 1) * P], b_t[:, b * P:(b + 1) * P],
                                           c_t[:, b * P:(b + 1) * P], start=True, stop=True)
                ins.then_inc(cb_made, 1)

            def sum_squares(g):
                pe.wait_ge(ysum_made, CREDIT + PAIRS * g + PAIRS)
                pe.wait_ge(prev_made, CREDIT + PAIRS * g + PAIRS)
                for b in range(BLK):
                    ins = nc.tensor.matmul(ps_x[:, b:b + 1], ysum[:, b * P:(b + 1) * P], ones_f[:, 0:1],
                                           start=True, stop=True)
                ins.then_inc(ss_summed, 1)

            def out_block(g, b):
                if b == 0:
                    pe.wait_ge(y_lo_made, CREDIT + PAIRS * g + PAIRS)
                    pe.wait_ge(wo_lo_made, CREDIT + PAIRS * g + PAIRS)
                if b == 1:
                    pe.wait_ge(y1_made, PAIRS * g + PAIRS)
                else:
                    pe.wait_ge(o_added, O_CREDIT + BLK * g + b - 1)
                bank = (ps_o if b % 2 == 0 else ps_y)[:]
                t = slice(b * P, (b + 1) * P)
                for u in range(PAIRS):
                    ins = three(bank, y_hi[:, u, t], y_lo[:, u, t], wo_hi[:, u, :], wo_lo[:, u, :],
                                u == 0, u == PAIRS - 1)
                ins.then_inc(o_made, 1)

            project(0, 0)
            project(0, 1)
            pe.wait_ge(vec_pre, V_ACS)
            for b in range(BLK):
                ins = nc.tensor.transpose(ps_y[:, b * P:(b + 1) * P], acs_h[:, b * P:(b + 1) * P], ident[:])
            ins.then_inc(pe_pre, 1)
            for b in range(BLK):
                ins = nc.tensor.transpose(ps_t[:, b * P:(b + 1) * P], dt_h[:, b * P:(b + 1) * P], ident[:])
            ins.then_inc(pe_pre, 1)
            pe.wait_ge(vec_pre, V_DTD)
            for b in range(SEQS):
                ins = nc.tensor.transpose(ps_x[:, b * P:(b + 1) * P], dtd_h[:, b, :], ident[:])
            ins.then_inc(pe_pre, 1)
            for t in range(2, TILES):
                project(0, t)
            pe.wait_ge(vec_pre, V_TOK)
            group_products(0)
            pe.wait_ge(btok_made, 1)
            turn_hid(0, 0)
            spread(0, 0)
            add_mask(0, 0)
            states(0, 0)

            def step(g, u, ahead):
                if u + 1 < PAIRS:
                    turn_hid(g, u + 1)
                    spread(g, u + 1)
                scan(g, u)
                if u + 1 < PAIRS:
                    add_mask(g, u + 1)
                if ahead:
                    project(g + 1, 2 * u)
                if u + 1 < PAIRS:
                    states(g, u + 1)
                if ahead:
                    project(g + 1, 2 * u + 1)

            with pe.Fori(0, last_group) as g:
                for u in range(PAIRS):
                    step(g, u, True)
                project(g + 1, TILES - 2)
                project(g + 1, TILES - 1)
                sum_squares(g)
                out_block(g, 0)
                out_block(g, 1)
                group_products(g + 1)
                pe.wait_ge(btok_made, g + 2)
                turn_hid(g + 1, 0)
                spread(g + 1, 0)
                out_block(g, 2)
                add_mask(g + 1, 0)
                out_block(g, 3)
                states(g + 1, 0)
            for u in range(PAIRS):
                step(last_group, u, False)
            sum_squares(last_group)
            for b in range(BLK):
                out_block(last_group, b)

            pe.wait_ge(o_added, O_CREDIT + BLK * GROUPS)
            for k in range(KT):
                if k >= 2:
                    pe.wait_ge(act_tail, k - 1)
                for b in range(BLK):
                    if k == 0:
                        pe.wait_ge(vec_tail, VT_LVL1 + b)
                    ins = nc.tensor.transpose(ps_bf(k)[:, b * P:(b + 1) * P],
                                              lvl1[:, b, k * P:(k + 1) * P], ident_bf[:])
                ins.then_inc(pe_tail, 1)
            for s in range(SEQS):
                pe.wait_ge(vec_tail, VT_LVL2 + VT_GAP * s)
                for k in range(KT):
                    ins = nc.tensor.matmul(ps_p[s][:], ones_bf[:], lvl2[:, s, k, :], start=(k == 0),
                                           stop=(k == KT - 1))
                ins.then_inc(pe_tail, 1)
            pe.wait_ge(act_tail, KT)
            for b in range(BLK):
                for k in range(KT):
                    ins = nc.tensor.matmul(ps_x[:, b:b + 1], lvl1_t[:, k, b * P:(b + 1) * P],
                                           ones_bf[:, 0:1], start=(k == 0), stop=(k == KT - 1))
            ins.then_inc(pe_tail, 1)
            banks = [ps_o, ps_a[:, 0, :], ps_a[:, 1, :], ps_t]
            for b in range(BLK):
                for k in range(KT):
                    ins = nc.tensor.matmul(banks[b][:], lvl1_t[:, k, b * P:(b + 1) * P], lvl2[:, b // 2, k, :],
                                           start=(k == 0), stop=(k == KT - 1))
                ins.then_inc(pe_tail, 1)
            for k in range(KT):
                bank = ps_t if k % 2 == 0 else ps_y
                if k >= 2:
                    pe.wait_ge(act_tail, KT + k - 1)
                for b in range(BLK):
                    if k == 0:
                        pe.wait_ge(vec_tail, VT_N2 + b)
                    ins = nc.tensor.transpose(bank[:, b * P:(b + 1) * P], n_t[:, b, k * P:(k + 1) * P],
                                              ident[:])
                ins.then_inc(pe_tail, 1)
            pe.wait_ge(ffn_in, 48)
            pe.wait_ge(act_tail, 2 * KT)
            nz = LORA + EXPERTS
            for b in range(BLK):
                for k in range(KT):
                    ins = nc.tensor.matmul(ps_x[:, b * nz:(b + 1) * nz], n_tt[:, k, b * P:(b + 1) * P],
                                           wz[:, k, :], start=(k == 0), stop=(k == KT - 1))
            ins.then_inc(pe_tail, 1)
            banks = [ps_o, ps_a[:, 0, :], ps_a[:, 1, :], ps_p[0]]
            for b in range(BLK):
                for k in range(KT):
                    nc.tensor.matmul(banks[b][:], n_tt[:, k, b * P:(b + 1) * P], wup[:, k, :],
                                     start=(k == 0), stop=False)
            pe.wait_ge(vec_tail, VT_ZM)
            for b in range(BLK):
                ins = nc.tensor.transpose(ps_t[0:LORA, b * P:(b + 1) * P], zm[:, b, :], ident[:])
            ins.then_inc(pe_tail, 1)
            pe.wait_ge(vec_tail, VT_ZMT)
            for b in range(BLK):
                nc.tensor.matmul(banks[b][:], zm_t[:, b, :], lb[:], start=False,
                                 stop=True).then_inc(pe_tail, 1)

        @block.vector
        def _(dve):
            pre = [0]

            def mark(ins):
                ins.then_inc(vec_pre, 1)
                pre[0] += 1
                return pre[0]

            dve.sem_inc(wo_lo_made, CREDIT)
            dve.sem_inc(ysum_made, CREDIT)
            dve.sem_inc(o_added, O_CREDIT)

            def layer_stats(mark_, s):
                pass

            dve.wait_ge(x_in, 16)
            for b in range(BLK):
                mark(nc.vector.bn_stats(stats[:, b, :], xt[:, b, :]))
            for b in range(BLK):
                dve.wait_ge(vec_pre, b + 1)
                mark(nc.vector.bn_aggr(mv[:, b, :], stats[:, b, :]))
            dve.wait_ge(vec_pre, pre[0])
            n = mark(nc.vector.tensor_scalar_add(var_e[:], mv[:, :, 1], EPS))
            assert n == V_VAR
            dve.wait_ge(pool_pre, G_CONST + 1)
            for b in range(BLK):
                n = mark(nc.vector.tensor_scalar(hn[:, b, :], xt[:, b, :], mv[:, b, 0:1], rstd_t[:, b:b + 1],
                                                 ALU.subtract, ALU.mult))
                assert n == V_HN + b
            for b in range(BLK):
                dve.wait_ge(vec_pre, V_HN + b)
                mark(nc.vector.tensor_tensor(acc[:, b, :], xt[:, b, :], hn[:, b, :], ALU.add))
            dve.wait_ge(act_pre, BLK)
            n = mark(nc.vector.tensor_scalar(ms_e[:], ms[:], 1.0 / D_MODEL, EPS, ALU.mult, ALU.add))
            assert n == V_MS
            dve.wait_ge(act_pre, 6)
            n = mark(nc.vector.tensor_tensor(wdt_lo[:], wdt_raw[:], wdt_hi[:].bitcast(F32), ALU.subtract))
            assert n == V_WDT
            mark(nc.vector.tensor_scalar_mul(neg_a[:], neg_a[:], -1.0))
            dve.wait_ge(pool_pre, G_CONST + 2)
            for b in range(BLK):
                n = mark(nc.vector.tensor_scalar(hs[:, b, :], hn[:, b, :], rms[:, b:b + 1], None, ALU.mult))
                assert n == V_HS + b
            n = mark(nc.vector.tensor_copy(ones_r[:], one_row[0:2, :]))
            mark(nc.vector.tensor_scalar_mul(conv_all[:], conv_all[:], 0.5))
            dve.wait_ge(vec_pre, pre[0])

            def conv_table(p):
                nc.vector.tensor_copy(conv_g[:], conv_all[:, bass.ds(p, 1)].rearrange(
                    "c o u k -> c (o u) k")).then_inc(tab_set, 1)

            conv_table(0)

            def lo_part(p, t):
                dve.wait_ge(w_hi_made, TILES * p + t + 1)
                s = t % WRING
                nc.vector.tensor_tensor(w_lo[:, s, :], w_raw[:, s, :], w_hi[:, s, :].bitcast(F32),
                                        ALU.subtract).then_inc(w_lo_made, 1)

            lo_part(0, 0)
            lo_part(0, 1)
            for k in range(KT):
                dve.wait_ge(act_pre, 7 + k)
                n = mark(nc.vector.scalar_tensor_tensor(
                    out=h_lo[:, k, :], in0=(ps_t if k % 2 == 0 else ps_y)[:], scalar=nw[:, k:k + 1],
                    in1=h_hi[:, k, :].bitcast(F32), op0=ALU.mult, op1=ALU.subtract))
                assert n == V_HLO + k
            dve.wait_ge(pe_pre, 5)
            n = mark(nc.vector.tensor_scalar(dtx[:], ps_x[:], dtb[:, 0:1], None, ALU.add))
            assert n == V_DTX
            dve.wait_ge(act_pre, 12)
            mark(nc.vector.tensor_scalar_add(poly[:], ex[:], 2.0))
            dve.wait_ge(vec_pre, pre[0])
            mark(nc.vector.reciprocal(zz[:, 1, :], poly[:]))
            dve.wait_ge(vec_pre, pre[0])
            mark(nc.vector.tensor_tensor(zz[:, 0, :], ex[:], zz[:, 1, :], ALU.mult))
            dve.wait_ge(vec_pre, pre[0])
            mark(nc.vector.tensor_tensor(zz[:, 1, :], zz[:, 0, :], zz[:, 0, :], ALU.mult))
            dve.wait_ge(vec_pre, pre[0])
            mark(nc.vector.tensor_scalar(poly[:], zz[:, 1, :], 1.0 / 17, 1.0 / 15, ALU.mult, ALU.add))
            for c in (13, 11, 9, 7, 5, 3, 1):
                dve.wait_ge(vec_pre, pre[0])
                mark(nc.vector.tensor_tensor(poly[:], poly[:], zz[:, 1, :], ALU.mult))
                dve.wait_ge(vec_pre, pre[0])
                mark(nc.vector.tensor_scalar_add(poly[:], poly[:], 1.0 / c))
            dve.wait_ge(vec_pre, pre[0])
            mark(nc.vector.scalar_tensor_tensor(out=poly[:], in0=poly[:], scalar=2.0, in1=zz[:, 0, :],
                                                op0=ALU.mult, op1=ALU.mult))
            dve.wait_ge(vec_pre, pre[0])
            mark(nc.vector.scalar_tensor_tensor(out=dt_h[:], in0=dtx[:], scalar=0.0, in1=poly[:],
                                                op0=ALU.max, op1=ALU.add))
            dve.wait_ge(vec_pre, pre[0])
            mark(nc.vector.tensor_scalar(ac_h[:], dt_h[:], neg_a[:, 0:1], None, ALU.mult))
            dve.wait_ge(vec_pre, pre[0])
            for b in range(BLK):
                t = slice(b * P, (b + 1) * P)
                n = mark(nc.vector.tensor_tensor_scan(acs_h[:, t], one_row[:], ac_h[:, t], 0.0,
                                                      ALU.mult, ALU.add))
            assert n == V_ACS
            dve.wait_ge(vec_pre, pre[0])
            mark(nc.vector.tensor_copy(acs_hi[:], acs_h[:]))
            dve.wait_ge(vec_pre, pre[0])
            n = mark(nc.vector.tensor_tensor(acs_lo[:], acs_h[:], acs_hi[:].bitcast(F32), ALU.subtract))
            assert n == V_ACS_SPLIT

            def conv(p, u):
                c = CONVS * p + u
                t = 2 * u if u < PAIRS else PAIRS + u
                dve.wait_ge(tapped, c + 1)
                src = ps_p[t % 2][:].rearrange("c (b t) -> c b t", b=SEQS)
                for i in range(1, TAPS):
                    if i > 1:
                        dve.wait_ge(conved, 3 * c + i - 1)
                    dst = cacc[:, u % 2, :, i:SEQ]
                    nc.vector.scalar_tensor_tensor(
                        out=dst, in0=src[:, :, 0:SEQ - i], scalar=conv_g[:, u, TAPS - 1 - i:TAPS - i],
                        in1=dst, op0=ALU.mult, op1=ALU.add).then_inc(conved, 1)

            def silu(p, u):
                c = CONVS * p + u
                dve.wait_ge(conv_tanh, c + 1)
                dst = hid[:, u, :] if u < PAIRS else (b_t if u == PAIRS else c_t)[:]
                nc.vector.scalar_tensor_tensor(
                    out=dst, in0=th[:, u % 2, :], scalar=1.0, in1=cacc[:, u % 2].rearrange("c b t -> c (b t)"),
                    op0=ALU.add, op1=ALU.mult).then_inc(silu_made, 1)

            def silu_gate(p, u):
                dve.wait_ge(gate_tanh, PAIRS * p + u + 1)
                nc.vector.scalar_tensor_tensor(out=gate[:, u, :], in0=thg[:], scalar=1.0, in1=ps_p[1][:],
                                               op0=ALU.add, op1=ALU.mult).then_inc(gate_made, 1)

            def tokens_hid(g, u):
                dve.wait_ge(hid_turned, PAIRS * g + u + 1)
                dve.wait_ge(y_made, CREDIT + PAIRS * g + u - 1)
                src = ps_t[:].rearrange("t (b h c) -> t b h c", b=BLK, h=2)
                heads = slice(2 * u, 2 * u + 2)
                nc.vector.tensor_tensor(
                    hc[:, u % 2].rearrange("t b (h c) -> t b h c", h=2), src,
                    dt_g[:, :, heads].unsqueeze(3).to_broadcast([P, BLK, 2, HD]), ALU.mult
                ).then_inc(hc_made, 1)
                dve.wait_ge(state_made, CREDIT + PAIRS * g + u - 1)
                nc.vector.tensor_tensor(
                    hcd[:, u % 2].rearrange("t b (h c) -> t b h c", h=2), src[:, 0:BLK:2],
                    dtd_g[:, :, heads].unsqueeze(3).to_broadcast([P, SEQS, 2, HD]), ALU.mult
                ).then_inc(hcd_made, 1)

            def mix(g, u):
                dve.wait_ge(l_made, PAIRS * g + u + 1)
                if u == 0:
                    dve.wait_ge(cb_kept, g + 1)
                m = decay[:, u % 2]
                nc.vector.tensor_tensor(m, m, cb[:].rearrange("j b i -> j (b i)").unsqueeze(1).to_broadcast(
                    [P, 2, TOK]), ALU.mult).then_inc(m_made, 1)

            def gated(g, u):
                dve.wait_ge(y_made, CREDIT + PAIRS * g + u + 1)
                nc.vector.scalar_tensor_tensor(out=y1[:], in0=hid[:, u, :], scalar=d_g[:, u:u + 1],
                                               in1=ps_y[:], op0=ALU.mult, op1=ALU.add).then_inc(y1_made, 1)
                dve.wait_ge(y1_made, PAIRS * g + u + 1)
                dve.wait_ge(ysq_made, CREDIT + PAIRS * g + u - 1)
                dve.wait_ge(y_lo_made, CREDIT + PAIRS * g + u - 1)
                nc.vector.tensor_tensor(yg[:, u % 2, :], y1[:], gate[:, u, :],
                                        ALU.mult).then_inc(yg_made, 1)

            def add_squares(g, u):
                dve.wait_ge(ysq_made, CREDIT + PAIRS * g + u + 1)
                if u == 0:
                    dve.wait_ge(ss_summed, g + 1)
                    ins = nc.vector.tensor_copy(ysum[:], ysq[:])
                else:
                    dve.wait_ge(ysum_made, CREDIT + PAIRS * g + u)
                    ins = nc.vector.tensor_tensor(ysum[:], ysum[:], ysq[:], ALU.add)
                ins.then_inc(ysum_made, 1)

            def lo_part_out(g, u):
                dve.wait_ge(wo_hi_made, PAIRS * g + u + 1)
                nc.vector.scalar_tensor_tensor(
                    out=wo_lo[:, u, :], in0=wo_raw[:, u % 2, :], scalar=gn_g[:, u:u + 1],
                    in1=wo_hi[:, u, :].bitcast(F32), op0=ALU.mult, op1=ALU.subtract
                ).then_inc(wo_lo_made, 1)

            def keep_squares(g):
                dve.wait_ge(ss_summed, g + 2)
                nc.vector.tensor_scalar(ss_g[:], ps_x[:, 0:BLK], 1.0 / (PAIRS * P), 4 * EPS, ALU.mult,
                                        ALU.add).then_inc(ss_kept, 1)

            def add_out(g, b):
                if b == 0:
                    dve.wait_ge(rstd_made, g + 1)
                dve.wait_ge(o_made, O_CREDIT + BLK * g + b + 1)
                dve.wait_ge(o_added, O_CREDIT + BLK * g + b - 3)
                nc.vector.scalar_tensor_tensor(
                    out=acc[:, b, :], in0=(ps_o if b % 2 == 0 else ps_y)[:], scalar=rstd_g[:, b:b + 1],
                    in1=acc[:, b, :], op0=ALU.mult, op1=ALU.add).then_inc(o_added, 1)

            def keep_cb(g):
                dve.wait_ge(cb_made, g + 1)
                nc.vector.tensor_copy(cb[:].rearrange("j b i -> j (b i)"), ps_x[:]).then_inc(cb_kept, 1)

            def group_tables(g):
                h = bass.ds(HEADS * g, HEADS)
                nc.vector.tensor_copy(nacs_g[:], nacs_all[:, :, h])
                nc.vector.tensor_copy(dt_g[:], dt_all[:, :, h])
                nc.vector.tensor_copy(dtd_g[:], dtd_all[:, :, h]).then_inc(head_tabs, 1)
                dve.wait_ge(head_tabs, g + 1)

            lo_part(0, 2)
            conv(0, 0)
            lo_part(0, 3)
            dve.wait_ge(act_pre, 14)
            n = mark(nc.vector.tensor_tensor(
                dtd_h[:], dtd_h[:], dt_h[:].rearrange("h (b c t) -> h b c t", b=SEQS, c=2)[:, :, 0, :],
                ALU.mult))
            assert n == V_DTD
            silu(0, 0)
            silu_gate(0, 0)
            dve.wait_ge(pe_pre, 7)
            mark(nc.vector.tensor_copy(dt_all[:].rearrange("t b h -> t (b h)"), ps_t[:]))
            dve.wait_ge(pe_pre, 8)
            mark(nc.vector.tensor_copy(dtd_all[:].rearrange("t b h -> t (b h)"), ps_x[:, 0:2 * P]))
            dve.wait_ge(act_pre, 15)
            dve.wait_ge(vec_pre, pre[0])
            n = mark(nc.vector.tensor_copy(ones_f[:, 1:2], ones_f[:, 0:1]))
            assert n == V_TOK
            for u in range(1, PAIRS):
                lo_part(0, 2 * u + 2)
                conv(0, u)
                lo_part(0, 2 * u + 3)
                silu(0, u)
                silu_gate(0, u)
            for u in (PAIRS, PAIRS + 1):
                conv(0, u)
            for u in (PAIRS, PAIRS + 1):
                silu(0, u)
            lo_part(0, TILES)
            lo_part(0, TILES + 1)
            group_tables(0)
            keep_cb(0)
            tokens_hid(0, 0)
            mix(0, 0)

            def set_tables(g, ahead):
                nc.vector.tensor_copy(d_g[:], d_all[:, bass.ds(g, 1)].rearrange("c o u -> c (o u)"))
                ins = nc.vector.tensor_copy(gn_g[:], gn_all[:, bass.ds(g, 1)].rearrange("c o u -> c (o u)"))
                if ahead:
                    conv_table(g + 1)
                else:
                    ins.then_inc(tab_set, 1)
                dve.wait_ge(tab_set, g + 2)

            def step(g, u, ahead):
                if u + 1 < PAIRS:
                    tokens_hid(g, u + 1)
                gated(g, u)
                if u + 1 < PAIRS:
                    mix(g, u + 1)
                if ahead:
                    lo_part(g + 1, 2 * u + 2)
                    conv(g + 1, u)
                add_squares(g, u)
                if ahead:
                    lo_part(g + 1, 2 * u + 3)
                    silu(g + 1, u)
                lo_part_out(g, u)
                if ahead:
                    silu_gate(g + 1, u)

            with dve.Fori(0, last_group) as g:
                set_tables(g, True)
                for u in range(PAIRS):
                    step(g, u, True)
                conv(g + 1, PAIRS)
                conv(g + 1, PAIRS + 1)
                silu(g + 1, PAIRS)
                dve.wait_ge(cdec_made, CREDIT + PAIRS * g + PAIRS)
                silu(g + 1, PAIRS + 1)
                lo_part(g + 1, TILES)
                lo_part(g + 1, TILES + 1)
                keep_squares(g)
                group_tables(g + 1)
                add_out(g, 0)
                add_out(g, 1)
                keep_cb(g + 1)
                tokens_hid(g + 1, 0)
                add_out(g, 2)
                mix(g + 1, 0)
                add_out(g, 3)
            set_tables(last_group, False)
            for u in range(PAIRS):
                step(last_group, u, False)
            keep_squares(last_group)
            for b in range(BLK):
                add_out(last_group, b)

            tail = [0]

            def note(ins):
                ins.then_inc(vec_tail, 1)
                tail[0] += 1
                return tail[0]

            def sync():
                dve.wait_ge(vec_tail, tail[0])

            def variances():
                for b in range(BLK):
                    note(nc.vector.bn_stats(stats[:, b, :], acc[:, b, :]))
                sync()
                for b in range(BLK):
                    note(nc.vector.bn_aggr(mv[:, b, :], stats[:, b, :]))
                sync()
                return note(nc.vector.tensor_scalar_add(var_e[:], mv[:, :, 1], EPS))

            dve.wait_ge(o_made, O_CREDIT + BLK * GROUPS)
            note(nc.vector.memset(ones_bf[:], 1.0))
            note(nc.vector.reciprocal(inv[:, 0:1], cst[:, 0:1]))
            note(nc.vector.reciprocal(inv[:, 1:2], cst[:, 2:3]))
            note(nc.vector.tensor_scalar(shift[:, 0:1], cst[:, 1:2], -1.0, MID, ALU.mult, ALU.add))
            note(nc.vector.tensor_scalar(shift[:, 1:2], cst[:, 3:4], -1.0, MID, ALU.mult, ALU.add))
            note(nc.vector.tensor_tensor(s12[:, 0:1], cst[:, 0:1], cst[:, 2:3], ALU.mult))
            sync()
            note(nc.vector.tensor_tensor(s12[:, 1:2], s12[:, 0:1], shift[:, 0:1], ALU.mult))
            note(nc.vector.tensor_tensor(s12[:, 2:3], s12[:, 0:1], shift[:, 1:2], ALU.mult))
            sync()
            note(nc.vector.scalar_tensor_tensor(out=s12[:, 3:4], in0=s12[:, 1:2], scalar=float(D_MODEL),
                                                in1=shift[:, 1:2], op0=ALU.mult, op1=ALU.mult))
            dve.wait_ge(o_added, O_CREDIT + BLK * GROUPS)
            n = variances()
            assert n == VT_VAR1, n

            def levels(dst, src, mid, i):
                note(nc.vector.tensor_scalar(mid, src, inv[:, i:i + 1], cst[:, 2 * i + 1:2 * i + 2],
                                             ALU.mult, ALU.add))
                sync()
                note(nc.vector.tensor_scalar(mid, mid, 0.0, 255.0, ALU.max, ALU.min))
                sync()
                return note(nc.vector.tensor_scalar(dst, mid, ROUND, -(ROUND + MID), ALU.add, ALU.add))

            dve.wait_ge(ctx_in_s, 16)
            n = levels(lvl2[:, 0], ctx_raw[:], ctx_q[:], 1)
            assert n == VT_LVL2, n
            assert n - 2 == VT_Q0
            dve.wait_ge(pool_tail, 1)
            for b in range(BLK):
                note(nc.vector.tensor_scalar(n_t[:, b, :], acc[:, b, :], mv[:, b, 0:1], rstd_t[:, b:b + 1],
                                             ALU.subtract, ALU.mult))
            sync()
            for b in range(BLK):
                note(nc.vector.tensor_scalar(q_a[:, b, :], n_t[:, b, :], inv[:, 0:1], cst[:, 1:2],
                                             ALU.mult, ALU.add))
            sync()
            for b in range(BLK):
                note(nc.vector.tensor_scalar(q_a[:, b, :], q_a[:, b, :], 0.0, 255.0, ALU.max, ALU.min))
            sync()
            for b in range(BLK):
                n = note(nc.vector.tensor_scalar(lvl1[:, b, :], q_a[:, b, :], ROUND, -(ROUND + MID), ALU.add,
                                                 ALU.add))
                assert n == VT_LVL1 + b, n
            dve.wait_ge(ctx_in_s, 32)
            n = levels(lvl2[:, 1], ctx_raw[:], ctx_q[:], 1)
            assert n == VT_LVL2 + VT_GAP, n
            for s in range(SEQS):
                dve.wait_ge(pe_tail, KT + 1 + s)
                note(nc.vector.tensor_scalar(col[:, s, :], ps_p[s][:], s12[:, 1:2], s12[:, 3:4], ALU.mult,
                                             ALU.add))
            sync()
            for b in range(BLK):
                note(nc.vector.tensor_tensor(acc[:, b, :], acc[:, b, :], col[:, b // 2, :], ALU.add))
            dve.wait_ge(pe_tail, KT + 3)
            note(nc.vector.tensor_scalar(rsum[:], ps_x[:, 0:BLK], s12[:, 2:3], None, ALU.mult))
            sync()
            for b in range(BLK):
                note(nc.vector.tensor_scalar(acc[:, b, :], acc[:, b, :], rsum[:, b:b + 1], None, ALU.add))
            sync()
            banks = [ps_o, ps_a[:, 0, :], ps_a[:, 1, :], ps_t]
            for b in range(BLK):
                dve.wait_ge(pe_tail, KT + 4 + b)
                note(nc.vector.scalar_tensor_tensor(out=acc[:, b, :], in0=banks[b][:], scalar=s12[:, 0:1],
                                                    in1=acc[:, b, :], op0=ALU.mult, op1=ALU.add))
            sync()
            n = variances()
            assert n == VT_VAR2, n
            dve.wait_ge(pool_tail, 2)
            for b in range(BLK):
                n = note(nc.vector.tensor_scalar(n_t[:, b, :], acc[:, b, :], mv[:, b, 0:1],
                                                 rstd_t[:, b:b + 1], ALU.subtract, ALU.mult))
                assert n == VT_N2 + b, n
            dve.wait_ge(pe_tail, PT_Z)
            note(nc.vector.tensor_copy(zl[:].rearrange("t b z -> t (b z)"),
                                       ps_x[:, 0:BLK * (LORA + EXPERTS)]))
            sync()
            logits = zl[:, :, LORA:LORA + EXPERTS]
            note(nc.vector.tensor_tensor(logits, logits, cst[:, 4:8].unsqueeze(1).to_broadcast(
                [P, BLK, EXPERTS]), ALU.add))
            sync()
            note(nc.vector.tensor_reduce(lmax[:], logits, AX_X, ALU.max))
            sync()
            note(nc.vector.tensor_tensor(hit[:], logits, lmax[:].unsqueeze(2).to_broadcast(
                [P, BLK, EXPERTS]), ALU.is_equal))
            sync()
            note(nc.vector.tensor_scalar(free_[:], hit[:], -1.0, 1.0, ALU.mult, ALU.add))
            sync()
            for e in range(1, EXPERTS):
                note(nc.vector.tensor_tensor(hit[:, :, e:], hit[:, :, e:],
                                             free_[:, :, e - 1:e].to_broadcast([P, BLK, EXPERTS - e]),
                                             ALU.mult))
                sync()
            n = note(nc.vector.tensor_tensor(
                zm[:].rearrange("t b (e r) -> t b e r", e=EXPERTS),
                zl[:, :, 0:LORA].rearrange("t b (e r) -> t b e r", e=EXPERTS),
                hit[:].unsqueeze(3).to_broadcast([P, BLK, EXPERTS, RANK]), ALU.mult))
            assert n == VT_ZM, n
            dve.wait_ge(pe_tail, PT_Z + 1)
            n = note(nc.vector.tensor_copy(zm_t[:].rearrange("z b t -> z (b t)"), ps_t[0:LORA, :]))
            assert n == VT_ZMT, n
            banks = [ps_o, ps_a[:, 0, :], ps_a[:, 1, :], ps_p[0]]
            for b in range(BLK):
                dve.wait_ge(pe_tail, PT_Z + 2 + b)
                n = note(nc.vector.tensor_tensor(acc[:, b, :], acc[:, b, :], banks[b][:], ALU.add))
                assert n == VT_OUT + b, n


G_CONST = 9
V_VAR = 2 * BLK + 1
V_HN = V_VAR + 1
V_MS = V_HN + 2 * BLK
V_WDT = V_MS + 1
V_HS = V_WDT + 2
V_HLO = V_HS + BLK + 2
V_DTX = V_HLO + KT
V_ACS = V_DTX + 5 + 14 + 3 + BLK
V_ACS_SPLIT = V_ACS + 2
V_DTD = V_ACS_SPLIT + 1
V_TOK = V_DTD + 3
PE_ACS_T = 6
VT_VAR1 = 18
VT_LVL2 = VT_VAR1 + 3
VT_Q0 = VT_LVL2 - 2
VT_LVL1 = VT_LVL2 + 13
VT_GAP = 16 + 3
VT_VAR2 = VT_LVL2 + VT_GAP + 2 + 4 + 1 + 4 + 4 + 9
VT_N2 = VT_VAR2 + 1
VT_ZM = VT_N2 + 3 + 9
VT_ZMT = VT_ZM + 1
VT_OUT = VT_ZMT + 1
PT_N2 = 12
PT_Z = 16


def kernel(**inputs):
    import concourse.bacc as bacc
    from concourse.bass_utils import run_bass_kernel_spmd as run

    a = {k: np.asarray(v) for k, v in inputs.items()}
    d_inner = GROUPS * PAIRS * P
    tiles = []
    for g in range(GROUPS):
        for u in range(PAIRS):
            c = (g * PAIRS + u) * P
            tiles += [d_inner + c, c]
        tiles += [2 * d_inner + g * P, 2 * d_inner + (GROUPS + g) * P]
    tiles.append(2 * d_inner + 2 * GROUPS * P)
    w = a["L0_attn_in_proj_w"]
    w_in = np.concatenate([w[t:t + P] for t in tiles]).reshape(len(tiles), P, KT, P).transpose(0, 3, 2, 1)
    w_in = w_in.reshape(len(tiles), P, D_MODEL)
    w_in = np.concatenate([w_in, np.zeros((PAD_TILES, P, D_MODEL), w_in.dtype)])
    conv = np.concatenate([a["L0_attn_conv_w"], a["L0_attn_conv_b"][:, None]], axis=1)
    hid_c = conv[:d_inner].reshape(GROUPS, PAIRS, P, TAPS + 1)
    bc_c = conv[d_inner:].reshape(2, GROUPS, 1, P, TAPS + 1)
    conv_tab = np.concatenate([hid_c, bc_c[0], bc_c[1]], axis=1).transpose(2, 0, 1, 3)
    arrays = {
        "x": a["x"],
        "w_in": w_in,
        "conv_tab": conv_tab,
        "d_tab": np.repeat(a["L0_attn_Dp"], HD).reshape(GROUPS, PAIRS, P).transpose(2, 0, 1),
        "gn_tab": a["L0_attn_gnorm_w"].reshape(GROUPS, PAIRS, P).transpose(2, 0, 1),
        "nw_tab": a["L0_attn_norm_w"].reshape(KT, P).T,
        "dtb_tab": a["L0_attn_dt_bias"].reshape(P, 1),
        "alog_tab": a["L0_attn_A_log"].reshape(P, 1),
        "w_out": a["L0_attn_out_proj_w"].T.reshape(GROUPS * PAIRS, P, D_MODEL),
        "ctx_in": a["ctx_4096"],
        "w_up": a["L0_ffn_W_up"].T.reshape(KT, P, D_MODEL).transpose(1, 0, 2),
        "w_z": np.concatenate([a["L0_ffn_lora_A"].reshape(LORA, D_MODEL), a["L0_ffn_gate_w"]]).T.reshape(
            KT, P, LORA + EXPERTS).transpose(1, 0, 2),
        "lora_b": a["L0_ffn_lora_B"].transpose(0, 2, 1).reshape(LORA, D_MODEL),
        "consts": np.concatenate([a["L0_xattn_x1_scale"], a["L0_xattn_x1_zp"], a["L0_xattn_x2_scale"],
                                  a["L0_xattn_x2_zp"], a["L0_ffn_expert_bias"]]).reshape(1, 8),
    }
    nc = bacc.Bacc("TRN2", target_bir_lowering=False, num_devices=1)
    feeds, args = {}, []
    for name, value in arrays.items():
        value = np.ascontiguousarray(value)
        feeds["in_" + name] = value
        args.append(nc.dram_tensor("in_" + name, value.shape, F32, kind="ExternalInput").ap())
    acs_rows = nc.dram_tensor("acs_rows", (2, GROUPS * PAIRS, 2, TOK), F32, kind="Internal").ap()
    out = nc.dram_tensor("out", a["x"].shape, F32, kind="ExternalOutput").ap()
    decoder_program(nc, *args, acs_rows, out)
    result = run(nc, [feeds], core_ids=[0])
    return result.results[0]["out"]
```

```python
from contextlib import ExitStack

import numpy as np

import concourse.bass as bass
from concourse import mybir

P = 128
D_MODEL = 512
KT = D_MODEL // P
TOK = 512
BLK = TOK // P
SEQS, SEQ = 2, 256
GROUPS = 8
PAIRS = 8
HEADS = 16
HD = 64
TILES = 2 * PAIRS + 2
CONVS = PAIRS + 2
WRING = 3
LEAD = 2
RING = 4
HALF = PAIRS // 2
TAPS = 4
PAD_TILES = 4
ROW = 32
EPS = 1e-5
MASKED = -1e30
EXPERTS, RANK = 4, 8
LORA = EXPERTS * RANK
ROUND = float(2 ** 23)
MID = 128.0

F32 = mybir.dt.float32
F32R = mybir.dt.float32r
BF16 = mybir.dt.bfloat16
ACT = mybir.ActivationFunctionType
ALU = mybir.AluOpType
AX_X = mybir.AxisListType.X

CREDIT = 2
O_CREDIT = 2 * BLK
A_CREDIT = BLK


def decoder_program(nc, x, w_in, conv_tab, d_tab, gn_tab, nw_tab, dtb_tab, alog_tab, w_out, ctx_in,
                    w_up, w_z, lora_b, consts, acs_rows, out):
    x_blocks = x.rearrange("b (c p) d -> p (b c) d", p=P)
    out_blocks = out.rearrange("b (c p) d -> p (b c) d", p=P)
    ctx_tiles = ctx_in.rearrange("b (k p) n -> p b k n", p=P)

    with ExitStack() as stack:
        def sem(name):
            return stack.enter_context(nc.semaphore(name))

        base = (nc.sbuf_base + 63) // 64 * 64
        top = [base]
        place = {}

        def put(name, shape, dt, at=None):
            size = int(np.prod(shape[1:])) * (2 if dt == BF16 else 4)
            where = top[0] if at is None else at[0]
            t = nc.alloc_sbuf_tensor_at(name, shape, dt, offset=where)
            place[name] = where
            if at is None:
                top[0] = where + (size + 31) // 32 * 32
            else:
                at[0] = where + (size + 31) // 32 * 32
            return t

        acc = put("acc", [P, BLK, D_MODEL], F32)
        ident = put("ident", [P, P], F32)
        ident_bf = put("ident_bf", [P, P], BF16)
        mask_bf = put("mask_bf", [P, BLK, P], BF16)
        ones_f = put("ones_f", [P, 2], F32)
        half_f = put("half_f", [P, BLK], F32)
        ones_r = put("ones_r", [ROW + 2, P], F32R)
        conv_all = put("conv_all", [P, GROUPS, CONVS, TAPS + 1], F32)
        d_all = put("d_all", [P, GROUPS, PAIRS], F32)
        gn_all = put("gn_all", [P, GROUPS, PAIRS], F32)
        cst = put("cst", [P, 8], F32)
        nacs_all = put("nacs_all", [P, BLK, P], F32)
        dt_all = put("dt_all", [P, BLK, P], F32)
        dtd_all = put("dtd_all", [P, SEQS, P], F32)
        conv_g = put("conv_g", [P, CONVS, TAPS + 1], F32)
        d_g = put("d_g", [P, PAIRS], F32)
        gn_g = put("gn_g", [P, PAIRS], F32)
        nacs_g = put("nacs_g", [P, BLK, HEADS], F32)
        dt_g = put("dt_g", [P, BLK, HEADS], F32)
        dtd_g = put("dtd_g", [P, SEQS, HEADS], F32)
        ss_g = put("ss_g", [P, BLK], F32)
        rstd_g = put("rstd_g", [P, BLK], F32)
        stats = put("stats", [P, BLK, 6], F32)
        mv = put("mv", [P, BLK, 2], F32)
        var_e = put("var_e", [P, BLK], F32)
        rstd_t = put("rstd_t", [P, BLK], F32)

        hid = put("hid", [P, RING, TOK], F32)
        gate = put("gate", [P, RING, TOK], F32)
        b_t = put("b_t", [P, TOK], F32)
        c_t = put("c_t", [P, TOK], F32)
        c_cur = put("c_cur", [P, SEQS, P], F32)
        b_tok = put("b_tok", [P, SEQS, P], F32)
        cb = put("cb", [P, BLK, P], F32)
        rows = put("rows", [ROW + 2, 2, TOK], F32R)
        decay = put("decay", [P, 2, 2, TOK], F32)
        eacs = put("eacs", [P, 2, 2, SEQS, P], F32)
        c_dec = put("c_dec", [P, 2, 2, SEQS, P], F32)
        hc = put("hc", [P, 2, BLK, P], F32)
        hcd = put("hcd", [P, 2, SEQS, P], F32)
        prev = put("prev", [P, 2, SEQS, P], F32)
        y1 = put("y1", [P, TOK], F32)
        yg = put("yg", [P, 2, TOK], F32)
        ysq = put("ysq", [P, 2, TOK], F32)
        ysum = put("ysum", [P, TOK], F32)
        o_part = put("o_part", [P, BLK, D_MODEL], F32)

        cacc = put("cacc", [P, 2, SEQS, SEQ], F32)
        th = put("th", [P, 2, TOK], F32)
        thg = put("thg", [P, TOK], F32)
        wo_raw = put("wo_raw", [P, 2, D_MODEL], F32)
        h_hi = put("h_hi", [P, KT, TOK], F32R)
        h_lo = put("h_lo", [P, KT, TOK], F32R)
        w_raw = put("w_raw", [P, WRING, D_MODEL], F32)
        w_hi = put("w_hi", [P, WRING, D_MODEL], F32R)
        w_lo = put("w_lo", [P, WRING, D_MODEL], F32R)

        y_hi = put("y_hi", [P, PAIRS, TOK], F32R)
        y_lo = put("y_lo", [P, PAIRS, TOK], F32R)
        wo_hi = put("wo_hi", [P, PAIRS, D_MODEL], F32R)
        wo_lo = put("wo_lo", [P, PAIRS, D_MODEL], F32R)
        assert top[0] <= nc.sbuf_usable_end, (top[0], nc.sbuf_usable_end)

        at = [place["y_hi"]]
        xt = put("xt", [P, BLK, D_MODEL], F32, at)
        hs = put("hs", [P, BLK, D_MODEL], F32, at)
        wdt_raw = put("wdt_raw", [P, D_MODEL], F32, at)
        wdt_hi = put("wdt_hi", [P, D_MODEL], F32R, at)
        wdt_lo = put("wdt_lo", [P, D_MODEL], F32R, at)
        dtx = put("dtx", [P, TOK], F32, at)
        dt_abs = put("dt_abs", [P, TOK], F32, at)
        ex = put("ex", [P, TOK], F32, at)
        zz = put("zz", [P, 2, TOK], F32, at)
        poly = put("poly", [P, TOK], F32, at)
        dt_h = put("dt_h", [P, TOK], F32, at)
        ac_h = put("ac_h", [P, TOK], F32, at)
        acs_h = put("acs_h", [P, TOK], F32, at)
        acs_hi = put("acs_hi", [P, TOK], F32R, at)
        acs_lo = put("acs_lo", [P, TOK], F32R, at)
        dtd_h = put("dtd_h", [P, SEQS, P], F32, at)
        one_row = put("one_row", [P, P], F32, at)
        nw = put("nw", [P, KT], F32, at)
        dtb = put("dtb", [P, 1], F32, at)
        alog = put("alog", [P, 1], F32, at)
        neg_a = put("neg_a", [P, 1], F32, at)
        ms_e = put("ms_e", [P, BLK], F32, at)
        rms = put("rms", [P, BLK], F32, at)
        both = put("both", [P, BLK], F32, at)
        assert at[0] <= top[0]

        at = [place["h_hi"]]
        ctx_raw = put("ctx_raw", [P, SEQS, KT, D_MODEL], F32, at)
        lvl2 = put("lvl2", [P, SEQS, KT, D_MODEL], BF16, at)
        wup = put("wup", [P, KT, D_MODEL], F32, at)
        wz = put("wz", [P, KT, LORA + EXPERTS], F32, at)
        ones_bf = put("ones_bf", [P, P], BF16, at)
        inv = put("inv", [P, 2], F32, at)
        shift = put("shift", [P, 2], F32, at)
        s12 = put("s12", [P, 4], F32, at)
        rsum = put("rsum", [P, BLK], F32, at)
        assert at[0] <= place["y_hi"]
        at = [place["hid"]]
        n_t = put("n_t", [P, BLK, D_MODEL], F32, at)
        n_tt = put("n_tt", [P, KT, TOK], F32, at)
        assert at[0] <= place["b_t"]
        at = [place["decay"]]
        lvl1 = put("lvl1", [P, BLK, D_MODEL], BF16, at)
        lvl1_t = put("lvl1_t", [P, KT, TOK], BF16, at)
        col = put("col", [P, SEQS, D_MODEL], F32, at)
        lb = put("lb", [LORA, D_MODEL], F32, at)
        zm_t = put("zm_t", [LORA, BLK, P], F32, at)
        zl = put("zl", [P, BLK, LORA + EXPERTS], F32, at)
        lmax = put("lmax", [P, BLK], F32, at)
        hit = put("hit", [P, BLK, EXPERTS], F32, at)
        none_yet = put("none_yet", [P, BLK, EXPERTS], F32, at)
        zm = put("zm", [P, BLK, LORA], F32, at)
        assert at[0] <= place["y1"]

        ps_p = [stack.enter_context(nc.psum_tensor(f"ps_p{i}", [P, TOK], F32)) for i in range(2)]
        ps_a = stack.enter_context(nc.psum_tensor("ps_a", [P, 2, TOK], F32))
        ps_t = stack.enter_context(nc.psum_tensor("ps_t", [P, TOK], F32))
        ps_y = stack.enter_context(nc.psum_tensor("ps_y", [P, TOK], F32))
        ps_o = stack.enter_context(nc.psum_tensor("ps_o", [P, TOK], F32))
        ps_x = stack.enter_context(nc.psum_tensor("ps_x", [P, TOK], F32))

        x_in = [sem(f"x_in{b}") for b in range(BLK)]
        tabs_in = sem("tabs_in")
        wdt_in = sem("wdt_in")
        w_in_s = [sem(f"w_in{i}") for i in range(WRING)]
        wo_in_s = [sem(f"wo_in{i}") for i in range(2)]
        rows_out = sem("rows_out")
        rows_in = [sem(f"rows_in{i}") for i in range(2)]
        ctx_in = [sem(f"ctx_in{s}") for s in range(SEQS)]
        ffn_in = sem("ffn_in")
        stored = sem("stored")
        pool_pre = sem("pool_pre")
        vec_pre = sem("vec_pre")
        act_pre = sem("act_pre")
        pe_pre = sem("pe_pre")
        w_hi_made = sem("w_hi_made")
        w_lo_made = sem("w_lo_made")
        proj_made = sem("proj_made")
        tapped = sem("tapped")
        conved = sem("conved")
        conv_tanh = sem("conv_tanh")
        silu_made = sem("silu_made")
        gate_tanh = sem("gate_tanh")
        gate_made = sem("gate_made")
        conv_tab_set = sem("conv_tab_set")
        out_tab_set = sem("out_tab_set")
        head_tabs = sem("head_tabs")
        hid_turned = sem("hid_turned")
        acs_spread = sem("acs_spread")
        acs_masked = sem("acs_masked")
        e_made = sem("e_made")
        l_made = sem("l_made")
        hc_made = sem("hc_made")
        hcd_made = sem("hcd_made")
        m_made = sem("m_made")
        c_copied = sem("c_copied")
        cdec_made = sem("cdec_made")
        state_made = sem("state_made")
        prev_made = sem("prev_made")
        y_made = sem("y_made")
        y1_made = sem("y1_made")
        yg_made = sem("yg_made")
        ysq_made = sem("ysq_made")
        ysum_made = sem("ysum_made")
        y_hi_made = sem("y_hi_made")
        y_lo_made = sem("y_lo_made")
        b_turned = sem("b_turned")
        btok_made = sem("btok_made")
        cb_made = sem("cb_made")
        cb_kept = sem("cb_kept")
        wo_hi_made = sem("wo_hi_made")
        wo_lo_made = sem("wo_lo_made")
        ss_summed = sem("ss_summed")
        ss_kept = sem("ss_kept")
        rstd_made = sem("rstd_made")
        o_made = sem("o_made")
        o_kept = sem("o_kept")
        o_added = sem("o_added")
        vec_chain = sem("vec_chain")
        scales_set = sem("scales_set")
        lvl2_made = sem("lvl2_made")
        var_set = sem("var_set")
        rstd_set = sem("rstd_set")
        lvl1_made = sem("lvl1_made")
        lvl1_turned = sem("lvl1_turned")
        lvl1_kept = sem("lvl1_kept")
        col_summed = sem("col_summed")
        row_summed = sem("row_summed")
        rows_kept = sem("rows_kept")
        x_made = sem("x_made")
        n_made = sem("n_made")
        n_turned = sem("n_turned")
        n_kept = sem("n_kept")
        z_made = sem("z_made")
        z_kept = sem("z_kept")
        zm_made = sem("zm_made")
        zm_turned = sem("zm_turned")
        zmt_kept = sem("zmt_kept")
        f_made = sem("f_made")
        out_made = sem("out_made")

        def past(eng, s, count):
            if isinstance(count, int) and count < 1:
                return
            eng.wait_ge(s, count)

        def following(g, u, by):
            return (g + (u + by) // PAIRS, (u + by) % PAIRS)

        def exists(last, u, by):
            return not last or u + by < PAIRS

        def run_steps(eng, step):
            for u in range(HALF):
                step(0, u, False, True)
            with eng.Fori(0, GROUPS - 1) as g:
                for u in range(HALF, PAIRS):
                    step(g, u, False, False)
                for u in range(HALF):
                    step(g + 1, u, False, False)
            for u in range(HALF, PAIRS):
                step(GROUPS - 1, u, True, False)

        def hid_tile(u):
            return 2 + 2 * u

        def gate_tile(u):
            return 3 + 2 * u

        def conv_of(t):
            return t if t < 2 else 1 + t // 2

        def free_slot(g, u):
            return O_CREDIT + 2 * BLK * g - (BLK if u < HALF else 0)

        def turn_bank(k):
            return ps_t if k % 2 == 0 else ps_y

        def turn_bank_bf(k):
            return turn_bank(k)[:, 0:TOK // 2].bitcast(BF16)

        def bank_of(p, t):
            if isinstance(p, int) and p == 0 and t in (2, 3):
                return (ps_o, ps_x)[t - 2]
            return ps_p[t % 2]

        last_group = GROUPS - 1
        block = stack.enter_context(nc.Block())

        h_banks = [ps_t, ps_y, ps_o, ps_a[:, 0, :]]

        @block.sync
        def _(sp):
            def load_w(p, t):
                past(sp, w_lo_made, TILES * p + t - WRING + 1)
                sp.dma_start(w_raw[:, t % WRING, :],
                             w_in[bass.ds(TILES * p + t, 1)].rearrange("o p d -> p (o d)")
                             ).then_inc(w_in_s[t % WRING], 16)

            def load_wo(g, u):
                past(sp, wo_lo_made, CREDIT + PAIRS * g + u - 1)
                sp.dma_start(wo_raw[:, u % 2, :],
                             w_out[bass.ds(PAIRS * g + u, 1)].rearrange("o p d -> p (o d)")
                             ).then_inc(wo_in_s[u % 2], 16)

            def load_rows(g, u):
                past(sp, acs_spread, PAIRS * g + u - 1)
                for h in range(2):
                    sp.dma_start(rows[ROW * h:ROW * h + 2, u % 2, :].bitcast(F32),
                                 acs_rows[:, bass.ds(PAIRS * g + u, 1), h].rearrange("s o t -> s (o t)")
                                 ).then_inc(rows_in[u % 2], 16)

            for b in range(BLK):
                sp.dma_start(xt[:, b], x_blocks[:, b]).then_inc(x_in[b], 16)
            sp.dma_start(wdt_raw[:], w_in[TILES * GROUPS]).then_inc(wdt_in, 16)
            for dst, src in ((nw, nw_tab), (dtb, dtb_tab), (alog, alog_tab), (conv_all, conv_tab)):
                sp.dma_start(dst[:], src).then_inc(tabs_in, 16)
            for t in range(WRING):
                load_w(0, t)
            for dst, src in ((d_all, d_tab), (gn_all, gn_tab)):
                sp.dma_start(dst[:], src).then_inc(tabs_in, 16)
            sp.dma_start(cst[:], consts.to_broadcast([P, 8])).then_inc(tabs_in, 16)
            for t in range(WRING, 2 + 2 * LEAD + WRING):
                load_w(0, t)
            sp.wait_ge(vec_pre, V_ACS_SPLIT)
            for i, part in enumerate((acs_hi, acs_lo)):
                sp.dma_start(acs_rows[i].rearrange("q h t -> (q h) t"), part[:].bitcast(F32)
                             ).then_inc(rows_out, 16)
            sp.wait_ge(rows_out, 32)
            load_rows(0, 0)
            load_rows(0, 1)
            load_wo(0, 0)
            load_wo(0, 1)
            for t in range(2 + 2 * LEAD + WRING, 2 + 2 * LEAD + 5):
                load_w(0, t)

            def step(g, u, last, first):
                if exists(last, u, 2):
                    load_rows(*following(g, u, 2))
                if exists(last, u, LEAD):
                    load_w(*weights_ahead(g, u, 0))
                if exists(last, u, 2):
                    load_wo(*following(g, u, 2))
                if exists(last, u, LEAD):
                    load_w(*weights_ahead(g, u, 1))
                    if u == 5 and not last or u == 6:
                        load_w(*weights_ahead(g, u, 2))

            def weights_ahead(g, u, i):
                p, v = following(g, u, LEAD)
                t = hid_tile(v) + i - (1 if u == 6 else 0)
                return p, t + 5

            run_steps(sp, step)
            sp.wait_ge(proj_made, TILES * GROUPS)
            sp.wait_ge(w_lo_made, TILES * GROUPS + 2)
            for s_w in range(WRING):
                sp.wait_ge(w_in_s[s_w], 16 * ((TILES * GROUPS + 4 - s_w) // WRING + 1))
            for b in range(SEQS):
                sp.dma_start(ctx_raw[:, b], ctx_tiles[:, b]).then_inc(ctx_in[b], 16)
            sp.dma_start(wup[:], w_up).then_inc(ffn_in, 16)
            sp.dma_start(wz[:], w_z).then_inc(ffn_in, 16)
            sp.wait_ge(y_made, CREDIT + PAIRS * GROUPS)
            sp.dma_start(lb[:], lora_b).then_inc(ffn_in, 16)
            for b in range(BLK):
                sp.wait_ge(out_made, b + 1)
                sp.dma_start(out_blocks[:, b], acc[:, b, :]).then_inc(stored, 16)
            sp.wait_ge(stored, 16 * BLK)

        @block.gpsimd
        def _(pool):
            nc.gpsimd.memset(half_f[:], -0.5).then_inc(pool_pre, 1)
            for i, ap in enumerate((ident, ident_bf, mask_bf)):
                nc.gpsimd.memset(ap[:], 0.0).then_inc(pool_pre, 1)
            nc.gpsimd.memset(ones_f[:], 1.0).then_inc(pool_pre, 1)
            nc.gpsimd.memset(one_row[:], 1.0).then_inc(pool_pre, 1)
            pool.wait_ge(pool_pre, 6)
            for ap in (ident, ident_bf):
                nc.gpsimd.affine_select(out=ap[:], in_=ap[:], compare_op=ALU.not_equal, fill=1.0, base=0,
                                        pattern=[[-1, P]], channel_multiplier=1).then_inc(pool_pre, 1)
            nc.gpsimd.affine_select(out=mask_bf[:], in_=mask_bf[:], compare_op=ALU.is_ge, fill=MASKED,
                                    base=0, pattern=[[0, BLK], [1, P]],
                                    channel_multiplier=-1).then_inc(pool_pre, 1)
            pool.sem_inc(cdec_made, CREDIT)
            pool.sem_inc(y_lo_made, CREDIT)
            pool.wait_ge(vec_pre, V_VAR)
            nc.gpsimd.tensor_tensor(rstd_t[:], var_e[:], half_f[:], ALU.pow).then_inc(pool_pre, 1)
            pool.wait_ge(vec_pre, V_MS)
            nc.gpsimd.tensor_tensor(rms[:], ms_e[:], half_f[:], ALU.pow).then_inc(pool_pre, 1)
            for b in range(BLK):
                pool.wait_ge(act_pre, A_HS + b)
                nc.gpsimd.tensor_tensor(acc[:, b, :], acc[:, b, :], xt[:, b, :], ALU.add
                                        ).then_inc(pool_pre, 1)

            def c_decayed(g, u):
                if u == 0:
                    pool.wait_ge(c_copied, g + 1)
                pool.wait_ge(e_made, PAIRS * g + u + 1)
                pool.wait_ge(y_made, CREDIT + PAIRS * g + u - 1)
                for h in range(2):
                    ins = nc.gpsimd.tensor_tensor(c_dec[:, u % 2, h], eacs[:, u % 2, h], c_cur[:], ALU.mult)
                ins.then_inc(cdec_made, 1)

            def low_part(g, u):
                pool.wait_ge(y_hi_made, PAIRS * g + u + 1)
                pool.wait_ge(o_made, free_slot(g, u))
                nc.gpsimd.tensor_tensor(y_lo[:, u, :], yg[:, u % 2, :], y_hi[:, u, :].bitcast(F32),
                                        ALU.subtract).then_inc(y_lo_made, 1)

            def norm(g):
                pool.wait_ge(ss_kept, g + 1)
                pool.wait_ge(o_added, A_CREDIT + 2 * BLK * g)
                nc.gpsimd.tensor_tensor(rstd_g[:], ss_g[:], half_f[:], ALU.pow).then_inc(rstd_made, 1)

            c_decayed(0, 0)

            def step(g, u, last, first):
                if exists(last, u, 1):
                    c_decayed(*following(g, u, 1))
                low_part(g, u)
                if u == 0 and not first:
                    norm(g - 1)

            run_steps(pool, step)
            norm(last_group)
            for i in range(2 * SEQS):
                s = slice(2 * (i % SEQS), 2 * (i % SEQS) + 2)
                pool.wait_ge(var_set, i + 1)
                nc.gpsimd.tensor_tensor(rstd_t[:, s], var_e[:, s], half_f[:, 0:2],
                                        ALU.pow).then_inc(rstd_set, 1)


        @block.scalar
        def _(act):
            act.sem_inc(ysq_made, CREDIT)
            act.sem_inc(prev_made, CREDIT)
            act.wait_ge(wdt_in, 16)
            nc.scalar.activation(wdt_hi[:], wdt_raw[:], ACT.Copy).then_inc(act_pre, 1)

            def hi_part(p, t):
                act.wait_ge(w_in_s[t % WRING], 96 * p + 16 * (t // WRING + 1))
                past(act, proj_made, TILES * p + t - WRING + 1)
                nc.scalar.activation(w_hi[:, t % WRING, :], w_raw[:, t % WRING, :],
                                     ACT.Copy).then_inc(w_hi_made, 1)

            act.wait_ge(pool_pre, G_CONST + 2)
            for b in range(BLK):
                act.wait_ge(vec_pre, V_ACC + b)
                nc.scalar.activation(hs[:, b, :], acc[:, b, :], ACT.Copy, scale=rms[:, b:b + 1]
                                     ).then_inc(act_pre, 1)
            hi_part(0, 0)
            act.wait_ge(tabs_in, 16 * 7)
            for k in range(KT):
                act.wait_ge(pe_pre, k + 1)
                nc.scalar.activation(h_hi[:, k, :], h_banks[k][:], ACT.Copy,
                                     scale=nw[:, k:k + 1]).then_inc(act_pre, 1)
            hi_part(0, 1)
            hi_part(0, 2)
            nc.scalar.activation(neg_a[:], alog[:], ACT.Exp).then_inc(act_pre, 1)
            act.wait_ge(pe_pre, PE_DT)
            nc.scalar.activation(dt_abs[:], ps_x[:], ACT.Abs, bias=dtb[:, 0:1]).then_inc(act_pre, 1)
            act.wait_ge(act_pre, A_ABS)
            nc.scalar.activation(ex[:], dt_abs[:], ACT.Exp, scale=-1.0).then_inc(act_pre, 1)

            def tap(p, t):
                i = conv_of(t)
                act.wait_ge(proj_made, TILES * p + t + 1)
                past(act, silu_made, CONVS * p + i - 1)
                nc.scalar.activation(cacc[:, i % 2].rearrange("c b t -> c (b t)"), bank_of(p, t)[:],
                                     ACT.Identity, bias=conv_g[:, i, TAPS:TAPS + 1],
                                     scale=conv_g[:, i, TAPS - 1:TAPS]).then_inc(tapped, 1)

            def tanh_conv(p, t):
                i = conv_of(t)
                act.wait_ge(conved, 3 * (CONVS * p + i) + 3)
                nc.scalar.activation(th[:, i % 2, :], cacc[:, i % 2].rearrange("c b t -> c (b t)"),
                                     ACT.Tanh).then_inc(conv_tanh, 1)

            def tanh_gate(p, u):
                act.wait_ge(proj_made, TILES * p + gate_tile(u) + 1)
                past(act, gate_made, PAIRS * p + u)
                nc.scalar.activation(thg[:], bank_of(p, gate_tile(u))[:], ACT.Tanh, scale=0.5).then_inc(gate_tanh, 1)

            def exp_rows(g, u):
                act.wait_ge(acs_spread, PAIRS * g + u + 1)
                act.wait_ge(cdec_made, CREDIT + PAIRS * g + u - 1)
                nc.scalar.activation(
                    eacs[:, u % 2], ps_a[:].rearrange("n h (b c i) -> n h b c i", b=SEQS, c=2)[:, :, :, 1, :],
                    ACT.Exp).then_inc(e_made, 1)

            def exp_decay(g, u):
                if u == 0:
                    act.wait_ge(head_tabs, g + 1)
                act.wait_ge(acs_masked, PAIRS * g + u + 1)
                act.wait_ge(y_made, CREDIT + PAIRS * g + u - 1)
                for h in range(2):
                    for b in range(BLK):
                        ins = nc.scalar.activation(
                            decay[:, u % 2, h, b * P:(b + 1) * P], ps_a[:, h, b * P:(b + 1) * P], ACT.Exp,
                            bias=nacs_g[:, b, 2 * u + h:2 * u + h + 1])
                ins.then_inc(l_made, 1)

            def keep_state(g, u):
                act.wait_ge(state_made, CREDIT + PAIRS * g + u + 1)
                act.wait_ge(y_made, CREDIT + PAIRS * g + u - 1)
                nc.scalar.copy(prev[:, u % 2], ps_x[:, 0:2 * P].rearrange("n (b c) -> n b c", b=SEQS)
                               ).then_inc(prev_made, 1)

            def high_and_square(g, u):
                act.wait_ge(yg_made, PAIRS * g + u + 1)
                act.wait_ge(o_made, free_slot(g, u))
                nc.scalar.activation(y_hi[:, u, :], yg[:, u % 2, :], ACT.Copy).then_inc(y_hi_made, 1)
                act.wait_ge(ysum_made, CREDIT + PAIRS * g + u - 1)
                nc.scalar.activation(ysq[:, u % 2, :], yg[:, u % 2, :], ACT.Square).then_inc(ysq_made, 1)

            def hi_part_out(g, u):
                if u == 0:
                    act.wait_ge(out_tab_set, g + 1)
                act.wait_ge(wo_in_s[u % 2], 64 * g + 16 * (u // 2 + 1))
                act.wait_ge(o_made, free_slot(g, u))
                nc.scalar.activation(wo_hi[:, u, :], wo_raw[:, u % 2, :], ACT.Copy,
                                     scale=gn_g[:, u:u + 1]).then_inc(wo_hi_made, 1)

            def keep_bc(g):
                act.wait_ge(b_turned, g + 1)
                past(act, state_made, CREDIT + PAIRS * g)
                nc.scalar.copy(b_tok[:], ps_t[:, 0:2 * P].rearrange("n (b c) -> n b c", b=SEQS)
                               ).then_inc(btok_made, 1)
                act.wait_ge(silu_made, CONVS * g + 2)
                act.wait_ge(cdec_made, CREDIT + PAIRS * g)
                nc.scalar.copy(c_cur[:], c_t[:].rearrange("n (b c i) -> n b c i", b=SEQS, c=2)[:, :, 1, :]
                               ).then_inc(c_copied, 1)

            def keep_half(g, b):
                act.wait_ge(o_made, O_CREDIT + 2 * BLK * g + b + 1)
                nc.scalar.copy(o_part[:, b, :], ps_o[:]).then_inc(o_kept, 1)

            act.wait_ge(conv_tab_set, 1)
            for t in (0, 1):
                hi_part(0, t + WRING)
                tap(0, t)
            hi_part(0, 5)
            tanh_gate(0, 0)
            act.wait_ge(vec_pre, V_ACS)
            for b in range(SEQS):
                nc.scalar.activation(dtd_h[:, b, :], acs_h[:, 2 * b * P:(2 * b + 1) * P], ACT.Exp,
                                     scale=-1.0, bias=acs_h[:, (2 * b + 1) * P - 1:(2 * b + 1) * P]
                                     ).then_inc(act_pre, 1)
            act.wait_ge(pe_pre, PE_ACS_T)
            nc.scalar.activation(nacs_all[:].rearrange("t b h -> t (b h)"), ps_y[:], ACT.Copy,
                                 scale=-1.0).then_inc(act_pre, 1)
            tanh_conv(0, 0)
            tanh_conv(0, 1)
            tap(0, 2)
            exp_rows(0, 0)
            hi_part(0, 6)
            tanh_conv(0, 2)
            keep_bc(0)
            tap(0, 4)
            exp_decay(0, 0)
            hi_part(0, 7)
            tanh_conv(0, 4)
            keep_state(0, 0)
            tanh_gate(0, 1)

            def step(g, u, last, first):
                near = exists(last, u, 1)
                ahead = exists(last, u, LEAD)
                p, v = following(g, u, LEAD)
                nxt = following(g, u, 1)
                if near:
                    exp_rows(*nxt)
                hi_part_out(g, u)
                if ahead:
                    hi_part(p, hid_tile(v) + 2 if u != 6 else 3)
                if u == 6 and not last:
                    tanh_conv(g + 1, 0)
                if near:
                    exp_decay(*nxt)
                if u == 7 and near:
                    keep_bc(nxt[0])
                high_and_square(g, u)
                if u == 6 and ahead:
                    tap(p, 1)
                    hi_part(p, 4)
                if ahead:
                    tap(p, hid_tile(v))
                if u == 6 and ahead:
                    tanh_conv(p, 1)
                if ahead:
                    hi_part(p, hid_tile(v) + 3)
                    tanh_conv(p, hid_tile(v))
                if u >= HALF:
                    keep_half(g, u - HALF)
                if near:
                    keep_state(*nxt)
                if ahead:
                    tanh_gate(p, v)
                if u == 5 and not last:
                    hi_part(g + 1, 2)
                    act.wait_ge(conv_tab_set, g + 2)
                    tap(g + 1, 0)

            run_steps(act, step)

            for s in range(SEQS):
                for k in range(KT):
                    act.wait_ge(lvl1_turned, KT * s + k + 1)
                    nc.scalar.copy(lvl1_t[:, k, 2 * s * P:2 * (s + 1) * P],
                                   turn_bank_bf(k)[:, 0:2 * P]).then_inc(lvl1_kept, 1)
            for s in range(SEQS):
                for k in range(KT):
                    act.wait_ge(n_turned, KT * s + k + 1)
                    nc.scalar.copy(n_tt[:, k, 2 * s * P:2 * (s + 1) * P],
                                   turn_bank(k)[:, 0:2 * P]).then_inc(n_kept, 1)

        @block.tensor
        def _(pe):
            pe.sem_inc(y_made, CREDIT)
            pe.sem_inc(state_made, CREDIT)
            pe.sem_inc(o_made, O_CREDIT)
            pe.sem_inc(ss_summed, 1)

            def three(bank, stat_hi, stat_lo, mov_hi, mov_lo, first, last):
                nc.tensor.matmul(bank, stat_hi, mov_hi, start=first, stop=False)
                nc.tensor.matmul(bank, stat_lo, mov_hi, start=False, stop=False)
                return nc.tensor.matmul(bank, stat_hi, mov_lo, start=False, stop=last)

            pe.wait_ge(pool_pre, G_CONST)
            for k in range(KT):
                for b in range(BLK):
                    if k == 0:
                        pe.wait_ge(act_pre, A_HS + b)
                    ins = nc.tensor.transpose(h_banks[k][:, b * P:(b + 1) * P],
                                              hs[:, b, k * P:(k + 1) * P], ident[:])
                ins.then_inc(pe_pre, 1)
            pe.wait_ge(vec_pre, V_WDT)
            for k in range(KT):
                pe.wait_ge(vec_pre, V_HLO + k)
                ins = three(ps_x[:], wdt_hi[:, k * P:(k + 1) * P], wdt_lo[:, k * P:(k + 1) * P],
                            h_hi[:, k, :], h_lo[:, k, :], k == 0, k == KT - 1)
            ins.then_inc(pe_pre, 1)

            def project(p, t):
                pe.wait_ge(w_lo_made, TILES * p + t + 1)
                if isinstance(p, int) and p == 0 and t < 6:
                    if t == 3:
                        pe.wait_ge(vec_pre, V_DTX)
                    elif t > 3:
                        pe.wait_ge(conved, 3 * (t - 3))
                elif t == 0:
                    past(pe, conved, 3 * CONVS * p)
                elif t == 1:
                    past(pe, gate_made, PAIRS * p)
                elif t == 2:
                    past(pe, conved, 3 * (CONVS * p + 1))
                elif t == 3:
                    past(pe, conved, 3 * (CONVS * p + 2))
                elif t % 2 == 0:
                    pe.wait_ge(conved, 3 * (CONVS * p + conv_of(t)))
                else:
                    pe.wait_ge(gate_made, PAIRS * p + t // 2 - 1)
                s = t % WRING
                for k in range(KT):
                    w = slice(k * P, (k + 1) * P)
                    ins = three(bank_of(p, t)[:], w_hi[:, s, w], w_lo[:, s, w], h_hi[:, k, :], h_lo[:, k, :],
                                k == 0, k == KT - 1)
                ins.then_inc(proj_made, 1)

            def turn_hid(g, u):
                past(pe, hcd_made, PAIRS * g + u)
                if u == 0:
                    pe.wait_ge(btok_made, g + 1)
                pe.wait_ge(silu_made, CONVS * g + 2 + u + 1)
                for b in range(BLK):
                    ins = nc.tensor.transpose(ps_t[:, b * P:(b + 1) * P],
                                              hid[:, u % RING, b * P:(b + 1) * P], ident[:])
                ins.then_inc(hid_turned, 1)

            def spread(g, u):
                pe.wait_ge(rows_in[u % 2], 32 * HALF * g + 32 * (u // 2 + 1))
                past(pe, l_made, PAIRS * g + u)
                for h in range(2):
                    r = slice(ROW * h, ROW * h + 2)
                    ins = nc.tensor.matmul(ps_a[:, h, :], ones_r[r, :], rows[r, u % 2, :], start=True, stop=True)
                ins.then_inc(acs_spread, 1)

            def add_mask(g, u):
                pe.wait_ge(e_made, PAIRS * g + u + 1)
                for h in range(2):
                    ins = nc.tensor.matmul(ps_a[:, h, :], ident_bf[:],
                                           mask_bf[:].rearrange("j b i -> j (b i)"),
                                           start=False, stop=True, skip_group_check=True)
                ins.then_inc(acs_masked, 1)

            def states(g, u):
                pe.wait_ge(hcd_made, PAIRS * g + u + 1)
                if u == 0:
                    pe.wait_ge(cb_kept, g + 1)
                    pe.wait_ge(btok_made, g + 1)
                else:
                    pe.wait_ge(prev_made, CREDIT + PAIRS * g + u)
                if u == 1:
                    past(pe, ss_kept, g)
                for b in range(SEQS):
                    ins = nc.tensor.matmul(ps_x[:, b * P:(b + 1) * P], b_tok[:, b, :],
                                           hcd[:, u % 2, b, :], start=True, stop=True)
                ins.then_inc(state_made, 1)

            def scan(g, u):
                pe.wait_ge(m_made, PAIRS * g + u + 1)
                pe.wait_ge(hc_made, PAIRS * g + u + 1)
                pe.wait_ge(prev_made, CREDIT + PAIRS * g + u + 1)
                pe.wait_ge(cdec_made, CREDIT + PAIRS * g + u + 1)
                past(pe, y1_made, PAIRS * g + u)
                r = u % 2
                for b in range(BLK):
                    for h in range(2):
                        ch = slice(h * HD, (h + 1) * HD)
                        dst = ps_y[ch, b * P:(b + 1) * P]
                        ins = nc.tensor.matmul(dst, hc[:, r, b, ch], decay[:, r, h, b * P:(b + 1) * P],
                                               start=True, stop=(b % 2 == 0))
                    if b % 2 == 1:
                        for h in range(2):
                            ch = slice(h * HD, (h + 1) * HD)
                            dst = ps_y[ch, b * P:(b + 1) * P]
                            ins = nc.tensor.matmul(dst, prev[:, r, b // 2, ch], c_dec[:, r, h, b // 2, :],
                                                   start=False, stop=True)
                ins.then_inc(y_made, 1)

            def group_products(g):
                pe.wait_ge(silu_made, CONVS * g + 2)
                past(pe, hcd_made, PAIRS * g)
                for b in range(SEQS):
                    ins = nc.tensor.transpose(ps_t[:, b * P:(b + 1) * P],
                                              b_t[:, 2 * b * P:(2 * b + 1) * P], ident[:])
                ins.then_inc(b_turned, 1)
                past(pe, prev_made, CREDIT + PAIRS * g)
                for b in range(BLK):
                    ins = nc.tensor.matmul(ps_x[:, b * P:(b + 1) * P], b_t[:, b * P:(b + 1) * P],
                                           c_t[:, b * P:(b + 1) * P], start=True, stop=True)
                ins.then_inc(cb_made, 1)

            def sum_squares(g):
                pe.wait_ge(ysum_made, CREDIT + PAIRS * g + PAIRS)
                if not (isinstance(g, int) and g == last_group):
                    pe.wait_ge(prev_made, CREDIT + PAIRS * g + PAIRS + 1)
                for b in range(BLK):
                    ins = nc.tensor.matmul(ps_x[:, b:b + 1], ysum[:, b * P:(b + 1) * P], ones_f[:, 0:1],
                                           start=True, stop=True)
                ins.then_inc(ss_summed, 1)

            def out_half(g, half, b):
                if b == 0:
                    pe.wait_ge(y_lo_made, CREDIT + PAIRS * g + HALF * (half + 1))
                    pe.wait_ge(wo_lo_made, CREDIT + PAIRS * g + HALF * (half + 1))
                if half == 0 and b == 0:
                    pe.wait_ge(o_added, A_CREDIT + 2 * BLK * g)
                elif half == 0 or b == 0:
                    pe.wait_ge(o_kept, BLK * g + (b if half == 0 else BLK))
                else:
                    pe.wait_ge(o_added, A_CREDIT + 2 * BLK * g + 2 * b - 1)
                t = slice(b * P, (b + 1) * P)
                for u in range(HALF * half, HALF * (half + 1)):
                    ins = three(ps_o[:], y_hi[:, u, t], y_lo[:, u, t], wo_hi[:, u, :], wo_lo[:, u, :],
                                u % HALF == 0, u % HALF == HALF - 1)
                ins.then_inc(o_made, 1)

            for t in range(4):
                project(0, t)
            pe.wait_ge(vec_pre, V_ACS)
            for b in range(BLK):
                ins = nc.tensor.transpose(ps_y[:, b * P:(b + 1) * P], acs_h[:, b * P:(b + 1) * P], ident[:])
            ins.then_inc(pe_pre, 1)
            for b in range(BLK):
                ins = nc.tensor.transpose(ps_t[:, b * P:(b + 1) * P], dt_h[:, b * P:(b + 1) * P], ident[:])
            ins.then_inc(pe_pre, 1)
            project(0, 4)
            spread(0, 0)
            pe.wait_ge(vec_pre, V_DTD)
            pe.wait_ge(gate_made, 1)
            for b in range(SEQS):
                ins = nc.tensor.transpose(ps_x[:, b * P:(b + 1) * P], dtd_h[:, b, :], ident[:])
            ins.then_inc(pe_pre, 1)
            pe.wait_ge(vec_pre, V_TOK)
            pe.wait_ge(act_pre, A_NACS)
            group_products(0)
            add_mask(0, 0)
            turn_hid(0, 0)
            project(0, 5)
            states(0, 0)

            def step(g, u, last, first):
                near = exists(last, u, 1)
                ahead = exists(last, u, LEAD)
                p, v = following(g, u, LEAD)
                nxt = following(g, u, 1)
                if near:
                    spread(*nxt)
                scan(g, u)
                if near:
                    add_mask(*nxt)
                if u == 0 and not first:
                    sum_squares(g - 1)
                if u == 7 and near:
                    group_products(nxt[0])
                elif near:
                    turn_hid(*nxt)
                if u == 6 and ahead:
                    project(p, 1)
                if ahead:
                    project(p, hid_tile(v))
                if u == 7 and near:
                    turn_hid(*nxt)
                if u >= HALF:
                    out_half(g, 0, u - HALF)
                elif not first:
                    out_half(g - 1, 1, u)
                if near:
                    states(*nxt)
                if ahead:
                    project(p, gate_tile(v))
                if u == 5 and not last:
                    project(g + 1, 0)

            run_steps(pe, step)
            for s in range(SEQS):
                pe.wait_ge(lvl2_made, s + 1)
                for k in range(KT):
                    ins = nc.tensor.matmul(ps_p[s][:], ones_bf[:], lvl2[:, s, k, :], start=(k == 0),
                                           stop=(k == KT - 1))
                ins.then_inc(col_summed, 1)
            sum_squares(last_group)
            for b in range(BLK):
                out_half(last_group, 1, b)

            for s in range(SEQS):
                for k in range(KT):
                    past(pe, lvl1_kept, KT * s + k - 1)
                    for b in (2 * s, 2 * s + 1):
                        if k == 0:
                            pe.wait_ge(lvl1_made, b + 1)
                        ins = nc.tensor.transpose(turn_bank_bf(k)[:, b % 2 * P:(b % 2 + 1) * P],
                                                  lvl1[:, b, k * P:(k + 1) * P], ident_bf[:])
                    ins.then_inc(lvl1_turned, 1)
            x_banks = [ps_o, ps_a[:, 0, :], ps_a[:, 1, :], ps_p[0]]
            for s in range(SEQS):
                pe.wait_ge(lvl1_kept, KT * (s + 1))
                if s == 0:
                    pe.wait_ge(o_added, A_CREDIT + 2 * BLK * GROUPS)
                for b in (2 * s, 2 * s + 1):
                    for k in range(KT):
                        ins = nc.tensor.matmul(ps_x[:, b:b + 1], lvl1_t[:, k, b * P:(b + 1) * P],
                                               ones_bf[:, 0:1], start=(k == 0), stop=(k == KT - 1))
                ins.then_inc(row_summed, 1)
                for b in (2 * s, 2 * s + 1):
                    if b == 3:
                        pe.wait_ge(vec_chain, C_COL)
                    for k in range(KT):
                        ins = nc.tensor.matmul(x_banks[b][:], lvl1_t[:, k, b * P:(b + 1) * P],
                                               lvl2[:, s, k, :], start=(k == 0), stop=(k == KT - 1))
                    ins.then_inc(x_made, 1)
                if s == 0:
                    pe.wait_ge(rows_kept, 1)
            nz = LORA + EXPERTS
            f_banks = [ps_o, ps_a[:, 0, :], ps_a[:, 1, :], ps_p[0]]
            for s in range(SEQS):
                blocks = (2 * s, 2 * s + 1)
                for k in range(KT):
                    past(pe, n_kept, KT * s + k - 1)
                    for b in blocks:
                        if k == 0:
                            pe.wait_ge(n_made, b + 1)
                        ins = nc.tensor.transpose(turn_bank(k)[:, b % 2 * P:(b % 2 + 1) * P],
                                                  n_t[:, b, k * P:(k + 1) * P], ident[:])
                    ins.then_inc(n_turned, 1)
                if s == 0:
                    pe.wait_ge(ffn_in, 48)
                    pe.wait_ge(rows_kept, 2)
                else:
                    pe.wait_ge(z_kept, 1)
                pe.wait_ge(n_kept, KT * (s + 1))
                for b in blocks:
                    for k in range(KT):
                        ins = nc.tensor.matmul(ps_x[:, b * nz:(b + 1) * nz], n_tt[:, k, b * P:(b + 1) * P],
                                               wz[:, k, :], start=(k == 0), stop=(k == KT - 1))
                ins.then_inc(z_made, 1)
                for b in blocks:
                    for k in range(KT):
                        nc.tensor.matmul(f_banks[b][:], n_tt[:, k, b * P:(b + 1) * P], wup[:, k, :],
                                         start=(k == 0), stop=False)
            for s in range(SEQS):
                blocks = (2 * s, 2 * s + 1)
                pe.wait_ge(zm_made, s + 1)
                for b in blocks:
                    ins = nc.tensor.transpose(ps_p[1][0:LORA, b * P:(b + 1) * P], zm[:, b, :], ident[:])
                ins.then_inc(zm_turned, 1)
                pe.wait_ge(zmt_kept, s + 1)
                for b in blocks:
                    nc.tensor.matmul(f_banks[b][:], zm_t[:, b, :], lb[:], start=False,
                                     stop=True).then_inc(f_made, 1)

        @block.vector
        def _(dve):
            pre = [0]

            def mark(ins):
                ins.then_inc(vec_pre, 1)
                pre[0] += 1
                return pre[0]

            dve.sem_inc(wo_lo_made, CREDIT)
            dve.sem_inc(ysum_made, CREDIT)
            dve.sem_inc(o_added, A_CREDIT)

            for b in range(BLK):
                dve.wait_ge(x_in[b], 16)
                mark(nc.vector.bn_stats(stats[:, b, :], xt[:, b, :]))
            for b in range(BLK):
                dve.wait_ge(vec_pre, b + 1)
                mark(nc.vector.bn_aggr(mv[:, b, :], stats[:, b, :]))
            dve.wait_ge(vec_pre, pre[0])
            n = mark(nc.vector.tensor_scalar_add(var_e[:], mv[:, :, 1], EPS))
            assert n == V_VAR
            dve.wait_ge(pool_pre, G_CONST + 1)
            mark(nc.vector.tensor_tensor(both[:], rstd_t[:], rstd_t[:], ALU.mult))
            dve.wait_ge(vec_pre, pre[0])
            mark(nc.vector.tensor_tensor(both[:], both[:], mv[:, :, 1], ALU.mult))
            dve.wait_ge(vec_pre, pre[0])
            n = mark(nc.vector.tensor_scalar_add(ms_e[:], both[:], EPS))
            assert n == V_MS
            for b in range(BLK):
                n = mark(nc.vector.tensor_scalar(acc[:, b, :], xt[:, b, :], mv[:, b, 0:1],
                                                 rstd_t[:, b:b + 1], ALU.subtract, ALU.mult))
                assert n == V_ACC + b
            dve.wait_ge(act_pre, A_WDT)
            n = mark(nc.vector.tensor_tensor(wdt_lo[:], wdt_raw[:], wdt_hi[:].bitcast(F32), ALU.subtract))
            assert n == V_WDT
            mark(nc.vector.tensor_copy(ones_r[:], one_row[0:ROW + 2, :]))
            dve.wait_ge(tabs_in, 16 * 7)
            mark(nc.vector.tensor_scalar_mul(conv_all[:], conv_all[:], 0.5))
            dve.wait_ge(vec_pre, pre[0])

            def conv_table(p):
                past(dve, conved, 3 * CONVS * p)
                nc.vector.tensor_copy(conv_g[:], conv_all[:, bass.ds(p, 1)].rearrange(
                    "c o u k -> c (o u) k")).then_inc(conv_tab_set, 1)
                dve.wait_ge(conv_tab_set, p + 1)

            conv_table(0)

            def lo_part(p, t):
                dve.wait_ge(w_hi_made, TILES * p + t + 1)
                s = t % WRING
                nc.vector.tensor_tensor(w_lo[:, s, :], w_raw[:, s, :], w_hi[:, s, :].bitcast(F32),
                                        ALU.subtract).then_inc(w_lo_made, 1)

            for k in range(KT):
                dve.wait_ge(act_pre, A_HHI + k)
                n = mark(nc.vector.scalar_tensor_tensor(
                    out=h_lo[:, k, :], in0=h_banks[k][:], scalar=nw[:, k:k + 1],
                    in1=h_hi[:, k, :].bitcast(F32), op0=ALU.mult, op1=ALU.subtract))
                assert n == V_HLO + k
            for t in range(WRING):
                lo_part(0, t)
            dve.wait_ge(act_pre, A_NEG)
            mark(nc.vector.tensor_scalar_mul(neg_a[:], neg_a[:], -1.0))

            def conv(p, t):
                i = conv_of(t)
                c = CONVS * p + i
                dve.wait_ge(tapped, c + 1)
                src = bank_of(p, t)[:].rearrange("c (b t) -> c b t", b=SEQS)
                for j in range(1, TAPS):
                    if j > 1:
                        dve.wait_ge(conved, 3 * c + j - 1)
                    dst = cacc[:, i % 2, :, j:SEQ]
                    nc.vector.scalar_tensor_tensor(
                        out=dst, in0=src[:, :, 0:SEQ - j], scalar=conv_g[:, i, TAPS - 1 - j:TAPS - j],
                        in1=dst, op0=ALU.mult, op1=ALU.add).then_inc(conved, 1)

            def silu(p, t):
                i = conv_of(t)
                dve.wait_ge(conv_tanh, CONVS * p + i + 1)
                dst = hid[:, (i - 2) % RING, :] if i >= 2 else (b_t, c_t)[i][:]
                if i == 1:
                    past(dve, c_copied, p)
                nc.vector.scalar_tensor_tensor(
                    out=dst, in0=th[:, i % 2, :], scalar=1.0, in1=cacc[:, i % 2].rearrange("c b t -> c (b t)"),
                    op0=ALU.add, op1=ALU.mult).then_inc(silu_made, 1)

            def silu_gate(p, u):
                dve.wait_ge(gate_tanh, PAIRS * p + u + 1)
                nc.vector.scalar_tensor_tensor(out=gate[:, u % RING, :], in0=thg[:], scalar=1.0,
                                               in1=bank_of(p, gate_tile(u))[:], op0=ALU.add,
                                               op1=ALU.mult).then_inc(gate_made, 1)

            def tokens_hid(g, u):
                dve.wait_ge(hid_turned, PAIRS * g + u + 1)
                dve.wait_ge(y_made, CREDIT + PAIRS * g + u - 1)
                src = ps_t[:].rearrange("t (b h c) -> t b h c", b=BLK, h=2)
                heads = slice(2 * u, 2 * u + 2)
                nc.vector.tensor_tensor(
                    hc[:, u % 2].rearrange("t b (h c) -> t b h c", h=2), src,
                    dt_g[:, :, heads].unsqueeze(3).to_broadcast([P, BLK, 2, HD]), ALU.mult
                ).then_inc(hc_made, 1)
                dve.wait_ge(state_made, CREDIT + PAIRS * g + u - 1)
                nc.vector.tensor_tensor(
                    hcd[:, u % 2].rearrange("t b (h c) -> t b h c", h=2), src[:, 0:BLK:2],
                    dtd_g[:, :, heads].unsqueeze(3).to_broadcast([P, SEQS, 2, HD]), ALU.mult
                ).then_inc(hcd_made, 1)

            def mix(g, u):
                dve.wait_ge(l_made, PAIRS * g + u + 1)
                if u == 0:
                    dve.wait_ge(cb_kept, g + 1)
                m = decay[:, u % 2]
                nc.vector.tensor_tensor(m, m, cb[:].rearrange("j b i -> j (b i)").unsqueeze(1).to_broadcast(
                    [P, 2, TOK]), ALU.mult).then_inc(m_made, 1)

            def gated(g, u):
                dve.wait_ge(y_made, CREDIT + PAIRS * g + u + 1)
                nc.vector.scalar_tensor_tensor(out=y1[:], in0=hid[:, u % RING, :], scalar=d_g[:, u:u + 1],
                                               in1=ps_y[:], op0=ALU.mult, op1=ALU.add).then_inc(y1_made, 1)
                dve.wait_ge(y1_made, PAIRS * g + u + 1)
                dve.wait_ge(ysq_made, CREDIT + PAIRS * g + u - 1)
                dve.wait_ge(y_lo_made, CREDIT + PAIRS * g + u - 1)
                nc.vector.tensor_tensor(yg[:, u % 2, :], y1[:], gate[:, u % RING, :],
                                        ALU.mult).then_inc(yg_made, 1)

            def add_squares(g, u):
                dve.wait_ge(ysq_made, CREDIT + PAIRS * g + u + 1)
                if u == 0:
                    dve.wait_ge(ss_summed, g + 1)
                    ins = nc.vector.tensor_copy(ysum[:], ysq[:, 0, :])
                else:
                    dve.wait_ge(ysum_made, CREDIT + PAIRS * g + u)
                    ins = nc.vector.tensor_tensor(ysum[:], ysum[:], ysq[:, u % 2, :], ALU.add)
                ins.then_inc(ysum_made, 1)

            def lo_part_out(g, u):
                dve.wait_ge(wo_hi_made, PAIRS * g + u + 1)
                nc.vector.scalar_tensor_tensor(
                    out=wo_lo[:, u, :], in0=wo_raw[:, u % 2, :], scalar=gn_g[:, u:u + 1],
                    in1=wo_hi[:, u, :].bitcast(F32), op0=ALU.mult, op1=ALU.subtract
                ).then_inc(wo_lo_made, 1)

            def keep_squares(g):
                dve.wait_ge(ss_summed, g + 2)
                nc.vector.tensor_scalar(ss_g[:], ps_x[:, 0:BLK], 1.0 / (PAIRS * P), 4 * EPS, ALU.mult,
                                        ALU.add).then_inc(ss_kept, 1)

            def add_out(g, b):
                if b == 0:
                    dve.wait_ge(rstd_made, g + 1)
                dve.wait_ge(o_made, O_CREDIT + 2 * BLK * g + BLK + b + 1)
                nc.vector.tensor_tensor(o_part[:, b, :], ps_o[:], o_part[:, b, :], ALU.add
                                        ).then_inc(o_added, 1)
                dve.wait_ge(o_added, A_CREDIT + 2 * BLK * g + 2 * b + 1)
                nc.vector.scalar_tensor_tensor(
                    out=acc[:, b, :], in0=o_part[:, b, :], scalar=rstd_g[:, b:b + 1],
                    in1=acc[:, b, :], op0=ALU.mult, op1=ALU.add).then_inc(o_added, 1)

            def keep_cb(g):
                dve.wait_ge(cb_made, g + 1)
                nc.vector.tensor_copy(cb[:].rearrange("j b i -> j (b i)"), ps_x[:]).then_inc(cb_kept, 1)

            def head_tables(g):
                h = bass.ds(HEADS * g, HEADS)
                nc.vector.tensor_copy(nacs_g[:], nacs_all[:, :, h])
                nc.vector.tensor_copy(dt_g[:], dt_all[:, :, h])
                nc.vector.tensor_copy(dtd_g[:], dtd_all[:, :, h]).then_inc(head_tabs, 1)
                dve.wait_ge(head_tabs, g + 1)

            def out_tables(g):
                past(dve, y1_made, PAIRS * g)
                dve.wait_ge(wo_lo_made, CREDIT + PAIRS * g)
                nc.vector.tensor_copy(d_g[:], d_all[:, bass.ds(g, 1)].rearrange("c o u -> c (o u)"))
                nc.vector.tensor_copy(gn_g[:], gn_all[:, bass.ds(g, 1)].rearrange("c o u -> c (o u)")
                                      ).then_inc(out_tab_set, 1)
                dve.wait_ge(out_tab_set, g + 1)

            dve.wait_ge(act_pre, A_ABS)
            n = mark(nc.vector.tensor_scalar(dtx[:], ps_x[:], dtb[:, 0:1], 0.0, ALU.add, ALU.max))
            assert n == V_DTX
            dve.wait_ge(act_pre, A_EX)
            mark(nc.vector.tensor_scalar_add(poly[:], ex[:], 2.0))
            dve.wait_ge(vec_pre, pre[0])
            mark(nc.vector.reciprocal(zz[:, 1, :], poly[:]))
            lo_part(0, 3)
            dve.wait_ge(vec_pre, pre[0])
            mark(nc.vector.tensor_tensor(zz[:, 0, :], ex[:], zz[:, 1, :], ALU.mult))
            dve.wait_ge(vec_pre, pre[0])
            mark(nc.vector.tensor_tensor(zz[:, 1, :], zz[:, 0, :], zz[:, 0, :], ALU.mult))
            dve.wait_ge(vec_pre, pre[0])
            mark(nc.vector.tensor_scalar_mul(poly[:], zz[:, 1, :], 1.0 / 13))
            lo_part(0, 4)
            for c in (11, 9, 7, 5, 3):
                dve.wait_ge(vec_pre, pre[0])
                mark(nc.vector.scalar_tensor_tensor(out=poly[:], in0=poly[:], scalar=1.0 / c,
                                                    in1=zz[:, 1, :], op0=ALU.add, op1=ALU.mult))
            lo_part(0, 5)
            dve.wait_ge(vec_pre, pre[0])
            mark(nc.vector.scalar_tensor_tensor(out=poly[:], in0=poly[:], scalar=1.0, in1=zz[:, 0, :],
                                                op0=ALU.add, op1=ALU.mult))
            silu_gate(0, 0)
            dve.wait_ge(vec_pre, pre[0])
            mark(nc.vector.scalar_tensor_tensor(out=dt_h[:], in0=poly[:], scalar=2.0, in1=dtx[:],
                                                op0=ALU.mult, op1=ALU.add))
            dve.wait_ge(vec_pre, pre[0])
            mark(nc.vector.tensor_scalar(ac_h[:], dt_h[:], neg_a[:, 0:1], None, ALU.mult))
            dve.wait_ge(vec_pre, pre[0])
            for b in range(BLK):
                t = slice(b * P, (b + 1) * P)
                n = mark(nc.vector.tensor_tensor_scan(acs_h[:, t], one_row[:], ac_h[:, t], 0.0,
                                                      ALU.mult, ALU.add))
            assert n == V_ACS, n
            dve.wait_ge(vec_pre, pre[0])
            mark(nc.vector.tensor_copy(acs_hi[:], acs_h[:]))
            dve.wait_ge(vec_pre, pre[0])
            n = mark(nc.vector.tensor_tensor(acs_lo[:], acs_h[:], acs_hi[:].bitcast(F32), ALU.subtract))
            assert n == V_ACS_SPLIT, n

            conv(0, 0)
            conv(0, 1)
            silu(0, 0)
            dve.wait_ge(pe_pre, PE_DT_T)
            mark(nc.vector.tensor_copy(dt_all[:].rearrange("t b h -> t (b h)"), ps_t[:]))
            silu(0, 1)
            dve.wait_ge(act_pre, A_DTD)
            n = mark(nc.vector.tensor_tensor(
                dtd_h[:], dtd_h[:], dt_h[:].rearrange("h (b c t) -> h b c t", b=SEQS, c=2)[:, :, 0, :],
                ALU.mult))
            assert n == V_DTD, n
            conv(0, 2)
            dve.wait_ge(pe_pre, PE_DTD_T)
            n = mark(nc.vector.tensor_copy(dtd_all[:].rearrange("t b h -> t (b h)"), ps_x[:, 0:2 * P]))
            assert n == V_TOK, n
            dve.wait_ge(act_pre, A_NACS)
            dve.wait_ge(vec_pre, V_TOK)
            head_tables(0)
            silu(0, 2)
            keep_cb(0)
            lo_part(0, 6)
            tokens_hid(0, 0)
            mix(0, 0)
            conv(0, 4)
            lo_part(0, 7)
            dve.wait_ge(pool_pre, G_RES)

            def step(g, u, last, first):
                near = exists(last, u, 1)
                ahead = exists(last, u, LEAD)
                p, v = following(g, u, LEAD)
                nxt = following(g, u, 1)
                if u == 7 and near:
                    head_tables(nxt[0])
                if exists(last, u, LEAD - 1):
                    if u == 7:
                        silu(nxt[0], 1)
                    silu(nxt[0], hid_tile(nxt[1]))
                    silu_gate(*nxt)
                if u == 6 and not last:
                    lo_part(g + 1, 2)
                    conv(g + 1, 0)
                if u == 0:
                    out_tables(g)
                lo_part_out(g, u)
                if ahead:
                    lo_part(p, hid_tile(v) + 2 if u != 6 else 3)
                gated(g, u)
                if u == 0 and not first:
                    keep_squares(g - 1)
                if u == 7 and near:
                    keep_cb(nxt[0])
                elif near:
                    tokens_hid(*nxt)
                if u == 6 and not last:
                    silu(g + 1, 0)
                if near:
                    mix(*nxt)
                if u == 7 and near:
                    tokens_hid(*nxt)
                if u == 6 and ahead:
                    conv(p, 1)
                    lo_part(p, 4)
                if ahead:
                    conv(p, hid_tile(v))
                add_squares(g, u)
                if ahead:
                    lo_part(p, hid_tile(v) + 3)
                if u < HALF and not first:
                    add_out(g - 1, u)
                if u == 5 and not last:
                    conv_table(g + 1)
                if last and u >= 6:
                    context_levels(u - 6)

            done = [0]

            def note(ins):
                ins.then_inc(vec_chain, 1)
                done[0] += 1

            def chain():
                dve.wait_ge(vec_chain, done[0])

            def context_levels(s):
                if s == 0:
                    scales()
                dve.wait_ge(ctx_in[s], 16)
                v = ctx_raw[:, s]
                note(nc.vector.tensor_scalar(v, v, inv[:, 1:2], cst[:, 3:4], ALU.mult, ALU.add))
                chain()
                note(nc.vector.tensor_scalar(v, v, 0.0, 255.0, ALU.max, ALU.min))
                chain()
                nc.vector.tensor_scalar(lvl2[:, s], v, ROUND, -(ROUND + MID), ALU.add, ALU.add
                                        ).then_inc(lvl2_made, 1)

            def scales():
                dve.wait_ge(proj_made, TILES * GROUPS)
                dve.wait_ge(w_lo_made, TILES * GROUPS + 2)
                dve.wait_ge(w_in_s[(TILES * GROUPS + 4) % WRING], 16 * ((TILES * GROUPS + 4) // WRING + 1))
                dve.wait_ge(w_in_s[(TILES * GROUPS + 3) % WRING], 16 * ((TILES * GROUPS + 3) // WRING + 1))
                dve.wait_ge(w_in_s[(TILES * GROUPS + 2) % WRING], 16 * ((TILES * GROUPS + 2) // WRING + 1))
                note(nc.vector.memset(ones_bf[:], 1.0))
                note(nc.vector.reciprocal(inv[:, 0:1], cst[:, 0:1]))
                note(nc.vector.reciprocal(inv[:, 1:2], cst[:, 2:3]))
                note(nc.vector.tensor_scalar(shift[:, 0:1], cst[:, 1:2], -1.0, MID, ALU.mult, ALU.add))
                note(nc.vector.tensor_scalar(shift[:, 1:2], cst[:, 3:4], -1.0, MID, ALU.mult, ALU.add))
                note(nc.vector.tensor_tensor(s12[:, 0:1], cst[:, 0:1], cst[:, 2:3], ALU.mult))
                chain()
                note(nc.vector.tensor_tensor(s12[:, 1:2], s12[:, 0:1], shift[:, 0:1], ALU.mult))
                note(nc.vector.tensor_tensor(s12[:, 2:3], s12[:, 0:1], shift[:, 1:2], ALU.mult))
                chain()
                note(nc.vector.scalar_tensor_tensor(out=s12[:, 3:4], in0=s12[:, 1:2], scalar=float(D_MODEL),
                                                    in1=shift[:, 1:2], op0=ALU.mult, op1=ALU.mult))
                chain()

            run_steps(dve, step)
            for s in range(SEQS):
                dve.wait_ge(col_summed, s + 1)
                note(nc.vector.tensor_scalar(col[:, s, :], ps_p[s][:], s12[:, 1:2], s12[:, 3:4], ALU.mult,
                                             ALU.add))
            assert done[0] == C_COL, done[0]
            keep_squares(last_group)

            def variances(s):
                pair = (2 * s, 2 * s + 1)
                for b in pair:
                    note(nc.vector.bn_stats(stats[:, b, :], acc[:, b, :]))
                chain()
                for b in pair:
                    note(nc.vector.bn_aggr(mv[:, b, :], stats[:, b, :]))
                chain()
                nc.vector.tensor_scalar_add(var_e[:, 2 * s:2 * s + 2], mv[:, 2 * s:2 * s + 2, 1], EPS
                                            ).then_inc(var_set, 1)

            for s in range(SEQS):
                pair = (2 * s, 2 * s + 1)
                for b in pair:
                    add_out(last_group, b)
                dve.wait_ge(o_added, A_CREDIT + 2 * BLK * last_group + 2 * pair[1] + 2)
                variances(s)
            for s in range(SEQS):
                pair = (2 * s, 2 * s + 1)
                dve.wait_ge(rstd_set, s + 1)
                for b in pair:
                    note(nc.vector.tensor_scalar(n_t[:, b, :], acc[:, b, :], mv[:, b, 0:1],
                                                 rstd_t[:, b:b + 1], ALU.subtract, ALU.mult))
                chain()
                for b in pair:
                    note(nc.vector.tensor_scalar(n_t[:, b, :], n_t[:, b, :], inv[:, 0:1], cst[:, 1:2],
                                                 ALU.mult, ALU.add))
                chain()
                for b in pair:
                    note(nc.vector.tensor_scalar(n_t[:, b, :], n_t[:, b, :], 0.0, 255.0, ALU.max, ALU.min))
                chain()
                for b in pair:
                    nc.vector.tensor_scalar(lvl1[:, b, :], n_t[:, b, :], ROUND, -(ROUND + MID), ALU.add,
                                            ALU.add).then_inc(lvl1_made, 1)
            x_banks = [ps_o, ps_a[:, 0, :], ps_a[:, 1, :], ps_p[0]]
            for s in range(SEQS):
                pair = (2 * s, 2 * s + 1)
                dve.wait_ge(row_summed, s + 1)
                nc.vector.tensor_scalar(rsum[:, 2 * s:2 * s + 2], ps_x[:, 2 * s:2 * s + 2], s12[:, 2:3], None,
                                        ALU.mult).then_inc(rows_kept, 1)
                dve.wait_ge(rows_kept, s + 1)
                for b in pair:
                    note(nc.vector.scalar_tensor_tensor(out=acc[:, b, :], in0=col[:, s, :],
                                                        scalar=rsum[:, b:b + 1], in1=acc[:, b, :],
                                                        op0=ALU.add, op1=ALU.add))
                chain()
                for b in pair:
                    dve.wait_ge(x_made, b + 1)
                    note(nc.vector.scalar_tensor_tensor(out=acc[:, b, :], in0=x_banks[b][:],
                                                        scalar=s12[:, 0:1], in1=acc[:, b, :],
                                                        op0=ALU.mult, op1=ALU.add))
                chain()
                variances(s)
            for s in range(SEQS):
                dve.wait_ge(rstd_set, SEQS + s + 1)
                for b in (2 * s, 2 * s + 1):
                    nc.vector.tensor_scalar(n_t[:, b, :], acc[:, b, :], mv[:, b, 0:1],
                                            rstd_t[:, b:b + 1], ALU.subtract, ALU.mult).then_inc(n_made, 1)
            nz = LORA + EXPERTS
            for s in range(SEQS):
                pair = slice(2 * s, 2 * s + 2)
                dve.wait_ge(z_made, s + 1)
                nc.vector.tensor_copy(zl[:, pair].rearrange("t b z -> t (b z)"),
                                      ps_x[:, 2 * s * nz:2 * (s + 1) * nz]).then_inc(z_kept, 1)
                dve.wait_ge(z_kept, s + 1)
                logits = zl[:, pair, LORA:nz]
                note(nc.vector.tensor_tensor(logits, logits, cst[:, 4:8].unsqueeze(1).to_broadcast(
                    [P, 2, EXPERTS]), ALU.add))
                chain()
                note(nc.vector.tensor_reduce(lmax[:, pair], logits, AX_X, ALU.max))
                chain()
                note(nc.vector.tensor_tensor(hit[:, pair], logits, lmax[:, pair].unsqueeze(2).to_broadcast(
                    [P, 2, EXPERTS]), ALU.is_equal))
                chain()
                note(nc.vector.tensor_scalar(none_yet[:, pair], hit[:, pair], -1.0, 1.0, ALU.mult, ALU.add))
                chain()
                for e in range(1, EXPERTS):
                    note(nc.vector.tensor_tensor(hit[:, pair, e:], hit[:, pair, e:],
                                                 none_yet[:, pair, e - 1:e].to_broadcast(
                                                     [P, 2, EXPERTS - e]), ALU.mult))
                    chain()
                nc.vector.tensor_tensor(
                    zm[:, pair].rearrange("t b (e r) -> t b e r", e=EXPERTS),
                    zl[:, pair, 0:LORA].rearrange("t b (e r) -> t b e r", e=EXPERTS),
                    hit[:, pair].unsqueeze(3).to_broadcast([P, 2, EXPERTS, RANK]), ALU.mult
                ).then_inc(zm_made, 1)
            f_banks = [ps_o, ps_a[:, 0, :], ps_a[:, 1, :], ps_p[0]]
            for s in range(SEQS):
                dve.wait_ge(zm_turned, s + 1)
                nc.vector.tensor_copy(zm_t[:, 2 * s:2 * s + 2].rearrange("z b t -> z (b t)"),
                                      ps_p[1][0:LORA, 2 * s * P:2 * (s + 1) * P]).then_inc(zmt_kept, 1)
                for b in (2 * s, 2 * s + 1):
                    dve.wait_ge(f_made, b + 1)
                    nc.vector.tensor_tensor(acc[:, b, :], acc[:, b, :], f_banks[b][:], ALU.add
                                            ).then_inc(out_made, 1)


G_CONST = 9
G_RES = G_CONST + 2 + BLK
A_WDT = 1
A_HS = A_WDT + 1
A_HHI = A_HS + BLK
A_NEG = A_HHI + KT
A_ABS = A_NEG + 1
A_EX = A_ABS + 1
A_DTD = A_EX + SEQS
A_NACS = A_DTD + 1
V_VAR = 2 * BLK + 1
V_MS = V_VAR + 3
V_ACC = V_MS + 1
V_WDT = V_ACC + BLK
V_HLO = V_WDT + 3
V_DTX = V_HLO + KT + 1
V_ACS = V_DTX + 5 + 5 + 3 + BLK
V_ACS_SPLIT = V_ACS + 2
V_DTD = V_ACS_SPLIT + 2
V_TOK = V_DTD + 1
PE_DT = KT + 1
PE_ACS_T = PE_DT + 1
PE_DT_T = PE_ACS_T + 1
PE_DTD_T = PE_DT_T + 1
C_COL = 9 + 2 * SEQS + SEQS


def kernel(**inputs):
    import concourse.bacc as bacc
    from concourse.bass_utils import run_bass_kernel_spmd as run

    a = {k: np.asarray(v) for k, v in inputs.items()}
    d_inner = GROUPS * PAIRS * P
    tiles = []
    for g in range(GROUPS):
        tiles += [2 * d_inner + g * P, 2 * d_inner + (GROUPS + g) * P]
        for u in range(PAIRS):
            c = (g * PAIRS + u) * P
            tiles += [d_inner + c, c]
    tiles.append(2 * d_inner + 2 * GROUPS * P)
    w = a["L0_attn_in_proj_w"]
    w_in = np.concatenate([w[t:t + P] for t in tiles]).reshape(len(tiles), P, KT, P).transpose(0, 3, 2, 1)
    w_in = w_in.reshape(len(tiles), P, D_MODEL)
    w_in = np.concatenate([w_in, np.zeros((PAD_TILES, P, D_MODEL), w_in.dtype)])
    conv = np.concatenate([a["L0_attn_conv_w"], a["L0_attn_conv_b"][:, None]], axis=1)
    hid_c = conv[:d_inner].reshape(GROUPS, PAIRS, P, TAPS + 1)
    bc_c = conv[d_inner:].reshape(2, GROUPS, 1, P, TAPS + 1)
    conv_tab = np.concatenate([bc_c[0], bc_c[1], hid_c], axis=1).transpose(2, 0, 1, 3)
    arrays = {
        "x": a["x"],
        "w_in": w_in,
        "conv_tab": conv_tab,
        "d_tab": np.repeat(a["L0_attn_Dp"], HD).reshape(GROUPS, PAIRS, P).transpose(2, 0, 1),
        "gn_tab": a["L0_attn_gnorm_w"].reshape(GROUPS, PAIRS, P).transpose(2, 0, 1),
        "nw_tab": a["L0_attn_norm_w"].reshape(KT, P).T,
        "dtb_tab": a["L0_attn_dt_bias"].reshape(P, 1),
        "alog_tab": a["L0_attn_A_log"].reshape(P, 1),
        "w_out": a["L0_attn_out_proj_w"].T.reshape(GROUPS * PAIRS, P, D_MODEL),
        "ctx_in": a["ctx_4096"],
        "w_up": a["L0_ffn_W_up"].T.reshape(KT, P, D_MODEL).transpose(1, 0, 2),
        "w_z": np.concatenate([a["L0_ffn_lora_A"].reshape(LORA, D_MODEL), a["L0_ffn_gate_w"]]).T.reshape(
            KT, P, LORA + EXPERTS).transpose(1, 0, 2),
        "lora_b": a["L0_ffn_lora_B"].transpose(0, 2, 1).reshape(LORA, D_MODEL),
        "consts": np.concatenate([a["L0_xattn_x1_scale"], a["L0_xattn_x1_zp"], a["L0_xattn_x2_scale"],
                                  a["L0_xattn_x2_zp"], a["L0_ffn_expert_bias"]]).reshape(1, 8),
    }
    nc = bacc.Bacc("TRN2", target_bir_lowering=False, num_devices=1)
    feeds, args = {}, []
    for name, value in arrays.items():
        value = np.ascontiguousarray(value)
        feeds["in_" + name] = value
        args.append(nc.dram_tensor("in_" + name, value.shape, F32, kind="ExternalInput").ap())
    acs_rows = nc.dram_tensor("acs_rows", (2, GROUPS * PAIRS, 2, TOK), F32, kind="Internal").ap()
    out = nc.dram_tensor("out", a["x"].shape, F32, kind="ExternalOutput").ap()
    decoder_program(nc, *args, acs_rows, out)
    result = run(nc, [feeds], core_ids=[0])
    return result.results[0]["out"]
```

```python
from contextlib import ExitStack

import numpy as np

import concourse.bass as bass
from concourse import mybir

P = 128
D_MODEL = 512
KT = D_MODEL // P
TOK = 512
BLK = TOK // P
SEQS, SEQ = 2, 256
GROUPS = 8
PAIRS = 8
HEADS = 16
HD = 64
TILES = 2 * PAIRS + 2
CONVS = PAIRS + 2
WRING = 3
LEAD = 2
RING = 4
HALF = PAIRS // 2
TAPS = 4
PAD_TILES = 4
EPS = 1e-5
EXPERTS, RANK = 4, 8
LORA = EXPERTS * RANK
ROUND = float(2 ** 23)
MID = 128.0

F32 = mybir.dt.float32
F32R = mybir.dt.float32r
BF16 = mybir.dt.bfloat16
ACT = mybir.ActivationFunctionType
ALU = mybir.AluOpType
AX_X = mybir.AxisListType.X

CREDIT = 2
O_CREDIT = 2 * BLK
A_CREDIT = BLK


def decoder_program(nc, x, w_in, conv_tab, d_tab, gn_tab, nw_tab, dtb_tab, alog_tab, w_out, ctx_in,
                    w_up, w_z, lora_b, consts, acs_rows, out):
    x_blocks = x.rearrange("b (c p) d -> p (b c) d", p=P)
    out_blocks = out.rearrange("b (c p) d -> p (b c) d", p=P)
    ctx_tiles = ctx_in.rearrange("b (k p) n -> p b k n", p=P)

    with ExitStack() as stack:
        def sem(name):
            return stack.enter_context(nc.semaphore(name))

        base = (nc.sbuf_base + 63) // 64 * 64
        top = [base]
        place = {}

        def put(name, shape, dt, at=None):
            size = int(np.prod(shape[1:])) * (2 if dt == BF16 else 4)
            where = top[0] if at is None else at[0]
            t = nc.alloc_sbuf_tensor_at(name, shape, dt, offset=where)
            place[name] = where
            if at is None:
                top[0] = where + (size + 31) // 32 * 32
            else:
                at[0] = where + (size + 31) // 32 * 32
            return t

        acc = put("acc", [P, BLK, D_MODEL], F32)
        ident = put("ident", [P, P], F32)
        ident_bf = put("ident_bf", [P, P], BF16)
        causal = put("causal", [P, P], F32)
        ones_f = put("ones_f", [P, 2], F32)
        half_f = put("half_f", [P, BLK], F32)
        conv_all = put("conv_all", [P, GROUPS, CONVS, TAPS + 1], F32)
        d_all = put("d_all", [P, GROUPS, PAIRS], F32)
        gn_all = put("gn_all", [P, GROUPS, PAIRS], F32)
        cst = put("cst", [P, 8], F32)
        acs_all = put("acs_all", [P, BLK, P], F32)
        dt_all = put("dt_all", [P, BLK, P], F32)
        dtd_all = put("dtd_all", [P, SEQS, P], F32)
        conv_g = put("conv_g", [P, CONVS, TAPS + 1], F32)
        d_g = put("d_g", [P, PAIRS], F32)
        gn_g = put("gn_g", [P, PAIRS], F32)
        acs_g = put("acs_g", [P, BLK, HEADS], F32)
        dt_g = put("dt_g", [P, BLK, HEADS], F32)
        dtd_g = put("dtd_g", [P, SEQS, HEADS], F32)
        ss_g = put("ss_g", [P, BLK], F32)
        rstd_g = put("rstd_g", [P, BLK], F32)
        stats = put("stats", [P, BLK, 6], F32)
        mv = put("mv", [P, BLK, 2], F32)
        var_e = put("var_e", [P, BLK], F32)
        rstd_t = put("rstd_t", [P, BLK], F32)
        mshift = put("mshift", [P, BLK], F32)
        aff = put("aff", [P, 2, BLK], F32)

        hid = put("hid", [P, RING, TOK], F32)
        gate = put("gate", [P, RING, TOK], F32)
        b_t = put("b_t", [P, TOK], F32)
        c_t = put("c_t", [P, TOK], F32)
        c_cur = put("c_cur", [P, SEQS, P], F32)
        b_tok = put("b_tok", [P, SEQS, P], F32)
        cb = put("cb", [P, BLK, P], F32)
        rows = put("rows", [P, 2, 2, TOK], F32)
        decay = put("decay", [P, 2, 2, TOK], F32)
        eacs = put("eacs", [P, 2, 2, SEQS, P], F32)
        c_dec = put("c_dec", [P, 2, 2, SEQS, P], F32)
        hc = put("hc", [P, 2, BLK, P], F32)
        hcd = put("hcd", [P, 2, SEQS, P], F32)
        prev = put("prev", [P, 2, SEQS, P], F32)
        y1 = put("y1", [P, TOK], F32)
        yg = put("yg", [P, 2, TOK], F32)
        ysq = put("ysq", [P, 2, TOK], F32)
        ysum = put("ysum", [P, TOK], F32)
        o_part = put("o_part", [P, BLK, D_MODEL], F32)

        cacc = put("cacc", [P, 2, SEQS, SEQ], F32)
        th = put("th", [P, 2, TOK], F32)
        thg = put("thg", [P, TOK], F32)
        wo_raw = put("wo_raw", [P, 2, D_MODEL], F32)
        h_hi = put("h_hi", [P, KT, TOK], F32R)
        h_lo = put("h_lo", [P, KT, TOK], F32R)
        w_raw = put("w_raw", [P, WRING, D_MODEL], F32)
        w_hi = put("w_hi", [P, WRING, D_MODEL], F32R)
        w_lo = put("w_lo", [P, WRING, D_MODEL], F32R)

        y_hi = put("y_hi", [P, PAIRS, TOK], F32R)
        y_lo = put("y_lo", [P, PAIRS, TOK], F32R)
        wo_hi = put("wo_hi", [P, PAIRS, D_MODEL], F32R)
        wo_lo = put("wo_lo", [P, PAIRS, D_MODEL], F32R)
        assert top[0] <= nc.sbuf_usable_end, (top[0], nc.sbuf_usable_end)

        at = [place["y_hi"]]
        xt = put("xt", [P, BLK, D_MODEL], F32, at)
        hs = put("hs", [P, BLK, D_MODEL], F32, at)
        wdt_raw = put("wdt_raw", [P, D_MODEL], F32, at)
        wdt_hi = put("wdt_hi", [P, D_MODEL], F32R, at)
        wdt_lo = put("wdt_lo", [P, D_MODEL], F32R, at)
        dtx = put("dtx", [P, TOK], F32, at)
        dt_abs = put("dt_abs", [P, TOK], F32, at)
        ex = put("ex", [P, TOK], F32, at)
        zz = put("zz", [P, 2, TOK], F32, at)
        poly = put("poly", [P, TOK], F32, at)
        dt_h = put("dt_h", [P, TOK], F32, at)
        ac_h = put("ac_h", [P, TOK], F32, at)
        acs_h = put("acs_h", [P, TOK], F32, at)
        dtd_h = put("dtd_h", [P, SEQS, P], F32, at)
        one_row = put("one_row", [P, P], F32, at)
        nw = put("nw", [P, KT], F32, at)
        dtb = put("dtb", [P, 1], F32, at)
        alog = put("alog", [P, 1], F32, at)
        neg_a = put("neg_a", [P, 1], F32, at)
        ms_e = put("ms_e", [P, BLK], F32, at)
        rms = put("rms", [P, BLK], F32, at)
        both = put("both", [P, BLK], F32, at)
        assert at[0] <= top[0]

        at = [place["h_hi"]]
        ctx_raw = put("ctx_raw", [P, SEQS, KT, D_MODEL], F32, at)
        lvl2 = put("lvl2", [P, SEQS, KT, D_MODEL], BF16, at)
        wup = put("wup", [P, KT, D_MODEL], F32, at)
        wz = put("wz", [P, KT, LORA + EXPERTS], F32, at)
        ones_bf = put("ones_bf", [P, P], BF16, at)
        inv = put("inv", [P, 2], F32, at)
        shift = put("shift", [P, 2], F32, at)
        s12 = put("s12", [P, 4], F32, at)
        unround = put("unround", [P, 1], F32, at)
        rsum = put("rsum", [P, BLK], F32, at)
        assert at[0] <= place["y_hi"]
        at = [place["hid"]]
        n_t = put("n_t", [P, BLK, D_MODEL], F32, at)
        assert at[0] <= place["b_t"]
        at = [place["decay"]]
        lvl1 = put("lvl1", [P, BLK, D_MODEL], BF16, at)
        lvl1_t = put("lvl1_t", [P, KT, TOK], BF16, at)
        col = put("col", [P, SEQS, D_MODEL], F32, at)
        lb = put("lb", [3 * LORA, D_MODEL], F32, at)
        lb_s = put("lb_s", [3 * LORA, D_MODEL], F32R, at)
        z_t = put("z_t", [LORA + EXPERTS, TOK], F32, at)
        zl = put("zl", [P, BLK, LORA + EXPERTS], F32, at)
        lmax = put("lmax", [P, BLK], F32, at)
        hit = put("hit", [P, BLK, EXPERTS], F32, at)
        none_yet = put("none_yet", [P, BLK, EXPERTS], F32, at)
        zm = put("zm", [P, BLK, 3, LORA], F32, at)
        zm_r = put("zm_r", [P, BLK, LORA], F32R, at)
        assert at[0] <= place["y1"]

        at = [place["y_hi"]]
        wup_hi = put("wup_hi", [P, KT, D_MODEL], F32R, at)
        wup_lo = put("wup_lo", [P, KT, D_MODEL], F32R, at)
        zm_t = put("zm_t", [3 * LORA, BLK, P], F32R, at)
        wz_hi = put("wz_hi", [P, KT, LORA + EXPERTS], F32R, at)
        wz_lo = put("wz_lo", [P, KT, LORA + EXPERTS], F32R, at)
        n_hi = put("n_hi", [P, KT, TOK], F32R, at)
        n_lo = put("n_lo", [P, KT, TOK], F32R, at)
        assert at[0] <= top[0]

        ps_p = [stack.enter_context(nc.psum_tensor(f"ps_p{i}", [P, TOK], F32)) for i in range(2)]
        ps_a = stack.enter_context(nc.psum_tensor("ps_a", [P, 2, TOK], F32))
        ps_t = stack.enter_context(nc.psum_tensor("ps_t", [P, TOK], F32))
        ps_y = stack.enter_context(nc.psum_tensor("ps_y", [P, TOK], F32))
        ps_o = stack.enter_context(nc.psum_tensor("ps_o", [P, TOK], F32))
        ps_x = stack.enter_context(nc.psum_tensor("ps_x", [P, TOK], F32))
        tail_banks = [ps_a[:, 0, :], ps_a[:, 1, :], ps_p[0], ps_o]
        sum_banks = [ps_p[1], ps_x]
        turn_banks = [ps_t, ps_y, ps_p[1], ps_x]

        x_in = [sem(f"x_in{b}") for b in range(BLK)]
        tabs_in = sem("tabs_in")
        wdt_in = sem("wdt_in")
        w_in_s = [sem(f"w_in{i}") for i in range(WRING)]
        wo_in_s = [sem(f"wo_in{i}") for i in range(2)]
        rows_out = sem("rows_out")
        rows_in = [sem(f"rows_in{i}") for i in range(2)]
        ctx_in = [sem(f"ctx_in{s}") for s in range(SEQS)]
        ffn_in = sem("ffn_in")
        stored = sem("stored")
        pool_pre = sem("pool_pre")
        vec_pre = sem("vec_pre")
        act_pre = sem("act_pre")
        pe_pre = sem("pe_pre")
        w_hi_made = sem("w_hi_made")
        w_lo_made = sem("w_lo_made")
        proj_made = sem("proj_made")
        tapped = sem("tapped")
        conved = sem("conved")
        conv_tanh = sem("conv_tanh")
        silu_made = sem("silu_made")
        gate_tanh = sem("gate_tanh")
        gate_made = sem("gate_made")
        conv_tab_set = sem("conv_tab_set")
        out_tab_set = sem("out_tab_set")
        head_tabs = sem("head_tabs")
        fall_tab = sem("fall_tab")
        hid_turned = sem("hid_turned")
        e_made = sem("e_made")
        fall_made = sem("fall_made")
        l_made = sem("l_made")
        hc_made = sem("hc_made")
        hcd_made = sem("hcd_made")
        m_made = sem("m_made")
        c_copied = sem("c_copied")
        cdec_made = sem("cdec_made")
        state_made = sem("state_made")
        prev_made = sem("prev_made")
        y_made = sem("y_made")
        y1_made = sem("y1_made")
        yg_made = sem("yg_made")
        ysq_made = sem("ysq_made")
        ysum_made = sem("ysum_made")
        y_hi_made = sem("y_hi_made")
        y_lo_made = sem("y_lo_made")
        b_turned = sem("b_turned")
        btok_made = sem("btok_made")
        cb_made = sem("cb_made")
        cb_kept = sem("cb_kept")
        wo_hi_made = sem("wo_hi_made")
        wo_lo_made = sem("wo_lo_made")
        ss_summed = sem("ss_summed")
        ss_kept = sem("ss_kept")
        rstd_made = sem("rstd_made")
        o_made = sem("o_made")
        o_kept = sem("o_kept")
        o_added = sem("o_added")
        vec_chain = sem("vec_chain")
        scales_set = sem("scales_set")
        ctx_scaled = sem("ctx_scaled")
        ctx_rounded = sem("ctx_rounded")
        lvl2_made = sem("lvl2_made")
        var_set = sem("var_set")
        rstd_set = sem("rstd_set")
        lvl1_made = sem("lvl1_made")
        lvl1_turned = sem("lvl1_turned")
        lvl1_kept = sem("lvl1_kept")
        col_summed = sem("col_summed")
        col_kept = sem("col_kept")
        row_summed = sem("row_summed")
        rows_kept = sem("rows_kept")
        x_made = sem("x_made")
        n_made = sem("n_made")
        n_turned = sem("n_turned")
        affine_set = sem("affine_set")
        affine_made = sem("affine_made")
        shift_set = sem("shift_set")
        n_hi_made = sem("n_hi_made")
        n_lo_made = sem("n_lo_made")
        f_hi_made = sem("f_hi_made")
        f_lo_made = sem("f_lo_made")
        lb_split = sem("lb_split")
        z_made = sem("z_made")
        zt_kept = sem("zt_kept")
        z_turned = sem("z_turned")
        zm_made = sem("zm_made")
        zm_turned = sem("zm_turned")
        zmt_kept = sem("zmt_kept")
        f_made = sem("f_made")
        out_made = sem("out_made")

        def past(eng, s, count):
            if isinstance(count, int) and count < 1:
                return
            eng.wait_ge(s, count)

        def following(g, u, by):
            return (g + (u + by) // PAIRS, (u + by) % PAIRS)

        def exists(last, u, by):
            return not last or u + by < PAIRS

        def run_steps(eng, step):
            for u in range(HALF):
                step(0, u, False, True)
            with eng.Fori(0, GROUPS - 1) as g:
                for u in range(HALF, PAIRS):
                    step(g, u, False, False)
                for u in range(HALF):
                    step(g + 1, u, False, False)
            for u in range(HALF, PAIRS):
                step(GROUPS - 1, u, True, False)

        def hid_tile(u):
            return 2 + 2 * u

        def gate_tile(u):
            return 3 + 2 * u

        def conv_of(t):
            return t if t < 2 else 1 + t // 2

        def free_slot(g, u):
            return O_CREDIT + 2 * BLK * g - (BLK if u < HALF else 0)

        def bank_of(p, t):
            if isinstance(p, int) and p == 0 and t in (2, 3):
                return (ps_o, ps_x)[t - 2]
            return ps_p[t % 2]

        last_group = GROUPS - 1
        block = stack.enter_context(nc.Block())

        h_banks = [ps_t, ps_y, ps_o, ps_a[:, 0, :]]

        @block.sync
        def _(sp):
            def load_w(p, t):
                past(sp, w_lo_made, TILES * p + t - WRING + 1)
                sp.dma_start(w_raw[:, t % WRING, :],
                             w_in[bass.ds(TILES * p + t, 1)].rearrange("o p d -> p (o d)")
                             ).then_inc(w_in_s[t % WRING], 16)

            def load_wo(g, u):
                past(sp, wo_lo_made, CREDIT + PAIRS * g + u - 1)
                sp.dma_start(wo_raw[:, u % 2, :],
                             w_out[bass.ds(PAIRS * g + u, 1)].rearrange("o p d -> p (o d)")
                             ).then_inc(wo_in_s[u % 2], 16)

            def load_rows(g, u):
                past(sp, fall_made, PAIRS * g + u - 1)
                sp.dma_start(rows[:, u % 2], acs_rows[bass.ds(PAIRS * g + u, 1)].to_broadcast([P, 2, TOK])
                             ).then_inc(rows_in[u % 2], 16)

            for b in range(BLK):
                sp.dma_start(xt[:, b], x_blocks[:, b]).then_inc(x_in[b], 16)
            sp.dma_start(wdt_raw[:], w_in[TILES * GROUPS]).then_inc(wdt_in, 16)
            for dst, src in ((nw, nw_tab), (dtb, dtb_tab), (alog, alog_tab), (conv_all, conv_tab)):
                sp.dma_start(dst[:], src).then_inc(tabs_in, 16)
            for t in range(WRING):
                load_w(0, t)
            for dst, src in ((d_all, d_tab), (gn_all, gn_tab)):
                sp.dma_start(dst[:], src).then_inc(tabs_in, 16)
            sp.dma_start(cst[:], consts.to_broadcast([P, 8])).then_inc(tabs_in, 16)
            for t in range(WRING, 2 + 2 * LEAD + WRING):
                load_w(0, t)
            sp.wait_ge(vec_pre, V_ACS)
            sp.dma_start(acs_rows.rearrange("q h t -> (q h) t"), acs_h[:]).then_inc(rows_out, 16)
            sp.wait_ge(rows_out, 16)
            load_rows(0, 0)
            load_rows(0, 1)
            load_wo(0, 0)
            load_wo(0, 1)
            for t in range(2 + 2 * LEAD + WRING, 2 + 2 * LEAD + 5):
                load_w(0, t)

            load_rows(0, 2)

            def step(g, u, last, first):
                if exists(last, u, 3):
                    load_rows(*following(g, u, 3))
                if exists(last, u, LEAD):
                    load_w(*weights_ahead(g, u, 0))
                if exists(last, u, 2):
                    load_wo(*following(g, u, 2))
                if exists(last, u, LEAD):
                    load_w(*weights_ahead(g, u, 1))
                    if u == 5 and not last or u == 6:
                        load_w(*weights_ahead(g, u, 2))

            def weights_ahead(g, u, i):
                p, v = following(g, u, LEAD)
                t = hid_tile(v) + i - (1 if u == 6 else 0)
                return p, t + 5

            run_steps(sp, step)
            sp.wait_ge(proj_made, TILES * GROUPS)
            sp.wait_ge(w_lo_made, TILES * GROUPS + 2)
            for s_w in range(WRING):
                sp.wait_ge(w_in_s[s_w], 16 * ((TILES * GROUPS + 4 - s_w) // WRING + 1))
            for b in range(SEQS):
                sp.dma_start(ctx_raw[:, b], ctx_tiles[:, b]).then_inc(ctx_in[b], 16)
            sp.dma_start(wup[:], w_up).then_inc(ffn_in, 16)
            sp.dma_start(wz[:], w_z).then_inc(ffn_in, 16)
            sp.wait_ge(y_made, CREDIT + PAIRS * GROUPS)
            for i in range(3):
                sp.dma_start(lb[i * LORA:(i + 1) * LORA, :], lora_b).then_inc(ffn_in, 16)
            for b in range(BLK):
                sp.wait_ge(out_made, b + 1)
                sp.dma_start(out_blocks[:, b], acc[:, b, :]).then_inc(stored, 16)
            sp.wait_ge(stored, 16 * BLK)

        @block.gpsimd
        def _(pool):
            nc.gpsimd.memset(half_f[:], -0.5).then_inc(pool_pre, 1)
            for ap in (ident, ident_bf):
                nc.gpsimd.memset(ap[:], 0.0).then_inc(pool_pre, 1)
            nc.gpsimd.memset(causal[:], 1.0).then_inc(pool_pre, 1)
            nc.gpsimd.memset(ones_f[:], 1.0).then_inc(pool_pre, 1)
            nc.gpsimd.memset(one_row[:], 1.0).then_inc(pool_pre, 1)
            pool.wait_ge(pool_pre, 6)
            for ap in (ident, ident_bf):
                nc.gpsimd.affine_select(out=ap[:], in_=ap[:], compare_op=ALU.not_equal, fill=1.0, base=0,
                                        pattern=[[-1, P]], channel_multiplier=1).then_inc(pool_pre, 1)
            nc.gpsimd.affine_select(out=causal[:], in_=causal[:], compare_op=ALU.is_ge, fill=0.0, base=0,
                                    pattern=[[1, P]], channel_multiplier=-1).then_inc(pool_pre, 1)
            pool.sem_inc(cdec_made, CREDIT)
            pool.sem_inc(y_lo_made, CREDIT)
            pool.wait_ge(vec_pre, V_VAR)
            nc.gpsimd.tensor_tensor(rstd_t[:], var_e[:], half_f[:], ALU.pow).then_inc(pool_pre, 1)
            pool.wait_ge(vec_pre, V_MS)
            nc.gpsimd.tensor_tensor(rms[:], ms_e[:], half_f[:], ALU.pow).then_inc(pool_pre, 1)
            for b in range(BLK):
                if b < 2:
                    pool.wait_ge(act_pre, A_HS + b)
                else:
                    pool.wait_ge(vec_pre, V_HS + b - 2)
                nc.gpsimd.tensor_tensor(acc[:, b, :], acc[:, b, :], xt[:, b, :], ALU.add
                                        ).then_inc(pool_pre, 1)

            def c_decayed(g, u):
                if u == 0:
                    pool.wait_ge(c_copied, g + 1)
                pool.wait_ge(e_made, PAIRS * g + u + 1)
                pool.wait_ge(y_made, CREDIT + PAIRS * g + u - 1)
                for h in range(2):
                    ins = nc.gpsimd.tensor_tensor(c_dec[:, u % 2, h], eacs[:, u % 2, h], c_cur[:], ALU.mult)
                ins.then_inc(cdec_made, 1)

            def low_part(g, u):
                pool.wait_ge(y_hi_made, PAIRS * g + u + 1)
                pool.wait_ge(o_made, free_slot(g, u))
                nc.gpsimd.tensor_tensor(y_lo[:, u, :], yg[:, u % 2, :], y_hi[:, u, :].bitcast(F32),
                                        ALU.subtract).then_inc(y_lo_made, 1)

            def norm(g):
                pool.wait_ge(ss_kept, g + 1)
                pool.wait_ge(o_added, A_CREDIT + 2 * BLK * g)
                nc.gpsimd.tensor_tensor(rstd_g[:], ss_g[:], half_f[:], ALU.pow).then_inc(rstd_made, 1)

            c_decayed(0, 0)

            def step(g, u, last, first):
                if exists(last, u, 1):
                    c_decayed(*following(g, u, 1))
                low_part(g, u)
                if u == 0 and not first:
                    norm(g - 1)

            run_steps(pool, step)
            norm(last_group)

            def inverse_deviation(i):
                b = slice(2 * (i % SEQS), 2 * (i % SEQS) + 2)
                pool.wait_ge(var_set, i + 1)
                nc.gpsimd.tensor_tensor(rstd_t[:, b], var_e[:, b], half_f[:, 0:2],
                                        ALU.pow).then_inc(rstd_set, 1)

            for i in range(SEQS):
                inverse_deviation(i)
            for i, (raw, hi, lo) in enumerate(((wz, wz_hi, wz_lo), (wup, wup_hi, wup_lo))):
                pool.wait_ge(f_hi_made, i + 1)
                nc.gpsimd.tensor_tensor(lo[:], raw[:], hi[:].bitcast(F32), ALU.subtract
                                        ).then_inc(f_lo_made, 1)
            for i in range(SEQS, 2 * SEQS):
                inverse_deviation(i)

        @block.scalar
        def _(act):
            act.sem_inc(ysq_made, CREDIT)
            act.sem_inc(prev_made, CREDIT)
            act.wait_ge(wdt_in, 16)
            nc.scalar.activation(wdt_hi[:], wdt_raw[:], ACT.Copy).then_inc(act_pre, 1)

            def hi_part(p, t):
                act.wait_ge(w_in_s[t % WRING], 96 * p + 16 * (t // WRING + 1))
                past(act, proj_made, TILES * p + t - WRING + 1)
                nc.scalar.activation(w_hi[:, t % WRING, :], w_raw[:, t % WRING, :],
                                     ACT.Copy).then_inc(w_hi_made, 1)

            act.wait_ge(pool_pre, G_CONST + 2)
            for b in range(2):
                act.wait_ge(vec_pre, V_ACC + b)
                nc.scalar.activation(hs[:, b, :], acc[:, b, :], ACT.Copy, scale=rms[:, b:b + 1]
                                     ).then_inc(act_pre, 1)
            hi_part(0, 0)
            act.wait_ge(tabs_in, 16 * 7)
            for k in range(KT):
                act.wait_ge(pe_pre, k + 1)
                nc.scalar.activation(h_hi[:, k, :], h_banks[k][:], ACT.Copy,
                                     scale=nw[:, k:k + 1]).then_inc(act_pre, 1)
            hi_part(0, 1)
            hi_part(0, 2)
            nc.scalar.activation(neg_a[:], alog[:], ACT.Exp).then_inc(act_pre, 1)
            act.wait_ge(pe_pre, PE_DT)
            nc.scalar.activation(dt_abs[:], ps_x[:], ACT.Abs, bias=dtb[:, 0:1]).then_inc(act_pre, 1)
            act.wait_ge(act_pre, A_ABS)
            nc.scalar.activation(ex[:], dt_abs[:], ACT.Exp, scale=-1.0).then_inc(act_pre, 1)

            def tap(p, t):
                i = conv_of(t)
                act.wait_ge(proj_made, TILES * p + t + 1)
                past(act, silu_made, CONVS * p + i - 1)
                nc.scalar.activation(cacc[:, i % 2].rearrange("c b t -> c (b t)"), bank_of(p, t)[:],
                                     ACT.Identity, bias=conv_g[:, i, TAPS:TAPS + 1],
                                     scale=conv_g[:, i, TAPS - 1:TAPS]).then_inc(tapped, 1)

            def tanh_conv(p, t):
                i = conv_of(t)
                act.wait_ge(conved, 3 * (CONVS * p + i) + 3)
                nc.scalar.activation(th[:, i % 2, :], cacc[:, i % 2].rearrange("c b t -> c (b t)"),
                                     ACT.Tanh).then_inc(conv_tanh, 1)

            def tanh_gate(p, u):
                act.wait_ge(proj_made, TILES * p + gate_tile(u) + 1)
                past(act, gate_made, PAIRS * p + u)
                nc.scalar.activation(thg[:], bank_of(p, gate_tile(u))[:], ACT.Tanh, scale=0.5).then_inc(gate_tanh, 1)

            def exp_rows(g, u):
                act.wait_ge(rows_in[u % 2], 16 * (HALF * g + u // 2 + 1))
                act.wait_ge(cdec_made, CREDIT + PAIRS * g + u - 1)
                nc.scalar.activation(
                    eacs[:, u % 2], rows[:, u % 2].rearrange("n h (b c i) -> n h b c i", b=SEQS, c=2)[:, :, :, 1, :],
                    ACT.Exp).then_inc(e_made, 1)

            def fall(g, u):
                if u == 0:
                    act.wait_ge(fall_tab, g + 1)
                act.wait_ge(rows_in[u % 2], 16 * (HALF * g + u // 2 + 1))
                act.wait_ge(y_made, CREDIT + PAIRS * g + u - 1)
                for h in range(2):
                    for b in range(BLK):
                        ins = nc.scalar.activation(
                            decay[:, u % 2, h, b * P:(b + 1) * P], rows[:, u % 2, h, b * P:(b + 1) * P], ACT.Relu,
                            scale=-1.0, bias=acs_g[:, b, 2 * u + h:2 * u + h + 1])
                ins.then_inc(fall_made, 1)

            def exp_decay(g, u):
                act.wait_ge(fall_made, PAIRS * g + u + 1)
                nc.scalar.activation(decay[:, u % 2], decay[:, u % 2], ACT.Exp, scale=-1.0
                                     ).then_inc(l_made, 1)

            def keep_state(g, u):
                act.wait_ge(state_made, CREDIT + PAIRS * g + u + 1)
                act.wait_ge(y_made, CREDIT + PAIRS * g + u - 1)
                nc.scalar.copy(prev[:, u % 2], ps_x[:, 0:2 * P].rearrange("n (b c) -> n b c", b=SEQS)
                               ).then_inc(prev_made, 1)

            def high_and_square(g, u):
                act.wait_ge(yg_made, PAIRS * g + u + 1)
                act.wait_ge(o_made, free_slot(g, u))
                nc.scalar.activation(y_hi[:, u, :], yg[:, u % 2, :], ACT.Copy).then_inc(y_hi_made, 1)
                act.wait_ge(ysum_made, CREDIT + PAIRS * g + u - 1)
                nc.scalar.activation(ysq[:, u % 2, :], yg[:, u % 2, :], ACT.Square).then_inc(ysq_made, 1)

            def hi_part_out(g, u):
                if u == 0:
                    act.wait_ge(out_tab_set, g + 1)
                act.wait_ge(wo_in_s[u % 2], 64 * g + 16 * (u // 2 + 1))
                act.wait_ge(o_made, free_slot(g, u))
                nc.scalar.activation(wo_hi[:, u, :], wo_raw[:, u % 2, :], ACT.Copy,
                                     scale=gn_g[:, u:u + 1]).then_inc(wo_hi_made, 1)

            def keep_bc(g):
                act.wait_ge(b_turned, g + 1)
                past(act, state_made, CREDIT + PAIRS * g)
                nc.scalar.copy(b_tok[:], ps_o[:, 0:2 * P].rearrange("n (b c) -> n b c", b=SEQS)
                               ).then_inc(btok_made, 1)
                act.wait_ge(silu_made, CONVS * g + 2)
                act.wait_ge(cdec_made, CREDIT + PAIRS * g)
                nc.scalar.copy(c_cur[:], c_t[:].rearrange("n (b c i) -> n b c i", b=SEQS, c=2)[:, :, 1, :]
                               ).then_inc(c_copied, 1)

            def keep_half(g, b):
                act.wait_ge(o_made, O_CREDIT + 2 * BLK * g + b + 1)
                nc.scalar.copy(o_part[:, b, :], ps_o[:]).then_inc(o_kept, 1)

            def context_scaled(q):
                act.wait_ge(scales_set, 1)
                act.wait_ge(ctx_in[q], 16)
                nc.scalar.activation(ctx_raw[:, q], ctx_raw[:, q], ACT.Relu, scale=inv[:, 1:2],
                                     bias=cst[:, 3:4]).then_inc(ctx_scaled, 1)

            def context_levels(q):
                act.wait_ge(ctx_rounded, q + 1)
                nc.scalar.activation(lvl2[:, q], ctx_raw[:, q], ACT.Identity, bias=unround[:, 0:1]
                                     ).then_inc(lvl2_made, 1)

            act.wait_ge(conv_tab_set, 1)
            for t in (0, 1):
                hi_part(0, t + WRING)
                tap(0, t)
            hi_part(0, 5)
            tanh_gate(0, 0)
            act.wait_ge(vec_pre, V_ACS)
            for b in range(SEQS):
                nc.scalar.activation(dtd_h[:, b, :], acs_h[:, 2 * b * P:(2 * b + 1) * P], ACT.Exp,
                                     scale=-1.0, bias=acs_h[:, (2 * b + 1) * P - 1:(2 * b + 1) * P]
                                     ).then_inc(act_pre, 1)
            act.wait_ge(pe_pre, PE_ACS_T)
            nc.scalar.activation(acs_all[:].rearrange("t b h -> t (b h)"), ps_y[:], ACT.Copy
                                 ).then_inc(act_pre, 1)
            act.wait_ge(pe_pre, PE_DT_T)
            nc.scalar.activation(dt_all[:].rearrange("t b h -> t (b h)"), ps_t[:], ACT.Copy
                                 ).then_inc(act_pre, 1)
            tanh_conv(0, 0)
            tanh_conv(0, 1)
            tap(0, 2)
            exp_rows(0, 0)
            hi_part(0, 6)
            tanh_conv(0, 2)
            fall(0, 0)
            keep_bc(0)
            exp_decay(0, 0)
            tap(0, 4)
            hi_part(0, 7)
            keep_state(0, 0)
            exp_rows(0, 1)
            fall(0, 1)
            tanh_conv(0, 4)
            tanh_gate(0, 1)

            def step(g, u, last, first):
                near = exists(last, u, 1)
                ahead = exists(last, u, LEAD)
                p, v = following(g, u, LEAD)
                nxt = following(g, u, 1)
                if u == 7 and near:
                    keep_bc(nxt[0])
                if ahead:
                    hi_part(p, hid_tile(v) + 2 if u != 6 else 3)
                if u == 6 and not last:
                    tanh_conv(g + 1, 0)
                if near:
                    exp_decay(*nxt)
                hi_part_out(g, u)
                if last and u == 7:
                    context_scaled(0)
                high_and_square(g, u)
                if u == 6 and ahead:
                    tap(p, 1)
                    hi_part(p, 4)
                if ahead:
                    tap(p, hid_tile(v))
                    exp_rows(p, v)
                    fall(p, v)
                if u == 6 and ahead:
                    tanh_conv(p, 1)
                if first or u == 6 and ahead:
                    keep_state(*nxt)
                if ahead:
                    hi_part(p, hid_tile(v) + 3)
                    tanh_conv(p, hid_tile(v))
                if u >= HALF:
                    keep_half(g, u - HALF)
                if near and not (first or u == 6 and ahead):
                    keep_state(*nxt)
                if ahead:
                    tanh_gate(p, v)
                if u == 5 and not last:
                    hi_part(g + 1, 2)
                    act.wait_ge(conv_tab_set, g + 2)
                    tap(g + 1, 0)

            run_steps(act, step)

            context_levels(0)
            context_scaled(1)
            context_levels(1)

            def affine_stream(q):
                act.wait_ge(affine_set, q + 1)
                for b in (2 * q, 2 * q + 1):
                    nc.scalar.activation(n_t[:, b, :], acc[:, b, :], ACT.Identity, scale=aff[:, 0, b:b + 1],
                                         bias=aff[:, 1, b:b + 1]).then_inc(affine_made, 1)

            affine_stream(0)
            act.wait_ge(ffn_in, 80)
            act.wait_ge(o_made, O_CREDIT + 2 * BLK * GROUPS)
            for raw, hi in ((wz, wz_hi), (wup, wup_hi)):
                nc.scalar.activation(hi[:].rearrange("d k o -> d (k o)"), raw[:].rearrange("d k o -> d (k o)"),
                                     ACT.Copy).then_inc(f_hi_made, 1)
            affine_stream(1)
            nc.scalar.activation(lb_s[:], lb[:], ACT.Copy).then_inc(f_hi_made, 1)
            for i in range(2 * SEQS):
                q, j = divmod(i, 2)
                act.wait_ge(lvl1_turned, i + 1)
                nc.scalar.copy(lvl1_t[:, 2 * j:2 * j + 2, 2 * q * P:2 * (q + 1) * P],
                               turn_banks[j][:, 0:TOK // 2].bitcast(BF16).rearrange("d (k t) -> d k t", k=2)
                               ).then_inc(lvl1_kept, 1)
            for q in range(SEQS):
                act.wait_ge(shift_set, q + 1)
                for b in (2 * q, 2 * q + 1):
                    nc.scalar.activation(n_t[:, b, :], acc[:, b, :], ACT.Identity, scale=rstd_t[:, b:b + 1],
                                         bias=mshift[:, b:b + 1]).then_inc(n_made, 1)
                for j in range(2):
                    act.wait_ge(n_turned, 2 * q + j + 1)
                    nc.scalar.activation(n_hi[:, 2 * j:2 * j + 2, 2 * q * P:2 * (q + 1) * P],
                                         turn_banks[2 * q + j][:].rearrange("d (k t) -> d k t", k=2),
                                         ACT.Copy).then_inc(n_hi_made, 1)
            act.wait_ge(z_made, SEQS)
            nc.scalar.copy(z_t[:], ps_t[0:LORA + EXPERTS, :]).then_inc(zt_kept, 1)

        @block.tensor
        def _(pe):
            pe.sem_inc(y_made, CREDIT)
            pe.sem_inc(state_made, CREDIT)
            pe.sem_inc(o_made, O_CREDIT)
            pe.sem_inc(ss_summed, 1)

            def three(bank, stat_hi, stat_lo, mov_hi, mov_lo, first, last):
                nc.tensor.matmul(bank, stat_hi, mov_hi, start=first, stop=False)
                nc.tensor.matmul(bank, stat_lo, mov_hi, start=False, stop=False)
                return nc.tensor.matmul(bank, stat_hi, mov_lo, start=False, stop=last)

            pe.wait_ge(pool_pre, G_CONST)
            for k in range(KT):
                for b in range(BLK):
                    if k == 0:
                        if b < 2:
                            pe.wait_ge(act_pre, A_HS + b)
                        else:
                            pe.wait_ge(vec_pre, V_HS + b - 2)
                    ins = nc.tensor.transpose(h_banks[k][:, b * P:(b + 1) * P],
                                              hs[:, b, k * P:(k + 1) * P], ident[:])
                ins.then_inc(pe_pre, 1)
            pe.wait_ge(vec_pre, V_WDT)
            for k in range(KT):
                pe.wait_ge(vec_pre, V_HLO + k)
                ins = three(ps_x[:], wdt_hi[:, k * P:(k + 1) * P], wdt_lo[:, k * P:(k + 1) * P],
                            h_hi[:, k, :], h_lo[:, k, :], k == 0, k == KT - 1)
            ins.then_inc(pe_pre, 1)

            def project(p, t):
                pe.wait_ge(w_lo_made, TILES * p + t + 1)
                if isinstance(p, int) and p == 0 and t < 6:
                    if t == 3:
                        pe.wait_ge(vec_pre, V_DTX)
                    elif t > 3:
                        pe.wait_ge(conved, 3 * (t - 3))
                elif t == 0:
                    past(pe, conved, 3 * CONVS * p)
                elif t == 1:
                    past(pe, gate_made, PAIRS * p)
                elif t == 2:
                    past(pe, conved, 3 * (CONVS * p + 1))
                elif t == 3:
                    past(pe, conved, 3 * (CONVS * p + 2))
                elif t % 2 == 0:
                    pe.wait_ge(conved, 3 * (CONVS * p + conv_of(t)))
                else:
                    pe.wait_ge(gate_made, PAIRS * p + t // 2 - 1)
                s = t % WRING
                for k in range(KT):
                    w = slice(k * P, (k + 1) * P)
                    ins = three(bank_of(p, t)[:], w_hi[:, s, w], w_lo[:, s, w], h_hi[:, k, :], h_lo[:, k, :],
                                k == 0, k == KT - 1)
                ins.then_inc(proj_made, 1)

            def turn_hid(g, u):
                past(pe, hcd_made, PAIRS * g + u)
                pe.wait_ge(silu_made, CONVS * g + 2 + u + 1)
                for b in range(BLK):
                    ins = nc.tensor.transpose(ps_t[:, b * P:(b + 1) * P],
                                              hid[:, u % RING, b * P:(b + 1) * P], ident[:])
                ins.then_inc(hid_turned, 1)

            def states(g, u):
                pe.wait_ge(hcd_made, PAIRS * g + u + 1)
                if u == 0:
                    pe.wait_ge(cb_kept, g + 1)
                    pe.wait_ge(btok_made, g + 1)
                else:
                    pe.wait_ge(prev_made, CREDIT + PAIRS * g + u)
                if u == 1:
                    past(pe, ss_kept, g)
                for b in range(SEQS):
                    ins = nc.tensor.matmul(ps_x[:, b * P:(b + 1) * P], b_tok[:, b, :],
                                           hcd[:, u % 2, b, :], start=True, stop=True)
                ins.then_inc(state_made, 1)

            def scan(g, u):
                pe.wait_ge(m_made, PAIRS * g + u + 1)
                pe.wait_ge(hc_made, PAIRS * g + u + 1)
                pe.wait_ge(prev_made, CREDIT + PAIRS * g + u + 1)
                pe.wait_ge(cdec_made, CREDIT + PAIRS * g + u + 1)
                past(pe, y1_made, PAIRS * g + u)
                r = u % 2
                for b in range(BLK):
                    for h in range(2):
                        ch = slice(h * HD, (h + 1) * HD)
                        dst = ps_y[ch, b * P:(b + 1) * P]
                        ins = nc.tensor.matmul(dst, hc[:, r, b, ch], decay[:, r, h, b * P:(b + 1) * P],
                                               start=True, stop=(b % 2 == 0))
                    if b % 2 == 1:
                        for h in range(2):
                            ch = slice(h * HD, (h + 1) * HD)
                            dst = ps_y[ch, b * P:(b + 1) * P]
                            ins = nc.tensor.matmul(dst, prev[:, r, b // 2, ch], c_dec[:, r, h, b // 2, :],
                                                   start=False, stop=True)
                ins.then_inc(y_made, 1)

            def group_products(g):
                pe.wait_ge(silu_made, CONVS * g + 2)
                past(pe, o_kept, BLK * g - 1)
                for b in range(SEQS):
                    ins = nc.tensor.transpose(ps_o[:, b * P:(b + 1) * P],
                                              b_t[:, 2 * b * P:(2 * b + 1) * P], ident[:])
                ins.then_inc(b_turned, 1)
                past(pe, prev_made, CREDIT + PAIRS * g)
                for b in range(BLK):
                    ins = nc.tensor.matmul(ps_x[:, b * P:(b + 1) * P], b_t[:, b * P:(b + 1) * P],
                                           c_t[:, b * P:(b + 1) * P], start=True, stop=True)
                ins.then_inc(cb_made, 1)

            def sum_squares(g):
                pe.wait_ge(ysum_made, CREDIT + PAIRS * g + PAIRS)
                if not (isinstance(g, int) and g == last_group):
                    pe.wait_ge(prev_made, CREDIT + PAIRS * g + PAIRS + 1)
                for b in range(BLK):
                    ins = nc.tensor.matmul(ps_x[:, b:b + 1], ysum[:, b * P:(b + 1) * P], ones_f[:, 0:1],
                                           start=True, stop=True)
                ins.then_inc(ss_summed, 1)

            def out_half(g, half, b):
                if b == 0:
                    pe.wait_ge(y_lo_made, CREDIT + PAIRS * g + HALF * (half + 1))
                    pe.wait_ge(wo_lo_made, CREDIT + PAIRS * g + HALF * (half + 1))
                if half == 0 and b == 0:
                    pe.wait_ge(o_added, A_CREDIT + 2 * BLK * g)
                elif half == 0 or b == 0:
                    pe.wait_ge(o_kept, BLK * g + (b if half == 0 else BLK))
                else:
                    pe.wait_ge(o_added, A_CREDIT + 2 * BLK * g + 2 * b - 1)
                t = slice(b * P, (b + 1) * P)
                for u in range(HALF * half, HALF * (half + 1)):
                    ins = three(ps_o[:], y_hi[:, u, t], y_lo[:, u, t], wo_hi[:, u, :], wo_lo[:, u, :],
                                u % HALF == 0, u % HALF == HALF - 1)
                ins.then_inc(o_made, 1)

            for t in range(4):
                project(0, t)
            pe.wait_ge(vec_pre, V_ACS)
            for b in range(BLK):
                ins = nc.tensor.transpose(ps_y[:, b * P:(b + 1) * P], acs_h[:, b * P:(b + 1) * P], ident[:])
            ins.then_inc(pe_pre, 1)
            for b in range(BLK):
                ins = nc.tensor.transpose(ps_t[:, b * P:(b + 1) * P], dt_h[:, b * P:(b + 1) * P], ident[:])
            ins.then_inc(pe_pre, 1)
            project(0, 4)
            pe.wait_ge(vec_pre, V_DTD)
            pe.wait_ge(gate_made, 1)
            for b in range(SEQS):
                ins = nc.tensor.transpose(ps_x[:, b * P:(b + 1) * P], dtd_h[:, b, :], ident[:])
            ins.then_inc(pe_pre, 1)
            pe.wait_ge(vec_pre, V_TOK)
            pe.wait_ge(act_pre, A_DT)
            group_products(0)
            turn_hid(0, 0)
            project(0, 5)
            states(0, 0)

            def step(g, u, last, first):
                near = exists(last, u, 1)
                ahead = exists(last, u, LEAD)
                p, v = following(g, u, LEAD)
                nxt = following(g, u, 1)
                scan(g, u)
                if u == 0 and not first:
                    sum_squares(g - 1)
                if u == 7 and near:
                    group_products(nxt[0])
                if near:
                    turn_hid(*nxt)
                if u == 6 and ahead:
                    project(p, 1)
                if ahead:
                    project(p, hid_tile(v))
                if u == 7 and near:
                    pe.wait_ge(btok_made, g + 2)
                if u >= HALF:
                    out_half(g, 0, u - HALF)
                elif not first:
                    out_half(g - 1, 1, u)
                if near:
                    states(*nxt)
                if ahead:
                    project(p, gate_tile(v))
                if u == 5 and not last:
                    project(g + 1, 0)

            run_steps(pe, step)
            for b in range(BLK):
                if b == 0:
                    pe.wait_ge(y_lo_made, CREDIT + PAIRS * GROUPS - 1)
                    pe.wait_ge(wo_lo_made, CREDIT + PAIRS * GROUPS - 1)
                if b == BLK - 1:
                    pe.wait_ge(o_kept, BLK * GROUPS)
                t = slice(b * P, (b + 1) * P)
                for u in range(HALF, PAIRS):
                    if b == 0 and u == HALF + 1:
                        sum_squares(last_group)
                    if b == 0 and u == PAIRS - 1:
                        pe.wait_ge(y_lo_made, CREDIT + PAIRS * GROUPS)
                        pe.wait_ge(wo_lo_made, CREDIT + PAIRS * GROUPS)
                    ins = three(tail_banks[b][:], y_hi[:, u, t], y_lo[:, u, t], wo_hi[:, u, :],
                                wo_lo[:, u, :], u == HALF, u == PAIRS - 1)
                ins.then_inc(o_made, 1)
            def column_sum(q):
                pe.wait_ge(lvl2_made, q + 1)
                for k in range(KT):
                    ins = nc.tensor.matmul(sum_banks[q][:], ones_bf[:], lvl2[:, q, k, :], start=(k == 0),
                                           stop=(k == KT - 1))
                ins.then_inc(col_summed, 1)

            for q in range(SEQS):
                if q == 1:
                    column_sum(0)
                for j in range(2):
                    past(pe, lvl1_kept, 2 * (q - 1) + j + 1)
                    bank = turn_banks[j][:, 0:TOK // 2].bitcast(BF16)
                    for k in (0, 1):
                        for b in (0, 1):
                            pe.wait_ge(lvl1_made, 2 * q + b + 1)
                            c = (2 * k + b) * P
                            ins = nc.tensor.transpose(
                                bank[:, c:c + P],
                                lvl1[:, 2 * q + b, (2 * j + k) * P:(2 * j + k + 1) * P], ident_bf[:])
                    ins.then_inc(lvl1_turned, 1)
            pe.wait_ge(lvl1_kept, 2 * SEQS)
            for b in range(BLK):
                for k in range(KT):
                    ins = nc.tensor.matmul(ps_t[:, b:b + 1], lvl1_t[:, k, b * P:(b + 1) * P],
                                           ones_bf[:, 0:1], start=(k == 0), stop=(k == KT - 1))
            ins.then_inc(row_summed, 1)
            for q in range(SEQS):
                for b in (2 * q, 2 * q + 1):
                    pe.wait_ge(o_added, A_CREDIT + 2 * BLK * last_group + BLK + b + 1)
                    for k in range(KT):
                        ins = nc.tensor.matmul(tail_banks[b][:], lvl1_t[:, k, b * P:(b + 1) * P],
                                               lvl2[:, q, k, :], start=(k == 0), stop=(k == KT - 1))
                    ins.then_inc(x_made, 1)
                if q == 0:
                    pe.wait_ge(ss_kept, GROUPS)
                    column_sum(1)

            nz = LORA + EXPERTS

            def forward(b, tiles=range(KT)):
                t = slice(b * P, (b + 1) * P)
                for k in tiles:
                    three(tail_banks[b][:], n_hi[:, k, t], n_lo[:, k, t], wup_hi[:, k, :], wup_lo[:, k, :],
                          k == 0, False)

            def add_lora(b):
                nc.tensor.matmul(tail_banks[b][:], zm_t[:, b, :], lb_s[:], start=False,
                                 stop=True).then_inc(f_made, 1)

            def turn_stream(q):
                for j in range(2):
                    if q == 0 and j == 0:
                        pe.wait_ge(rows_kept, 1)
                    elif q == 1:
                        pe.wait_ge(col_kept, j + 1)
                    for k in (0, 1):
                        for b in (0, 1):
                            pe.wait_ge(n_made, 2 * q + b + 1)
                            c = (2 * k + b) * P
                            ins = nc.tensor.transpose(
                                turn_banks[2 * q + j][:, c:c + P],
                                n_t[:, 2 * q + b, (2 * j + k) * P:(2 * j + k + 1) * P], ident[:])
                    ins.then_inc(n_turned, 1)

            def small_products(q):
                pe.wait_ge(n_lo_made, 2 * (q + 1))
                t = slice(2 * q * P, 2 * (q + 1) * P)
                for k in range(KT):
                    ins = three(ps_t[0:nz, t], wz_hi[:, k, :], wz_lo[:, k, :], n_hi[:, k, t], n_lo[:, k, t],
                                k == 0, k == KT - 1)
                ins.then_inc(z_made, 1)

            turn_stream(0)
            pe.wait_ge(f_lo_made, 1)
            small_products(0)
            pe.wait_ge(f_lo_made, 2)
            forward(0)
            turn_stream(1)
            forward(1)
            small_products(1)
            forward(2, (0, 1))
            pe.wait_ge(zt_kept, 1)
            for b in range(BLK):
                ins = nc.tensor.transpose(ps_y[:, b * nz:(b + 1) * nz], z_t[:, b * P:(b + 1) * P],
                                          ident[0:nz, 0:nz])
            ins.then_inc(z_turned, 1)
            forward(2, (2, 3))
            forward(3)
            pe.wait_ge(zm_made, 1)
            for b in range(BLK):
                ins = nc.tensor.transpose(ps_p[1][0:3 * LORA, b * P:(b + 1) * P],
                                          zm[:, b].rearrange("t i z -> t (i z)"), ident[:])
            ins.then_inc(zm_turned, 1)
            pe.wait_ge(zmt_kept, 1)
            pe.wait_ge(lb_split, 1)
            for b in range(BLK):
                add_lora(b)

        @block.vector
        def _(dve):
            pre = [0]

            def mark(ins):
                ins.then_inc(vec_pre, 1)
                pre[0] += 1
                return pre[0]

            dve.sem_inc(wo_lo_made, CREDIT)
            dve.sem_inc(ysum_made, CREDIT)
            dve.sem_inc(o_added, A_CREDIT)

            for b in range(BLK):
                dve.wait_ge(x_in[b], 16)
                mark(nc.vector.bn_stats(stats[:, b, :], xt[:, b, :]))
            for b in range(BLK):
                dve.wait_ge(vec_pre, b + 1)
                mark(nc.vector.bn_aggr(mv[:, b, :], stats[:, b, :]))
            dve.wait_ge(vec_pre, pre[0])
            n = mark(nc.vector.tensor_scalar_add(var_e[:], mv[:, :, 1], EPS))
            assert n == V_VAR
            dve.wait_ge(pool_pre, G_CONST + 1)
            mark(nc.vector.tensor_tensor(both[:], rstd_t[:], rstd_t[:], ALU.mult))
            dve.wait_ge(vec_pre, pre[0])
            mark(nc.vector.tensor_tensor(both[:], both[:], mv[:, :, 1], ALU.mult))
            dve.wait_ge(vec_pre, pre[0])
            n = mark(nc.vector.tensor_scalar_add(ms_e[:], both[:], EPS))
            assert n == V_MS
            for b in range(BLK):
                n = mark(nc.vector.tensor_scalar(acc[:, b, :], xt[:, b, :], mv[:, b, 0:1],
                                                 rstd_t[:, b:b + 1], ALU.subtract, ALU.mult))
                assert n == V_ACC + b
            dve.wait_ge(pool_pre, G_CONST + 2)
            for b in (2, 3):
                dve.wait_ge(vec_pre, V_ACC + b)
                n = mark(nc.vector.tensor_scalar(hs[:, b, :], acc[:, b, :], rms[:, b:b + 1], None, ALU.mult))
                assert n == V_HS + b - 2
            dve.wait_ge(act_pre, A_WDT)
            n = mark(nc.vector.tensor_tensor(wdt_lo[:], wdt_raw[:], wdt_hi[:].bitcast(F32), ALU.subtract))
            assert n == V_WDT
            dve.wait_ge(tabs_in, 16 * 7)
            mark(nc.vector.tensor_scalar_mul(conv_all[:], conv_all[:], 0.5))
            dve.wait_ge(vec_pre, pre[0])

            def conv_table(p):
                past(dve, conved, 3 * CONVS * p)
                nc.vector.tensor_copy(conv_g[:], conv_all[:, bass.ds(p, 1)].rearrange(
                    "c o u k -> c (o u) k")).then_inc(conv_tab_set, 1)
                dve.wait_ge(conv_tab_set, p + 1)

            conv_table(0)

            def lo_part(p, t):
                dve.wait_ge(w_hi_made, TILES * p + t + 1)
                s = t % WRING
                nc.vector.tensor_tensor(w_lo[:, s, :], w_raw[:, s, :], w_hi[:, s, :].bitcast(F32),
                                        ALU.subtract).then_inc(w_lo_made, 1)

            for k in range(KT):
                dve.wait_ge(act_pre, A_HHI + k)
                n = mark(nc.vector.scalar_tensor_tensor(
                    out=h_lo[:, k, :], in0=h_banks[k][:], scalar=nw[:, k:k + 1],
                    in1=h_hi[:, k, :].bitcast(F32), op0=ALU.mult, op1=ALU.subtract))
                assert n == V_HLO + k
            for t in range(WRING):
                lo_part(0, t)
            dve.wait_ge(act_pre, A_NEG)
            mark(nc.vector.tensor_scalar_mul(neg_a[:], neg_a[:], -1.0))

            def conv(p, t):
                i = conv_of(t)
                c = CONVS * p + i
                dve.wait_ge(tapped, c + 1)
                src = bank_of(p, t)[:].rearrange("c (b t) -> c b t", b=SEQS)
                for j in range(1, TAPS):
                    if j > 1:
                        dve.wait_ge(conved, 3 * c + j - 1)
                    dst = cacc[:, i % 2, :, j:SEQ]
                    nc.vector.scalar_tensor_tensor(
                        out=dst, in0=src[:, :, 0:SEQ - j], scalar=conv_g[:, i, TAPS - 1 - j:TAPS - j],
                        in1=dst, op0=ALU.mult, op1=ALU.add).then_inc(conved, 1)

            def silu(p, t):
                i = conv_of(t)
                dve.wait_ge(conv_tanh, CONVS * p + i + 1)
                dst = hid[:, (i - 2) % RING, :] if i >= 2 else (b_t, c_t)[i][:]
                if i == 1:
                    past(dve, c_copied, p)
                nc.vector.scalar_tensor_tensor(
                    out=dst, in0=th[:, i % 2, :], scalar=1.0, in1=cacc[:, i % 2].rearrange("c b t -> c (b t)"),
                    op0=ALU.add, op1=ALU.mult).then_inc(silu_made, 1)

            def silu_gate(p, u):
                dve.wait_ge(gate_tanh, PAIRS * p + u + 1)
                nc.vector.scalar_tensor_tensor(out=gate[:, u % RING, :], in0=thg[:], scalar=1.0,
                                               in1=bank_of(p, gate_tile(u))[:], op0=ALU.add,
                                               op1=ALU.mult).then_inc(gate_made, 1)

            def tokens_hid(g, u):
                dve.wait_ge(hid_turned, PAIRS * g + u + 1)
                dve.wait_ge(y_made, CREDIT + PAIRS * g + u - 1)
                src = ps_t[:].rearrange("t (b h c) -> t b h c", b=BLK, h=2)
                heads = slice(2 * u, 2 * u + 2)
                nc.vector.tensor_tensor(
                    hc[:, u % 2].rearrange("t b (h c) -> t b h c", h=2), src,
                    dt_g[:, :, heads].unsqueeze(3).to_broadcast([P, BLK, 2, HD]), ALU.mult
                ).then_inc(hc_made, 1)
                dve.wait_ge(state_made, CREDIT + PAIRS * g + u - 1)
                nc.vector.tensor_tensor(
                    hcd[:, u % 2].rearrange("t b (h c) -> t b h c", h=2), src[:, 0:BLK:2],
                    dtd_g[:, :, heads].unsqueeze(3).to_broadcast([P, SEQS, 2, HD]), ALU.mult
                ).then_inc(hcd_made, 1)

            def mix(g, u):
                dve.wait_ge(l_made, PAIRS * g + u + 1)
                if u == 0:
                    dve.wait_ge(cb_kept, g + 1)
                m = decay[:, u % 2]
                nc.vector.tensor_tensor(m, m, cb[:].rearrange("j b i -> j (b i)").unsqueeze(1).to_broadcast(
                    [P, 2, TOK]), ALU.mult).then_inc(m_made, 1)

            def gated(g, u):
                dve.wait_ge(y_made, CREDIT + PAIRS * g + u + 1)
                nc.vector.scalar_tensor_tensor(out=y1[:], in0=hid[:, u % RING, :], scalar=d_g[:, u:u + 1],
                                               in1=ps_y[:], op0=ALU.mult, op1=ALU.add).then_inc(y1_made, 1)
                dve.wait_ge(y1_made, PAIRS * g + u + 1)
                dve.wait_ge(ysq_made, CREDIT + PAIRS * g + u - 1)
                dve.wait_ge(y_lo_made, CREDIT + PAIRS * g + u - 1)
                nc.vector.tensor_tensor(yg[:, u % 2, :], y1[:], gate[:, u % RING, :],
                                        ALU.mult).then_inc(yg_made, 1)

            def add_squares(g, u):
                if u == 0:
                    return
                dve.wait_ge(ysq_made, CREDIT + PAIRS * g + u + 1)
                if u == 1:
                    dve.wait_ge(ss_summed, g + 1)
                    nc.vector.tensor_tensor(ysum[:], ysq[:, 0, :], ysq[:, 1, :], ALU.add
                                            ).then_inc(ysum_made, 2)
                else:
                    dve.wait_ge(ysum_made, CREDIT + PAIRS * g + u)
                    nc.vector.tensor_tensor(ysum[:], ysum[:], ysq[:, u % 2, :], ALU.add
                                            ).then_inc(ysum_made, 1)

            def lo_part_out(g, u):
                dve.wait_ge(wo_hi_made, PAIRS * g + u + 1)
                nc.vector.scalar_tensor_tensor(
                    out=wo_lo[:, u, :], in0=wo_raw[:, u % 2, :], scalar=gn_g[:, u:u + 1],
                    in1=wo_hi[:, u, :].bitcast(F32), op0=ALU.mult, op1=ALU.subtract
                ).then_inc(wo_lo_made, 1)

            def keep_squares(g):
                dve.wait_ge(ss_summed, g + 2)
                nc.vector.tensor_scalar(ss_g[:], ps_x[:, 0:BLK], 1.0 / (PAIRS * P), 4 * EPS, ALU.mult,
                                        ALU.add).then_inc(ss_kept, 1)

            def add_out(g, b):
                if b == 0:
                    dve.wait_ge(rstd_made, g + 1)
                dve.wait_ge(o_made, O_CREDIT + 2 * BLK * g + BLK + b + 1)
                nc.vector.tensor_tensor(o_part[:, b, :], ps_o[:], o_part[:, b, :], ALU.add
                                        ).then_inc(o_added, 1)
                dve.wait_ge(o_added, A_CREDIT + 2 * BLK * g + 2 * b + 1)
                nc.vector.scalar_tensor_tensor(
                    out=acc[:, b, :], in0=o_part[:, b, :], scalar=rstd_g[:, b:b + 1],
                    in1=acc[:, b, :], op0=ALU.mult, op1=ALU.add).then_inc(o_added, 1)

            def keep_cb(g):
                dve.wait_ge(cb_made, g + 1)
                nc.vector.tensor_tensor(cb[:], ps_x[:].rearrange("j (b i) -> j b i", b=BLK),
                                        causal[:].unsqueeze(1).to_broadcast([P, BLK, P]), ALU.mult
                                        ).then_inc(cb_kept, 1)

            def fall_table(g):
                past(dve, fall_made, PAIRS * g)
                nc.vector.tensor_copy(acs_g[:], acs_all[:, :, bass.ds(HEADS * g, HEADS)]
                                      ).then_inc(fall_tab, 1)

            def head_tables(g):
                h = bass.ds(HEADS * g, HEADS)
                nc.vector.tensor_copy(dt_g[:], dt_all[:, :, h])
                nc.vector.tensor_copy(dtd_g[:], dtd_all[:, :, h]).then_inc(head_tabs, 1)
                dve.wait_ge(head_tabs, g + 1)

            def out_tables(g):
                past(dve, y1_made, PAIRS * g)
                dve.wait_ge(wo_lo_made, CREDIT + PAIRS * g)
                nc.vector.tensor_copy(d_g[:], d_all[:, bass.ds(g, 1)].rearrange("c o u -> c (o u)"))
                nc.vector.tensor_copy(gn_g[:], gn_all[:, bass.ds(g, 1)].rearrange("c o u -> c (o u)")
                                      ).then_inc(out_tab_set, 1)
                dve.wait_ge(out_tab_set, g + 1)

            dve.wait_ge(act_pre, A_ABS)
            n = mark(nc.vector.tensor_scalar(dtx[:], ps_x[:], dtb[:, 0:1], 0.0, ALU.add, ALU.max))
            assert n == V_DTX
            dve.wait_ge(act_pre, A_EX)
            mark(nc.vector.tensor_scalar_add(poly[:], ex[:], 2.0))
            dve.wait_ge(vec_pre, pre[0])
            mark(nc.vector.reciprocal(zz[:, 1, :], poly[:]))
            lo_part(0, 3)
            dve.wait_ge(vec_pre, pre[0])
            mark(nc.vector.tensor_tensor(zz[:, 0, :], ex[:], zz[:, 1, :], ALU.mult))
            dve.wait_ge(vec_pre, pre[0])
            mark(nc.vector.tensor_tensor(zz[:, 1, :], zz[:, 0, :], zz[:, 0, :], ALU.mult))
            dve.wait_ge(vec_pre, pre[0])
            mark(nc.vector.tensor_scalar_mul(poly[:], zz[:, 1, :], 1.0 / 13))
            lo_part(0, 4)
            for c in (11, 9, 7, 5, 3):
                dve.wait_ge(vec_pre, pre[0])
                mark(nc.vector.scalar_tensor_tensor(out=poly[:], in0=poly[:], scalar=1.0 / c,
                                                    in1=zz[:, 1, :], op0=ALU.add, op1=ALU.mult))
            lo_part(0, 5)
            dve.wait_ge(vec_pre, pre[0])
            mark(nc.vector.scalar_tensor_tensor(out=poly[:], in0=poly[:], scalar=1.0, in1=zz[:, 0, :],
                                                op0=ALU.add, op1=ALU.mult))
            silu_gate(0, 0)
            dve.wait_ge(vec_pre, pre[0])
            mark(nc.vector.scalar_tensor_tensor(out=dt_h[:], in0=poly[:], scalar=2.0, in1=dtx[:],
                                                op0=ALU.mult, op1=ALU.add))
            dve.wait_ge(vec_pre, pre[0])
            mark(nc.vector.tensor_scalar(ac_h[:], dt_h[:], neg_a[:, 0:1], None, ALU.mult))
            dve.wait_ge(vec_pre, pre[0])
            for b in range(BLK):
                t = slice(b * P, (b + 1) * P)
                n = mark(nc.vector.tensor_tensor_scan(acs_h[:, t], one_row[:], ac_h[:, t], 0.0,
                                                      ALU.mult, ALU.add))
            assert n == V_ACS, n

            conv(0, 0)
            conv(0, 1)
            silu(0, 0)
            silu(0, 1)
            dve.wait_ge(act_pre, A_DTD)
            n = mark(nc.vector.tensor_tensor(
                dtd_h[:], dtd_h[:], dt_h[:].rearrange("h (b c t) -> h b c t", b=SEQS, c=2)[:, :, 0, :],
                ALU.mult))
            assert n == V_DTD, n
            conv(0, 2)
            dve.wait_ge(pe_pre, PE_DTD_T)
            n = mark(nc.vector.tensor_copy(dtd_all[:].rearrange("t b h -> t (b h)"), ps_x[:, 0:2 * P]))
            assert n == V_TOK, n
            dve.wait_ge(act_pre, A_DT)
            dve.wait_ge(vec_pre, V_TOK)
            fall_table(0)
            head_tables(0)
            silu(0, 2)
            keep_cb(0)
            lo_part(0, 6)
            tokens_hid(0, 0)
            mix(0, 0)
            conv(0, 4)
            lo_part(0, 7)
            dve.wait_ge(pool_pre, G_RES)

            def step(g, u, last, first):
                near = exists(last, u, 1)
                ahead = exists(last, u, LEAD)
                p, v = following(g, u, LEAD)
                nxt = following(g, u, 1)
                if exists(last, u, LEAD - 1):
                    if u == 7:
                        silu(nxt[0], 1)
                        head_tables(nxt[0])
                    silu(nxt[0], hid_tile(nxt[1]))
                    silu_gate(*nxt)
                if u == 6 and not last:
                    fall_table(g + 1)
                    lo_part(g + 1, 2)
                    conv(g + 1, 0)
                if u == 0:
                    out_tables(g)
                gated(g, u)
                if u == 0 and not first:
                    keep_squares(g - 1)
                if u == 7 and near:
                    keep_cb(nxt[0])
                if near:
                    tokens_hid(*nxt)
                if u == 6 and not last:
                    silu(g + 1, 0)
                if near:
                    mix(*nxt)
                if u == 6 and ahead:
                    conv(p, 1)
                    lo_part(p, 3)
                    lo_part(p, 4)
                elif ahead:
                    lo_part(p, hid_tile(v) + 2)
                lo_part_out(g, u)
                if ahead:
                    conv(p, hid_tile(v))
                add_squares(g, u)
                if ahead:
                    lo_part(p, hid_tile(v) + 3)
                if u < HALF and not first:
                    add_out(g - 1, u)
                if u == 5 and not last:
                    conv_table(g + 1)
                if last and u == 6:
                    scales()

            done = [0]

            def note(ins):
                ins.then_inc(vec_chain, 1)
                done[0] += 1

            def chain():
                dve.wait_ge(vec_chain, done[0])

            def context_rounded(q):
                dve.wait_ge(ctx_scaled, q + 1)
                v = ctx_raw[:, q]
                nc.vector.tensor_scalar(v, v, 255.0, ROUND, ALU.min, ALU.add).then_inc(ctx_rounded, 1)

            def scales():
                dve.wait_ge(proj_made, TILES * GROUPS)
                dve.wait_ge(w_lo_made, TILES * GROUPS + 2)
                dve.wait_ge(w_in_s[(TILES * GROUPS + 4) % WRING], 16 * ((TILES * GROUPS + 4) // WRING + 1))
                dve.wait_ge(w_in_s[(TILES * GROUPS + 3) % WRING], 16 * ((TILES * GROUPS + 3) // WRING + 1))
                dve.wait_ge(w_in_s[(TILES * GROUPS + 2) % WRING], 16 * ((TILES * GROUPS + 2) // WRING + 1))
                note(nc.vector.reciprocal(inv[:, 0:1], cst[:, 0:1]))
                note(nc.vector.reciprocal(inv[:, 1:2], cst[:, 2:3]))
                note(nc.vector.tensor_scalar(shift[:, 0:1], cst[:, 1:2], -1.0, MID, ALU.mult, ALU.add))
                note(nc.vector.tensor_scalar(shift[:, 1:2], cst[:, 3:4], -1.0, MID, ALU.mult, ALU.add))
                note(nc.vector.tensor_tensor(s12[:, 0:1], cst[:, 0:1], cst[:, 2:3], ALU.mult))
                chain()
                note(nc.vector.tensor_tensor(s12[:, 1:2], s12[:, 0:1], shift[:, 0:1], ALU.mult))
                note(nc.vector.tensor_tensor(s12[:, 2:3], s12[:, 0:1], shift[:, 1:2], ALU.mult))
                chain()
                note(nc.vector.scalar_tensor_tensor(out=s12[:, 3:4], in0=s12[:, 1:2], scalar=float(D_MODEL),
                                                    in1=shift[:, 1:2], op0=ALU.mult, op1=ALU.mult))
                chain()
                note(nc.vector.memset(unround[:], -(ROUND + MID)))
                nc.vector.memset(ones_bf[:], 1.0).then_inc(scales_set, 1)

            def shift_mean(s):
                b = slice(2 * s, 2 * s + 2)
                dve.wait_ge(rstd_set, SEQS + s + 1)
                nc.vector.scalar_tensor_tensor(out=mshift[:, b], in0=mv[:, b, 0], scalar=-1.0,
                                               in1=rstd_t[:, b], op0=ALU.mult, op1=ALU.mult
                                               ).then_inc(shift_set, 1)

            run_steps(dve, step)
            context_rounded(0)
            keep_squares(last_group)

            def variances(q):
                pair = (2 * q, 2 * q + 1)
                for b in pair[1:]:
                    note(nc.vector.bn_stats(stats[:, b, :], acc[:, b, :]))
                chain()
                for b in pair:
                    note(nc.vector.bn_aggr(mv[:, b, :], stats[:, b, :]))
                chain()
                nc.vector.tensor_scalar_add(var_e[:, 2 * q:2 * q + 2], mv[:, 2 * q:2 * q + 2, 1], EPS
                                            ).then_inc(var_set, 1)

            def affine(q):
                b = slice(2 * q, 2 * q + 2)
                dve.wait_ge(rstd_set, q + 1)
                note(nc.vector.tensor_scalar(aff[:, 0, b], rstd_t[:, b], inv[:, 0:1], None, ALU.mult))
                chain()
                note(nc.vector.scalar_tensor_tensor(out=aff[:, 1, b], in0=mv[:, b, 0], scalar=-1.0,
                                                    in1=aff[:, 0, b], op0=ALU.mult, op1=ALU.mult))
                chain()
                nc.vector.tensor_scalar(aff[:, 1, b], aff[:, 1, b], cst[:, 1:2], None, ALU.add
                                        ).then_inc(affine_set, 1)

            dve.wait_ge(rstd_made, GROUPS)
            dve.wait_ge(o_kept, BLK * GROUPS)
            for b in range(BLK):
                nc.vector.scalar_tensor_tensor(out=acc[:, b, :], in0=o_part[:, b, :],
                                               scalar=rstd_g[:, b:b + 1], in1=acc[:, b, :], op0=ALU.mult,
                                               op1=ALU.add).then_inc(o_added, 1)
            context_rounded(1)
            for q in range(SEQS):
                for b in (2 * q, 2 * q + 1):
                    dve.wait_ge(o_made, O_CREDIT + 2 * BLK * last_group + BLK + b + 1)
                    dve.wait_ge(o_added, A_CREDIT + 2 * BLK * last_group + b + 1)
                    nc.vector.scalar_tensor_tensor(out=acc[:, b, :], in0=tail_banks[b][:],
                                                   scalar=rstd_g[:, b:b + 1], in1=acc[:, b, :], op0=ALU.mult,
                                                   op1=ALU.add).then_inc(o_added, 1)
                    dve.wait_ge(o_added, A_CREDIT + 2 * BLK * last_group + BLK + b + 1)
                    if b % 2 == 0:
                        note(nc.vector.bn_stats(stats[:, b, :], acc[:, b, :]))
                    if b == 2:
                        affine(0)
                variances(q)

            def levels(q):
                pair = (2 * q, 2 * q + 1)
                for b in pair:
                    dve.wait_ge(affine_made, b + 1)
                    note(nc.vector.tensor_scalar(n_t[:, b, :], n_t[:, b, :], 0.0, 255.0, ALU.max, ALU.min))
                chain()
                for b in pair:
                    nc.vector.tensor_scalar(lvl1[:, b, :], n_t[:, b, :], ROUND, -(ROUND + MID), ALU.add,
                                            ALU.add).then_inc(lvl1_made, 1)

            levels(0)
            affine(1)
            levels(1)

            def column_sums(q):
                dve.wait_ge(col_summed, q + 1)
                nc.vector.tensor_scalar(col[:, q, :], sum_banks[q][:], s12[:, 1:2], s12[:, 3:4],
                                        ALU.mult, ALU.add).then_inc(col_kept, 1)
                dve.wait_ge(col_kept, q + 1)

            def add_sums(b):
                note(nc.vector.scalar_tensor_tensor(out=acc[:, b, :], in0=col[:, b // 2, :],
                                                    scalar=rsum[:, b:b + 1], in1=acc[:, b, :],
                                                    op0=ALU.add, op1=ALU.add))
                chain()

            def add_product(b):
                dve.wait_ge(x_made, b + 1)
                note(nc.vector.scalar_tensor_tensor(out=acc[:, b, :], in0=tail_banks[b][:],
                                                    scalar=s12[:, 0:1], in1=acc[:, b, :],
                                                    op0=ALU.mult, op1=ALU.add))
                chain()
                if b % 2 == 0:
                    note(nc.vector.bn_stats(stats[:, b, :], acc[:, b, :]))

            def low_part_stream(q):
                for j in range(2):
                    dve.wait_ge(n_hi_made, 2 * q + j + 1)
                    part = n_hi[:, 2 * j:2 * j + 2, 2 * q * P:2 * (q + 1) * P]
                    nc.vector.tensor_tensor(n_lo[:, 2 * j:2 * j + 2, 2 * q * P:2 * (q + 1) * P],
                                            turn_banks[2 * q + j][:].rearrange("d (k t) -> d k t", k=2),
                                            part.bitcast(F32), ALU.subtract).then_inc(n_lo_made, 1)

            column_sums(0)
            dve.wait_ge(row_summed, 1)
            nc.vector.tensor_scalar(rsum[:], ps_t[:, 0:BLK], s12[:, 2:3], None, ALU.mult
                                    ).then_inc(rows_kept, 1)
            dve.wait_ge(rows_kept, 1)
            add_sums(0)
            add_sums(1)
            add_product(0)
            add_product(1)
            variances(0)
            column_sums(1)
            shift_mean(0)
            add_sums(2)
            add_product(2)
            add_sums(3)
            low_part_stream(0)
            add_product(3)
            variances(1)
            low = slice(2 * LORA, 3 * LORA)
            dve.wait_ge(f_hi_made, 3)
            nc.vector.tensor_tensor(lb_s[low, :], lb[low, :], lb_s[low, :].bitcast(F32),
                                    ALU.subtract).then_inc(lb_split, 1)
            shift_mean(1)
            low_part_stream(1)
            nz = LORA + EXPERTS
            dve.wait_ge(z_turned, 1)
            note(nc.vector.tensor_copy(zl[:].rearrange("t b z -> t (b z)"), ps_y[:, 0:BLK * nz]))
            chain()
            logits = zl[:, :, LORA:nz]
            note(nc.vector.tensor_tensor(logits, logits, cst[:, 4:8].unsqueeze(1).to_broadcast(
                [P, BLK, EXPERTS]), ALU.add))
            chain()
            note(nc.vector.tensor_reduce(lmax[:], logits, AX_X, ALU.max))
            chain()
            note(nc.vector.tensor_tensor(hit[:], logits, lmax[:].unsqueeze(2).to_broadcast(
                [P, BLK, EXPERTS]), ALU.is_equal))
            chain()
            note(nc.vector.tensor_scalar(none_yet[:], hit[:], -1.0, 1.0, ALU.mult, ALU.add))
            chain()
            for e in range(1, EXPERTS):
                note(nc.vector.tensor_tensor(hit[:, :, e:], hit[:, :, e:],
                                             none_yet[:, :, e - 1:e].to_broadcast([P, BLK, EXPERTS - e]),
                                             ALU.mult))
                chain()
            note(nc.vector.tensor_tensor(
                zm[:, :, 2, :].rearrange("t b (e r) -> t b e r", e=EXPERTS),
                zl[:, :, 0:LORA].rearrange("t b (e r) -> t b e r", e=EXPERTS),
                hit[:].unsqueeze(3).to_broadcast([P, BLK, EXPERTS, RANK]), ALU.mult))
            chain()
            note(nc.vector.tensor_copy(zm_r[:], zm[:, :, 2, :]))
            chain()
            note(nc.vector.tensor_tensor(zm[:, :, 1, :], zm[:, :, 2, :], zm_r[:].bitcast(F32), ALU.subtract))
            note(nc.vector.tensor_copy(zm[:, :, 0, :], zm_r[:].bitcast(F32)))
            chain()
            nc.vector.tensor_copy(zm[:, :, 2, :], zm_r[:].bitcast(F32)).then_inc(zm_made, 1)
            dve.wait_ge(zm_turned, 1)
            nc.vector.tensor_copy(zm_t[:].rearrange("z b t -> z (b t)"), ps_p[1][0:3 * LORA, :]
                                  ).then_inc(zmt_kept, 1)
            for b in range(BLK):
                dve.wait_ge(f_made, b + 1)
                nc.vector.tensor_tensor(acc[:, b, :], acc[:, b, :], tail_banks[b][:], ALU.add
                                        ).then_inc(out_made, 1)


G_CONST = 9
G_RES = G_CONST + 2 + BLK
A_WDT = 1
A_HS = A_WDT + 1
A_HHI = A_HS + 2
A_NEG = A_HHI + KT
A_ABS = A_NEG + 1
A_EX = A_ABS + 1
A_DTD = A_EX + SEQS
A_ACS = A_DTD + 1
A_DT = A_ACS + 1
V_VAR = 2 * BLK + 1
V_MS = V_VAR + 3
V_ACC = V_MS + 1
V_HS = V_ACC + BLK
V_WDT = V_HS + 2
V_HLO = V_WDT + 2
V_DTX = V_HLO + KT + 1
V_ACS = V_DTX + 5 + 5 + 3 + BLK
V_DTD = V_ACS + 1
V_TOK = V_DTD + 1
PE_DT = KT + 1
PE_ACS_T = PE_DT + 1
PE_DT_T = PE_ACS_T + 1
PE_DTD_T = PE_DT_T + 1


def kernel(**inputs):
    import concourse.bacc as bacc
    from concourse.bass_utils import run_bass_kernel_spmd as run

    a = {k: np.asarray(v) for k, v in inputs.items()}
    d_inner = GROUPS * PAIRS * P
    tiles = []
    for g in range(GROUPS):
        tiles += [2 * d_inner + g * P, 2 * d_inner + (GROUPS + g) * P]
        for u in range(PAIRS):
            c = (g * PAIRS + u) * P
            tiles += [d_inner + c, c]
    tiles.append(2 * d_inner + 2 * GROUPS * P)
    w = a["L0_attn_in_proj_w"]
    w_in = np.concatenate([w[t:t + P] for t in tiles]).reshape(len(tiles), P, KT, P).transpose(0, 3, 2, 1)
    w_in = w_in.reshape(len(tiles), P, D_MODEL)
    w_in = np.concatenate([w_in, np.zeros((PAD_TILES, P, D_MODEL), w_in.dtype)])
    conv = np.concatenate([a["L0_attn_conv_w"], a["L0_attn_conv_b"][:, None]], axis=1)
    hid_c = conv[:d_inner].reshape(GROUPS, PAIRS, P, TAPS + 1)
    bc_c = conv[d_inner:].reshape(2, GROUPS, 1, P, TAPS + 1)
    conv_tab = np.concatenate([bc_c[0], bc_c[1], hid_c], axis=1).transpose(2, 0, 1, 3)
    arrays = {
        "x": a["x"],
        "w_in": w_in,
        "conv_tab": conv_tab,
        "d_tab": np.repeat(a["L0_attn_Dp"], HD).reshape(GROUPS, PAIRS, P).transpose(2, 0, 1),
        "gn_tab": a["L0_attn_gnorm_w"].reshape(GROUPS, PAIRS, P).transpose(2, 0, 1),
        "nw_tab": a["L0_attn_norm_w"].reshape(KT, P).T,
        "dtb_tab": a["L0_attn_dt_bias"].reshape(P, 1),
        "alog_tab": a["L0_attn_A_log"].reshape(P, 1),
        "w_out": a["L0_attn_out_proj_w"].T.reshape(GROUPS * PAIRS, P, D_MODEL),
        "ctx_in": a["ctx_4096"],
        "w_up": a["L0_ffn_W_up"].T.reshape(KT, P, D_MODEL).transpose(1, 0, 2),
        "w_z": np.concatenate([a["L0_ffn_lora_A"].reshape(LORA, D_MODEL), a["L0_ffn_gate_w"]]).T.reshape(
            KT, P, LORA + EXPERTS).transpose(1, 0, 2),
        "lora_b": a["L0_ffn_lora_B"].transpose(0, 2, 1).reshape(LORA, D_MODEL),
        "consts": np.concatenate([a["L0_xattn_x1_scale"], a["L0_xattn_x1_zp"], a["L0_xattn_x2_scale"],
                                  a["L0_xattn_x2_zp"], a["L0_ffn_expert_bias"]]).reshape(1, 8),
    }
    nc = bacc.Bacc("TRN2", target_bir_lowering=False, num_devices=1)
    feeds, args = {}, []
    for name, value in arrays.items():
        value = np.ascontiguousarray(value)
        feeds["in_" + name] = value
        args.append(nc.dram_tensor("in_" + name, value.shape, F32, kind="ExternalInput").ap())
    acs_rows = nc.dram_tensor("acs_rows", (GROUPS * PAIRS, 2, TOK), F32, kind="Internal").ap()
    out = nc.dram_tensor("out", a["x"].shape, F32, kind="ExternalOutput").ap()
    decoder_program(nc, *args, acs_rows, out)
    result = run(nc, [feeds], core_ids=[0])
    return result.results[0]["out"]
```
